# Optimizing a Trainium2 kernel written in Bass

```python
import numpy as np
import jax
import jax.numpy as jnp

def _softmax(x, axis=-1):
    return jax.nn.softmax(x, axis=axis)

def _gelu(x):
    return jax.nn.gelu(x, approximate=True)

def _silu(x):
    return jax.nn.silu(x)

def _sigmoid(x):
    return jax.nn.sigmoid(x)

def _layernorm(x, axis=-1, eps=1e-05):
    m = jnp.mean(x, axis=axis, keepdims=True)
    v = jnp.var(x, axis=axis, keepdims=True)
    return (x - m) / jnp.sqrt(v + eps)

def _scatter_add(tgt, idx, src, axis=0):
    return tgt.at[idx].add(src)

def _segment_sum(src, seg, n):
    return jax.ops.segment_sum(src, seg, n)
kernel_name = 'mk_conv_attn_hybrid_d2_conv_nhwc128_r2_56ab4b'

def setup_inputs(seed: int=0):
    np.random.seed(seed)
    _w = jnp.asarray

    def _rec_inputs():
        import jax
        import jax.numpy as jnp
        _gk = jax.random.key(seed)
        x = -0.000929 + 1 * jax.random.normal(jax.random.fold_in(_gk, 1), (2, 32, 32, 64), jnp.float32)
        return x
    x = _rec_inputs()

    def _L0_conv_setup():
        import jax, jax.numpy as jnp
        import numpy as np
        B, H, W, C = (2, 32, 32, 64)
        NH, K = (4, 7)
        HD = C // NH
        SCALE = HD ** (-0.5)

        def _window_starts(L):
            i = jnp.arange(L)
            return jnp.clip(i - K // 2, 0, L - K)
        key = jax.random.key(seed)
        ks = jax.random.split(key, 5)
        return {'x': jax.random.normal(ks[0], (B, H, W, C), jnp.float32), 'w_qkv': jax.random.normal(ks[1], (C, 3 * C), jnp.float32) * 0.02, 'b_qkv': jnp.zeros((3 * C,), jnp.float32), 'rpb': jax.random.normal(ks[2], (NH, 2 * K - 1, 2 * K - 1), jnp.float32) * 0.02, 'w_proj': jax.random.normal(ks[3], (C, C), jnp.float32) * 0.02, 'b_proj': jnp.zeros((C,), jnp.float32)}
    _L0_conv_all = _L0_conv_setup()
    _L0_conv_in = {k: v for k, v in _L0_conv_all.items() if k in ('w_qkv', 'b_qkv', 'rpb', 'w_proj', 'b_proj')}
    del _L0_conv_all

    def _L1_attn_setup():
        import jax, jax.numpy as jnp
        import numpy as np
        SCALE = 0.1
        TEMP = 0.5
        EPS = 1e-06
        key = jax.random.key(seed)
        k1, = jax.random.split(key, 1)
        x = jax.random.normal(k1, (4, 2048, 64), dtype=jnp.float32)
        ln_weight = jnp.ones((64,), dtype=jnp.float32)
        ln_bias = jnp.zeros((64,), dtype=jnp.float32)
        return {'x': x, 'ln_weight': ln_weight, 'ln_bias': ln_bias}
    _L1_attn_all = _L1_attn_setup()
    _L1_attn_in = {k: v for k, v in _L1_attn_all.items() if k in ('ln_weight', 'ln_bias')}
    del _L1_attn_all

    def _L1_ffn_setup():
        import jax, jax.numpy as jnp
        import numpy as np
        NB, NOPS = (33, 19)
        D, H = (64, 256)
        B, S = (8, 512)
        CARRY_OPS = [0, 1, 2, 10, 11, 12, 13]

        def _build_masks():
            am = np.zeros((NB, NOPS), dtype=bool)
            fm = np.zeros((NB, NOPS), dtype=bool)
            fm[0, :] = True
            for b in range(1, 8):
                am[b, CARRY_OPS] = True
                fm[b, CARRY_OPS] = True
            am[8, [14, 15, 8, 9]] = True
            fm[8, [14, 15, 8, 9]] = True
            for b in range(16, 32):
                fm[b, [3, 4]] = True
            am[32, [10, 11, 12, 13]] = True
            fm[32, [5, 6, 7, 2, 4, 10, 11, 12, 13]] = True
            return (jnp.asarray(am), jnp.asarray(fm))
        key = jax.random.key(seed)
        ks = jax.random.split(key, 9)
        sd = 1.0 / np.sqrt(D)
        sh = 1.0 / np.sqrt(H)
        am, fm = _build_masks()
        return {'x': jax.random.normal(ks[0], (B, S, D), jnp.float32), 'ffn_w1': jax.random.normal(ks[1], (NB, NOPS, D, H), jnp.float32) * sd, 'ffn_b1': jnp.zeros((NB, NOPS, H), jnp.float32), 'ffn_w2': jax.random.normal(ks[2], (NB, NOPS, H, D), jnp.float32) * sh, 'ffn_b2': jnp.zeros((NB, NOPS, D), jnp.float32), 'wq': jax.random.normal(ks[3], (NB, NOPS, D, D), jnp.float32) * sd, 'wk': jax.random.normal(ks[4], (NB, NOPS, D, D), jnp.float32) * sd, 'wv': jax.random.normal(ks[5], (NB, NOPS, D, D), jnp.float32) * sd, 'wo': jax.random.normal(ks[6], (NB, NOPS, D, D), jnp.float32) * sd, 'attn_mask': am, 'ffn_mask': fm}
    _L1_ffn_all = _L1_ffn_setup()
    _L1_ffn_in = {k: v for k, v in _L1_ffn_all.items() if k in ('ffn_w1', 'ffn_b1', 'ffn_w2', 'ffn_b2', 'wq', 'wk', 'wv', 'wo', 'attn_mask', 'ffn_mask')}
    del _L1_ffn_all
    return {'x': x, 'L0_conv_w_qkv': _L0_conv_in['w_qkv'], 'L0_conv_b_qkv': _L0_conv_in['b_qkv'], 'L0_conv_rpb': _L0_conv_in['rpb'], 'L0_conv_w_proj': _L0_conv_in['w_proj'], 'L0_conv_b_proj': _L0_conv_in['b_proj'], 'L1_attn_ln_weight': _L1_attn_in['ln_weight'], 'L1_attn_ln_bias': _L1_attn_in['ln_bias'], 'L1_ffn_ffn_w1': _L1_ffn_in['ffn_w1'], 'L1_ffn_ffn_b1': _L1_ffn_in['ffn_b1'], 'L1_ffn_ffn_w2': _L1_ffn_in['ffn_w2'], 'L1_ffn_ffn_b2': _L1_ffn_in['ffn_b2'], 'L1_ffn_wq': _L1_ffn_in['wq'], 'L1_ffn_wk': _L1_ffn_in['wk'], 'L1_ffn_wv': _L1_ffn_in['wv'], 'L1_ffn_wo': _L1_ffn_in['wo'], 'L1_ffn_attn_mask': _L1_ffn_in['attn_mask'], 'L1_ffn_ffn_mask': _L1_ffn_in['ffn_mask']}

def reference(x, L0_conv_w_qkv, L0_conv_b_qkv, L0_conv_rpb, L0_conv_w_proj, L0_conv_b_proj, L1_attn_ln_weight, L1_attn_ln_bias, L1_ffn_ffn_w1, L1_ffn_ffn_b1, L1_ffn_ffn_w2, L1_ffn_ffn_b2, L1_ffn_wq, L1_ffn_wk, L1_ffn_wv, L1_ffn_wo, L1_ffn_attn_mask, L1_ffn_ffn_mask):
    import jax
    import jax.numpy as jnp

    def _L0_conv_ref(x, w_qkv, b_qkv, rpb, w_proj, b_proj):
        import jax, jax.numpy as jnp
        import numpy as np
        B, H, W, C = (2, 32, 32, 64)
        NH, K = (4, 7)
        HD = C // NH
        SCALE = HD ** (-0.5)

        def _window_starts(L):
            i = jnp.arange(L)
            return jnp.clip(i - K // 2, 0, L - K)
        qkv = (x @ w_qkv + b_qkv).reshape(B, H, W, 3, NH, HD)
        q = qkv[..., 0, :, :] * SCALE
        k = qkv[..., 1, :, :]
        v = qkv[..., 2, :, :]
        a = jnp.arange(K)
        idx_h = _window_starts(H)[:, None] + a[None, :]
        idx_w = _window_starts(W)[:, None] + a[None, :]
        k_nb = k[:, idx_h][:, :, :, idx_w]
        v_nb = v[:, idx_h][:, :, :, idx_w]
        attn = jnp.einsum('bhwnd,bhpwqnd->bnhwpq', q, k_nb)
        bidx_h = idx_h - jnp.arange(H)[:, None] + (K - 1)
        bidx_w = idx_w - jnp.arange(W)[:, None] + (K - 1)
        bias = rpb[:, bidx_h[:, :, None, None], bidx_w[None, None]]
        attn = attn + bias.transpose(0, 1, 3, 2, 4)[None]
        attn = jax.nn.softmax(attn.reshape(B, NH, H, W, K * K), axis=-1)
        attn = attn.reshape(B, NH, H, W, K, K)
        out = jnp.einsum('bnhwpq,bhpwqnd->bhwnd', attn, v_nb).reshape(B, H, W, C)
        return out @ w_proj + b_proj

    def _L1_attn_ref(x, ln_weight, ln_bias):
        import jax, jax.numpy as jnp
        import numpy as np
        SCALE = 0.1
        TEMP = 0.5
        EPS = 1e-06
        xn = x / jnp.maximum(jnp.linalg.norm(x, axis=-1, keepdims=True), 1e-12)
        sim = jnp.einsum('bnd,bmd->bnm', xn, xn) / TEMP
        sim = jax.nn.softmax(sim, axis=-1)
        sim = sim + jax.nn.softmax(sim, axis=-2)
        x_neg = jnp.einsum('bnm,bmd->bnd', sim, x)
        y = x - SCALE * x_neg
        mu = jnp.mean(y, axis=-1, keepdims=True)
        var = jnp.mean((y - mu) ** 2, axis=-1, keepdims=True)
        out = (y - mu) / jnp.sqrt(var + EPS) * ln_weight + ln_bias
        return out

    def _L1_ffn_ref(x, ffn_w1, ffn_b1, ffn_w2, ffn_b2, wq, wk, wv, wo, attn_mask, ffn_mask):
        import jax, jax.numpy as jnp
        import numpy as np
        NB, NOPS = (33, 19)
        D, H = (64, 256)
        B, S = (8, 512)
        CARRY_OPS = [0, 1, 2, 10, 11, 12, 13]

        def _build_masks():
            am = np.zeros((NB, NOPS), dtype=bool)
            fm = np.zeros((NB, NOPS), dtype=bool)
            fm[0, :] = True
            for b in range(1, 8):
                am[b, CARRY_OPS] = True
                fm[b, CARRY_OPS] = True
            am[8, [14, 15, 8, 9]] = True
            fm[8, [14, 15, 8, 9]] = True
            for b in range(16, 32):
                fm[b, [3, 4]] = True
            am[32, [10, 11, 12, 13]] = True
            fm[32, [5, 6, 7, 2, 4, 10, 11, 12, 13]] = True
            return (jnp.asarray(am), jnp.asarray(fm))
        scale = jnp.asarray(1.0 / np.sqrt(D), x.dtype)

        def step(h, p):
            op = jnp.argmax(h[0, 0, :NOPS])
            q = h @ p['wq'][op]
            k = h @ p['wk'][op]
            v = h @ p['wv'][op]
            attn = jax.nn.softmax(jnp.einsum('bqd,bkd->bqk', q, k) * scale, axis=-1)
            y = jnp.einsum('bqk,bkd->bqd', attn, v) @ p['wo'][op]
            h = jnp.where(p['am'][op], y, h)
            z = jax.nn.relu(h @ p['w1'][op] + p['b1'][op]) @ p['w2'][op] + p['b2'][op]
            h = jnp.where(p['fm'][op], z, h)
            return (h, None)
        xs = {'w1': ffn_w1, 'b1': ffn_b1, 'w2': ffn_w2, 'b2': ffn_b2, 'wq': wq, 'wk': wk, 'wv': wv, 'wo': wo, 'am': attn_mask, 'fm': ffn_mask}
        out, _ = jax.lax.scan(step, x, xs)
        return out

    def _gn(v, G=32, eps=1e-05):
        B_, H_, W_, C_ = v.shape
        g = v.reshape(B_, H_, W_, G, C_ // G)
        m = jnp.mean(g, axis=(1, 2, 4), keepdims=True)
        s = jnp.var(g, axis=(1, 2, 4), keepdims=True)
        return ((g - m) / jnp.sqrt(s + eps)).reshape(v.shape)

    def _ln_c(v, eps=1e-06):
        m = jnp.mean(v, axis=-1, keepdims=True)
        s = jnp.var(v, axis=-1, keepdims=True)
        return (v - m) / jnp.sqrt(s + eps)

    def _ln_t(v, eps=1e-05):
        m = jnp.mean(v, axis=-1, keepdims=True)
        s = jnp.var(v, axis=-1, keepdims=True)
        return (v - m) / jnp.sqrt(s + eps)

    def _to_tokens(v):
        B_, H_, W_, C_ = v.shape
        return v.reshape(B_, H_ * W_, C_)

    def _from_tokens(t, like):
        return t.reshape(like.shape)
    x = x + _L0_conv_ref(_gn(x), L0_conv_w_qkv, L0_conv_b_qkv, L0_conv_rpb, L0_conv_w_proj, L0_conv_b_proj)
    t = _to_tokens(x)
    t = t + _L1_attn_ref(_ln_t(t), L1_attn_ln_weight, L1_attn_ln_bias)
    t = t + _L1_ffn_ref(_ln_t(t), L1_ffn_ffn_w1, L1_ffn_ffn_b1, L1_ffn_ffn_w2, L1_ffn_ffn_b2, L1_ffn_wq, L1_ffn_wk, L1_ffn_wv, L1_ffn_wo, L1_ffn_attn_mask, L1_ffn_ffn_mask)
    x = _from_tokens(t, x)
    return x

_drawn_inputs = setup_inputs


def setup_inputs(seed=0):
    import zlib

    import numpy as np

    out = dict(_drawn_inputs(seed))
    spreads = {'L0_conv_b_qkv': (0.0, 0.492),
     'L0_conv_b_proj': (0.0, 0.1),
     'L1_attn_ln_weight': (1.0, 0.2),
     'L1_attn_ln_bias': (0.0, 0.1),
     'L1_ffn_ffn_b1': (0.0, 0.1),
     'L1_ffn_ffn_b2': (0.0, 0.1)}
    factors = {'L0_conv_w_qkv': 8.0, 'L0_conv_rpb': 8.0, 'L0_conv_w_proj': 3.088}
    for name, (base, spread) in spreads.items():
        noise = np.random.default_rng([zlib.crc32(name.encode()), seed]).standard_normal(out[name].shape)
        drawn = base * np.exp(spread * noise) if base else spread * noise
        out[name] = jnp.asarray(drawn.astype(out[name].dtype))
    for name, factor in factors.items():
        out[name] = (out[name] * factor).astype(out[name].dtype)
    return out
```

```python
import concourse.bass as bass
from concourse import mybir
from concourse.alu_op_type import AluOpType as ALU
from contextlib import ExitStack

F32 = mybir.dt.float32
F32R = mybir.dt.float32r
I32 = mybir.dt.int32
U32 = mybir.dt.uint32
U8 = mybir.dt.uint8
ACT = mybir.ActivationFunctionType
AX = mybir.AxisListType

B, IMG, C = 2, 32, 64
N = IMG * IMG
NT = N // 128
NH, KW = 4, 7
HD = C // NH
RW = 2 * KW - 1
WIN = KW * IMG
OUTSIDE = 1.0e30
NB, NOPS = 33, 19
HID = 256
DEAD = 1000.0

CONST = {}
_at = 0
for _name, _w in (("ident", 128), ("pairavg", 128), ("qmask", B * NH), ("vmask", B * C), ("eye32", IMG),
                  ("outside", IMG), ("shift", NH * (2 * IMG - 1)), ("fold", C), ("ones", 128), ("step4", NB)):
    CONST[_name] = (_at, _at + _w)
    _at += _w
NCONST = _at


def constants():
    import numpy as np
    k = np.zeros((128, NCONST), np.float32)
    p = np.arange(128)

    def put(name, a):
        lo, hi = CONST[name]
        k[:a.shape[0], lo:hi] = a.reshape(a.shape[0], hi - lo)

    put("ident", np.eye(128))
    put("pairavg", 0.5 * (p[:, None] // 2 == p[None, :] // 2))
    own = (p[:, None] // C == np.arange(B * NH)[None] // NH) & (p[:, None] % C // HD == np.arange(B * NH)[None] % NH)
    put("qmask", -(HD ** -0.5) * own)
    put("vmask", 1.0 * (p[:, None] // IMG == np.arange(B * C)[None] % C // HD))
    put("eye32", 1.0 * (p[:, None] % IMG == np.arange(IMG)[None]))
    qw, kw = p[:, None] % IMG, np.arange(IMG)[None]
    first = np.clip(qw - KW // 2, 0, IMG - KW)
    put("outside", OUTSIDE * ((kw < first) | (kw >= first + KW)))
    row, u = np.arange(NH * RW)[:, None, None], np.arange(2 * IMG - 1)[None, None, :]
    put("shift", 1.0 * ((row // RW == np.arange(NH)[None, :, None]) & (row % RW == KW - 1 - (u - (IMG - 1)))))
    put("fold", 1.0 * (p[:, None] % C == np.arange(C)[None]))
    put("ones", np.ones((128, 128)))
    put("step4", 4.0 * np.arange(NB)[None])
    return k


def first_row(r):
    return min(max(r - KW // 2, 0), IMG - KW)


ROWS = 8
GROUPS = IMG // ROWS
LANES = ROWS * IMG


def key_rows(g):
    out = []
    for kr in range(IMG):
        qs = [q for q in range(ROWS * g, ROWS * g + ROWS) if first_row(q) <= kr < first_row(q) + KW]
        runs = []
        for q in qs:
            if runs and len(runs[-1]) > 1 and first_row(q) - first_row(q - 1) != first_row(runs[-1][1]) - first_row(runs[-1][0]):
                runs.append([q])
            elif runs:
                runs[-1].append(q)
            else:
                runs.append([q])
        out += [(kr, run) for run in runs]
    return out


def build(nc, x, w_qkv, b_qkv, rpb, w_proj, b_proj, ln_w, ln_b, w1, b1, w2, b2, wq, wk, wv, wo,
          attn_mask, ffn_mask, const, out):
    ctx = ExitStack()
    with ctx:
        def sb(name, shape, dt=F32):
            return ctx.enter_context(nc.sbuf_tensor(name, shape, dt))

        def sem(name):
            return ctx.enter_context(nc.semaphore(name))

        konst = sb("konst", [128, NCONST])

        def kc(name, rows=128):
            lo, hi = CONST[name]
            return konst[0:rows, lo:hi]

        ident = kc("ident")
        xtok = sb("xtok", [128, NT, B, C])
        wqkv = sb("wqkv", [128, 3, B, C])
        wpr = sb("wpr", [128, B, C])
        qkb = sb("qkb", [128, 2])
        vb = sb("vb", [C, 1])
        pb = sb("pb", [128, C])
        brow = sb("brow", [128, C])
        lnw = sb("lnw", [128, C])
        lnb = sb("lnb", [128, C])
        rpbt = sb("rpbt", [NH * RW, RW])
        bias = sb("bias", [128, RW, IMG])
        gstat = sb("gstat", [128, 2, 6])
        gmv = sb("gmv", [128, 2])
        gtmp = sb("gtmp", [128, 6])
        qbm = sb("qbm", [128, B * NH])
        gnT = sb("gnT", [128, N])
        kT = sb("kT", [128, N])
        big = sb("big", [128, NT * N])
        qbd = big[:, :].rearrange("p (r b h w) -> p r b h w", r=IMG, b=B, h=NH)
        vbd = sb("vbd", [128, IMG, B, C])
        sneg = sb("sneg", [128, 4, WIN])
        nmax = sb("nmax", [128, IMG * B])
        psumr = sb("psumr", [128, IMG * B])
        prinv = sb("prinv", [128, IMG, B])
        prob = sb("prob", [128, 3, 4 * WIN])
        probT = sb("probT", [128, 2, ROWS, B, WIN])
        dinv = sb("dinv", [128, 2, B, ROWS, IMG])
        rbs = sb("rbs", [128, 2, LANES])
        att = sb("att", [128, N])
        t1 = sb("t1", [128, NT, B, C])
        cen = sb("cen", [128, NT, B, C])
        sq = sb("sq", [128, NT, B, C])
        lst = sb("lst", [128, 8, NT * B])
        xh = sb("xh", [128, B, N], F32R)
        xl = sb("xl", [128, B, N], F32R)
        xa = sb("xa", [128, B, N], F32R)
        sim1 = sb("sim1", [128, NT * N])
        rsum = sb("rsum", [128, B * NT])
        rinv = sb("rinv", [128, B * NT])
        csum = sb("csum", [128, B * NT])
        cinv = sb("cinv", [128, B * NT])
        xc = sb("xc", [128, NT, C])
        w1s = sb("w1s", [128, HID])
        w2s = sb("w2s", [128, 2, C])
        b1s = sb("b1s", [128, 2])
        b2s = sb("b2s", [128, 1])
        w1z = sb("w1z", [128, B, HID])
        w2l = sb("w2l", [128, 2, C])
        b1l = sb("b1l", [128, 2])
        b2l = sb("b2l", [128, 1])
        aw = sb("aw", [128, 4, B, C])
        m8 = sb("m8", [1, 2, NB * NOPS], U8)
        code = sb("code", [1, NOPS * NB])
        mx8 = sb("mx8", [1, 8])
        ix8 = sb("ix8", [1, 8], U32)
        keyf = sb("keyf", [1, 1])
        kcand = sb("kcand", [1, 2, NB])
        ctl = sb("ctl", [1, 1], I32)

        sims = [big, sim1]
        spare = probT[:, :, :, :, :].rearrange("p g r b w -> p (g r b w)")
        rr = spare[:, 0:3 * N].rearrange("p (i n) -> p i n", i=3)
        ff = spare[:, 3 * N:5 * N].rearrange("p (i n) -> p i n", i=2)
        us = spare[:, 5 * N:6 * N]
        dia = vbd[:, 0:NT, :, :].rearrange("p t b c -> p t (b c)")
        tokens = dict(t=NT, b=B, c=C)
        a = gnT[:, :].rearrange("p (t b c) -> p t b c", **tokens)
        xn = kT[:, :].rearrange("p (t b c) -> p t b c", **tokens)
        flatp = prob[:, :, :].rearrange("p i w -> p (i w)")
        t2 = flatp[:, 0:N].rearrange("p (t b c) -> p t b c", **tokens)
        mf = flatp[0:1, N:N + 2 * NB * NOPS].rearrange("u (i n) -> u i n", i=2)
        H = att[:, :]
        shifts = sim1[0:NH * RW, 0:IMG * NH * IMG].rearrange("p (k m) -> p k m", k=IMG)
        xn2 = big[:, 0:2 * NT * B * C].rearrange("p (t b w) -> p t b w", t=NT, b=B)
        z = big[:, 0:8 * 512].rearrange("p (j b m n) -> p j b m n", j=2, b=B, m=2)
        aq, ak, av, ao, ap_, apt = (sim1[:, i * N:(i + 1) * N] for i in range(6))
        am_stat = lst[:, 0, 0:4]

        PS = ctx.enter_context(nc.psum_tensor("PS", [128, 8 * 512], F32))

        def bank(i, n=1):
            return PS[:, 512 * i:512 * (i + n)]

        d_x, d_const, d_wqkv, d_qkb, d_rpb = sem("d_x"), sem("d_const"), sem("d_wqkv"), sem("d_qkb"), sem("d_rpb")
        d_wpr, d_rows, d_mask, d_w, d_aw, d_out = sem("d_wpr"), sem("d_rows"), sem("d_mask"), sem("d_w"), sem("d_aw"), sem("d_out")
        zeroed, held = sem("zeroed"), sem("held")
        pe_xT, pe_tab, pe_vb, pe_avg, pe_q, pe_k = sem("pe_xT"), sem("pe_tab"), sem("pe_vb"), sem("pe_avg"), sem("pe_q"), sem("pe_k")
        pe_s, pe_v, pe_rb, pe_pv, pe_pr = sem("pe_s"), sem("pe_v"), sem("pe_rb"), sem("pe_pv"), sem("pe_pr")
        pe_nT, pe_sim, pe_rB, pe_u, pe_y = sem("pe_nT"), sem("pe_sim"), sem("pe_rB"), sem("pe_u"), sem("pe_y")
        pe_hT, pe_row, pe_z, pe_h, pe_oT = sem("pe_hT"), sem("pe_row"), sem("pe_z"), sem("pe_h"), sem("pe_oT")
        pe_aqkv, pe_asc, pe_atr, pe_ao, pe_ay = sem("pe_aqkv"), sem("pe_asc"), sem("pe_atr"), sem("pe_ao"), sem("pe_ay")
        chain, dve_shift = sem("chain"), sem("dve_shift")
        dve_brow, dve_avg, dve_var, dve_gn, dve_tab, dve_qb = (sem("dve_brow"), sem("dve_avg"), sem("dve_var"),
                                                              sem("dve_gn"), sem("dve_tab"), sem("dve_qb"))
        dve_q, dve_s, dve_v, dve_t, dve_ri, dve_att, dve_t1 = (sem("dve_q"), sem("dve_s"), sem("dve_v"), sem("dve_t"),
                                                               sem("dve_ri"), sem("dve_att"), sem("dve_t1"))
        dve_c, dve_ve, dve_xn, dve_xa, dve_dia, dve_r, dve_xc, dve_y, dve_h0 = (
            sem("dve_c"), sem("dve_ve"), sem("dve_xn"), sem("dve_xa"), sem("dve_dia"), sem("dve_r"), sem("dve_xc"),
            sem("dve_y"), sem("dve_h0"))
        h_ready, decided, w_live, dve_z, dve_o = sem("h_ready"), sem("decided"), sem("w_live"), sem("dve_z"), sem("dve_o")
        dve_aqkv, dve_amx, dve_apn, dve_apt, dve_ao = (sem("dve_aqkv"), sem("dve_amx"), sem("dve_apn"), sem("dve_apt"),
                                                       sem("dve_ao"))
        act_sd, act_q, act_k, act_p, act_rb = sem("act_sd"), sem("act_q"), sem("act_k"), sem("act_p"), sem("act_rb")
        act_sq, act_sqrt, act_xh, act_e, act_f, act_us = (sem("act_sq"), sem("act_sqrt"), sem("act_xh"), sem("act_e"),
                                                          sem("act_f"), sem("act_us"))
        act_z, act_ap = sem("act_z"), sem("act_ap")
        pool_xb, pool_d = sem("pool_xb"), sem("pool_d")

        w1_v = w1.rearrange("s o c h -> (s o) c h")
        w2_v = w2.rearrange("s o (k p) d -> (s o) p k d", p=128)
        b1_v = b1.rearrange("s o (m p) -> (s o) p m", p=128)
        b2_v = b2.rearrange("s o (d u) -> (s o) d u", u=1)
        aw_v = [w.rearrange("s o c d -> (s o) c d") for w in (wq, wk, wv, wo)]
        x_v = x.rearrange("b h w c -> b (h w) c").rearrange("b (t p) c -> b p t c", p=128)
        out_v = out.rearrange("b h w c -> b (h w) c").rearrange("b (t p) c -> b p t c", p=128)
        NQ = 2
        HALF = N // NQ

        def pending(eng, reg):
            k = eng.snap(reg, min_val=0, max_val=4 * NB - 1)
            return k

        def hold(eng, s, value):
            eng.wait_ge(s, value)
            eng.sem_inc(held, 1)

        block = ctx.enter_context(nc.Block())

        @block.sync
        def _(sp):
            for b in range(B):
                sp.dma_start(xtok[:, :, b, :], x_v[b]).then_inc(d_x, 16)
            sp.dma_start(konst[:, :], const).then_inc(d_const, 16)
            sp.wait_ge(zeroed, 1)
            for b in range(B):
                sp.dma_start(wqkv[C * b:C * b + C, :, b, :],
                             w_qkv.rearrange("c (k d) -> c k d", k=3)).then_inc(d_wqkv, 16)
            for h in range(NH):
                sp.dma_start(rpbt[RW * h:RW * h + RW, :], rpb[h].rearrange("i j -> j i"),
                             allow_slow_non_contiguous=True).then_inc(d_rpb, 16)
            for b in range(B):
                sp.dma_start(qkb[C * b:C * b + C, :], b_qkv[0:2 * C].rearrange("(k d) -> d k", k=2),
                             allow_slow_non_contiguous=True).then_inc(d_qkb, 16)
            for b in range(B):
                sp.dma_start(wpr[C * b:C * b + C, b, :], w_proj).then_inc(d_wpr, 16)
            sp.dma_start(vb[:, :], b_qkv[2 * C:3 * C].rearrange("(d u) -> d u", u=1)).then_inc(d_rows, 16)
            for dst, src in ((pb, b_proj), (lnw, ln_w), (lnb, ln_b)):
                sp.dma_start(dst[:, :], src.rearrange("(u d) -> u d", u=1).broadcast_to([128, C])).then_inc(d_rows, 16)
            for i, src in enumerate((attn_mask, ffn_mask)):
                sp.dma_start(m8[0:1, i, :], src.rearrange("s o -> (s o)").rearrange("(u n) -> u n", u=1)).then_inc(d_mask, 16)

            n = sp.alloc_register("sp_n")
            nf = sp.alloc_register("sp_nf")
            na = sp.alloc_register("sp_na")
            for r in (n, nf, na):
                sp.reg_mov(r, 0)
            key = sp.alloc_register("sp_key")
            sp.wait_ge(decided, 1)
            sp.reg_load(key, ctl[0:1, 0:1])
            with sp.While(lambda: sp.snap(key) < 4 * NB):
                k = pending(sp, key)
                op = sp.value_load(ix8[0:1, 0:1], min_val=0, max_val=NOPS - 1)
                row = sp.snap((k // 4) * NOPS + op, min_val=0, max_val=NB * NOPS - 1)
                with sp.If(k % 2 == 1):
                    sp.wait_ge(pe_ay, sp.snap(na) * NQ + 1)
                    for i in range(4):
                        for b in range(B):
                            sp.dma_start(aw[C * b:C * b + C, i, b, :],
                                         aw_v[i][bass.ds(row, 1), :, :].rearrange("u c d -> (u c) d")).then_inc(d_aw, 16)
                    sp.reg_add(na, na, 1)
                with sp.If((k // 2) % 2 == 1):
                    sp.wait_ge(w_live, sp.snap(nf) + 1)
                    for b in range(B):
                        sp.dma_start(w1s[C * b:C * b + C, :],
                                     w1_v[bass.ds(row, 1), :, :].rearrange("u c h -> (u c) h")).then_inc(d_w, 16)
                    sp.dma_start(b1s[:, :], b1_v[bass.ds(row, 1), :, :].rearrange("u p m -> (u p) m"),
                                 allow_slow_non_contiguous=True).then_inc(d_w, 16)
                    sp.dma_start(w2s[:, :, :], w2_v[bass.ds(row, 1), :, :, :].rearrange("u p k d -> (u p) k d")).then_inc(d_w, 16)
                    for b in range(B):
                        sp.dma_start(b2s[C * b:C * b + C, :],
                                     b2_v[bass.ds(row, 1), :, :].rearrange("u p m -> (u p) m")).then_inc(d_w, 16)
                    sp.reg_add(nf, nf, 1)
                sp.reg_add(n, n, 1)
                hold(sp, decided, sp.snap(n) + 1)
                sp.reg_load(key, ctl[0:1, 0:1])

            for j in range(NQ):
                sp.wait_ge(dve_o, j + 1)
                for b in range(B):
                    sp.dma_start(out_v[b][:, 4 * j:4 * j + 4, :], cen[:, 4 * j:4 * j + 4, b, :]).then_inc(d_out, 16)
            sp.wait_ge(d_out, 16 * B * NQ)

        @block.gpsimd
        def _(pool):
            nc.gpsimd.memset(wqkv[:, :, :, :], 0.0)
            nc.gpsimd.memset(wpr[:, :, :], 0.0)
            nc.gpsimd.memset(w1z[:, :, :], 0.0)
            nc.gpsimd.memset(aw[:, :, :, :], 0.0)
            nc.gpsimd.memset(keyf[:, :], -1.0)
            pool.drain()
            pool.sem_inc(zeroed, 1)
            pool.wait_ge(zeroed, 1)
            nc.gpsimd.memset(qbd[0:C, :, 1, :, :], 0.0).then_inc(zeroed, 1)
            pool.wait_ge(zeroed, 2)
            nc.gpsimd.memset(qbd[C:2 * C, :, 0, :, :], 0.0).then_inc(zeroed, 1)
            pool.wait_ge(zeroed, 3)
            pool.wait_ge(d_x, 16 * B)
            pool.wait_ge(pe_xT, NT)
            pool.wait_ge(dve_brow, 1)
            nc.gpsimd.tensor_tensor(xtok[:, :, :, :].rearrange("p t b c -> p (t b) c"),
                                    xtok[:, :, :, :].rearrange("p t b c -> p (t b) c"),
                                    brow[:, :].unsqueeze(1).broadcast_to([128, NT * B, C]), ALU.add).then_inc(pool_xb, 1)
            pool.wait_ge(d_const, 16)
            for g in range(GROUPS):
                pool.wait_ge(dve_ri, g + 1)
                if g >= 2:
                    pool.wait_ge(pe_rb, g - 1)
                for b in range(B):
                    ins = nc.gpsimd.tensor_tensor(
                        dinv[:, g % 2, b, :, :],
                        kc("eye32").unsqueeze(1).broadcast_to([128, ROWS, IMG]),
                        prinv[:, ROWS * g:ROWS * g + ROWS, b].unsqueeze(2).broadcast_to([128, ROWS, IMG]), ALU.mult)
                ins.then_inc(pool_d, 1)

        @block.tensor
        def _(pe):
            pe.sem_inc(pe_ay, 1)
            pe.wait_ge(d_const, 16)
            pe.wait_ge(d_x, 16 * B)
            for t in range(NT):
                nc.tensor.transpose(PS[:, 128 * t:128 * t + 128], xtok[:, t, :, :].rearrange("p b c -> p (b c)"),
                                    ident).then_inc(pe_xT, 1)
            pe.wait_ge(d_rpb, 16 * NH)
            pe.wait_ge(dve_shift, 1)
            for kw in range(IMG):
                ins = nc.tensor.matmul(bank(3)[:, RW * kw:RW * kw + RW], shifts[:, IMG - 1 - kw, :],
                                       rpbt[:, :], start=True, stop=True)
            ins.then_inc(pe_tab, 1)
            pe.wait_ge(dve_avg, 1)
            nc.tensor.matmul(bank(2)[:, 0:1], kc("pairavg"), gmv[:, 0:1], start=True, stop=True).then_inc(pe_avg, 1)
            pe.wait_ge(d_wpr, 16 * B)
            pe.wait_ge(d_rows, 16 * 4)
            nc.tensor.matmul(bank(4)[:, 0:C], vb[:, 0:1].broadcast_to([C, 128]), wpr[0:C, 0, :],
                             start=True, stop=True).then_inc(pe_vb, 1)
            pe.wait_ge(dve_avg, 2)
            nc.tensor.matmul(bank(2)[:, 1:2], kc("pairavg"), gtmp[:, 1:2], start=True, stop=True).then_inc(pe_avg, 1)
            pe.wait_ge(dve_brow, 1)
            pe.wait_ge(d_wqkv, 16 * B)
            for j in range(NQ):
                pe.wait_ge(dve_gn, j + 1)
                cols = gnT[:, HALF * j:HALF * j + HALF]
                nc.tensor.matmul(bank(4 + j), wqkv[:, 0, :, :].rearrange("p b c -> p (b c)"), cols,
                                 start=True, stop=True).then_inc(pe_q, 1)
                nc.tensor.matmul(bank(6 + j), wqkv[:, 1, :, :].rearrange("p b c -> p (b c)"), cols,
                                 start=True, stop=True).then_inc(pe_k, 1)

            def values(r):
                for h in range(NH):
                    ins = nc.tensor.matmul(bank(0, 2)[IMG * h:IMG * h + IMG, IMG * r:IMG * r + IMG],
                                           gnT[:, IMG * r:IMG * r + IMG], wqkv[:, 2, :, HD * h:HD * h + HD],
                                           start=True, stop=True)
                if r % 16 == 15:
                    ins.then_inc(pe_v, 1)

            def scores(r):
                if r >= 2:
                    pe.wait_ge(dve_s, B * (r - 1))
                for b in range(B):
                    i = B * r + b
                    ins = nc.tensor.matmul(bank(2 + r % 2)[:, 256 * b:256 * b + WIN],
                                     qbd[:, r, b, :, :].rearrange("p h w -> p (h w)"),
                                     kT[:, IMG * first_row(r):IMG * first_row(r) + WIN],
                                     start=True, stop=True)
                ins.then_inc(pe_s, 1)

            def norms(g):
                pe.wait_ge(pool_d, g + 1)
                if g >= 1:
                    pe.wait_ge(act_rb, g)
                for b in range(B):
                    ins = nc.tensor.matmul(bank(6)[C * b:C * b + C, 0:LANES], kc("vmask")[:, 0:C],
                                           dinv[:, g % 2, b, :, :].rearrange("p r w -> p (r w)"), start=True, stop=True)
                ins.then_inc(pe_rb, 1)

            def weighted(g):
                pieces = key_rows(g)
                begun = set()
                for n, (kr, run) in enumerate(pieces):
                    q0, nq = run[0] - ROWS * g, len(run)
                    for b in range(B):
                        base = (q0 * B + b) * WIN + (kr - first_row(run[0])) * IMG
                        step = B * WIN if nq == 1 else B * WIN - IMG * (first_row(run[1]) - first_row(run[0]))
                        flat = probT[:, g % 2, :, :, :].rearrange("p r b w -> p (r b w)")
                        if nq == 1:
                            rhs = flat[:, base:base + IMG]
                        else:
                            rhs = bass.AP(flat.tensor, flat.offset + base, [flat.ap[0], [step, nq], [1, IMG]])
                        ins = nc.tensor.matmul(bank(4 + g % 2)[C * b:C * b + C, IMG * q0:IMG * (q0 + nq)],
                                               vbd[:, kr, b, :], rhs, start=b not in begun, stop=n == len(pieces) - 1,
                                               skip_group_check=True)
                        begun.add(b)
                    if n == len(pieces) - 1:
                        ins.then_inc(pe_pv, 1)
                    yield

            def project(g):
                pe.wait_ge(dve_att, g + 1)
                for t in (2 * g, 2 * g + 1):
                    ins = nc.tensor.matmul(bank(7)[:, 128 * (t % 4):128 * (t % 4) + 128], att[:, 128 * t:128 * t + 128],
                                           wpr[:, :, :].rearrange("p b c -> p (b c)"), start=True, stop=True)
                ins.then_inc(pe_pr, 1)

            pe.wait_ge(dve_tab, 1)
            for j in range(NQ):
                pe.wait_ge(act_k, 1)
            work = None
            for r in range(IMG):
                if r % (IMG // 2) == 0:
                    pe.wait_ge(act_q, r // (IMG // 2) + 1)
                    pe.wait_ge(dve_q, r // (IMG // 2) + 1)
                if first_row(r) + KW > IMG // 2 and (r == 0 or first_row(r - 1) + KW <= IMG // 2):
                    pe.wait_ge(act_k, 2)
                scores(r)
                if r % 8 in (1, 2, 3, 4) and r < 16:
                    for rv in range(16 * (r // 8) + 4 * (r % 8 - 1), 16 * (r // 8) + 4 * (r % 8)):
                        values(rv)
                g = r // ROWS
                if g >= 1:
                    if r % ROWS == 2:
                        norms(g - 1)
                        pe.wait_ge(dve_t, 4 * g)
                        pe.wait_ge(dve_v, min(g, 2))
                        if g == 1:
                            pe.wait_ge(act_q, 2)
                            pe.wait_ge(dve_q, 2)
                            pe.wait_ge(act_k, 2)
                        work = weighted(g - 1)
                    if r % ROWS >= 2:
                        for _ in range(4):
                            next(work, None)
                    if r % ROWS == 7:
                        for _ in work:
                            pass
                        project(g - 1)
            norms(GROUPS - 1)
            pe.wait_ge(dve_t, 4 * GROUPS)
            for _ in weighted(GROUPS - 1):
                pass
            project(GROUPS - 1)

            pe.wait_ge(dve_t1, GROUPS)
            for b in range(B):
                pe.wait_ge(dve_xn, 1)
                for t in range(NT):
                    ins = nc.tensor.transpose(bank(6 * b, 2)[:, 128 * t:128 * t + 128],
                                              xn2[:, t, b, :], ident)
                ins.then_inc(pe_nT, 1)

            def similarities(b, m):
                i = NT * b + m
                if m == 0:
                    pe.wait_ge(dve_xa, b + 1)
                if i >= 2:
                    pe.wait_ge(act_e, i - 1)
                for part, lhs in enumerate((xh, xl)):
                    for j in range(NQ):
                        ins = nc.tensor.matmul(bank(2 + 2 * (i % 2) + j), lhs[:, b, 128 * m:128 * m + 128],
                                               xa[:, b, HALF * j:HALF * j + HALF], start=part == 0, stop=part == 1)
                ins.then_inc(pe_sim, 1)

            def row_norms(b):
                pe.wait_ge(dve_dia, b + 1)
                for j in range(NQ):
                    ins = nc.tensor.matmul(bank(j), kc("ones"), dia[:, 4 * j:4 * j + 4, :].rearrange("p t n -> p (t n)"),
                                           start=True, stop=True)
                ins.then_inc(pe_rB, 1)

            def gathered(b, m):
                i = NT * b + m
                pe.wait_ge(dve_r, i + 1)
                if m == 0 and b == 1:
                    pe.wait_ge(act_us, 1)
                if m == 0 and b == 0:
                    pe.wait_ge(dve_xa, 2)
                pe.wait_ge(act_f, i + 1)
                pe.wait_ge(dve_xc, i + 1)
                for j in range(NQ):
                    cols = slice(HALF * j, HALF * j + HALF)
                    nc.tensor.matmul(bank(6 + j)[0:C, :], a[:, m, b, :], rr[:, i % 3, cols], start=m == 0, stop=m == NT - 1)
                    ins = nc.tensor.matmul(bank(6 + j)[C:2 * C, :], xc[:, m, :], ff[:, i % 2, cols],
                                           start=m == 0, stop=m == NT - 1)
                ins.then_inc(pe_u, 1)

            def to_tokens(b):
                pe.wait_ge(act_us, b + 1)
                for t in range(NT):
                    ins = nc.tensor.matmul(bank(0)[:, C * t:C * t + C], us[:, 128 * t:128 * t + 128], kc("fold"),
                                           start=True, stop=True)
                ins.then_inc(pe_y, 1)

            for m in range(NT):
                similarities(0, m)
            similarities(1, 0)
            similarities(1, 1)
            row_norms(0)
            for m in range(2, 6):
                similarities(1, m)
            for m in range(NT):
                gathered(0, m)
            similarities(1, 6)
            similarities(1, 7)
            to_tokens(0)
            pe.wait_ge(dve_y, 1)
            row_norms(1)
            for m in range(NT):
                gathered(1, m)
            to_tokens(1)

            for j in range(NQ):
                pe.wait_ge(dve_y, 2)
                pe.wait_ge(dve_h0, 2)
                for t in range(4 * j, 4 * j + 4):
                    ins = nc.tensor.transpose(bank(6 + j)[:, 128 * (t % 4):128 * (t % 4) + 128],
                                              xn[:, t, :, :].rearrange("p b c -> p (b c)"), ident)
                ins.then_inc(pe_hT, 1)

            def decide_row(count):
                pe.wait_ge(h_ready, count)
                nc.tensor.transpose(bank(1)[0:1, 0:C], H[0:C, 0:1], ident[0:C, 0:C]).then_inc(pe_row, 1)

            decide_row(1)
            n, nf, na, hv = (pe.alloc_register(f"pe_{s}") for s in ("n", "nf", "na", "hv"))
            for r in (n, nf, na):
                pe.reg_mov(r, 0)
            pe.reg_mov(hv, NQ)
            key = pe.alloc_register("pe_key")
            pe.wait_ge(decided, 1)
            pe.reg_load(key, ctl[0:1, 0:1])
            with pe.While(lambda: pe.snap(key) < 4 * NB):
                k = pending(pe, key)
                with pe.If(k % 2 == 1):
                    done = pe.snap(na)
                    hold(pe, d_aw, done * (16 * 4 * B) + 16 * 4 * B)
                    pe.wait_ge(h_ready, pe.snap(hv))
                    for i in range(2):
                        for j in range(NQ):
                            nc.tensor.matmul(bank(2 * i + j), aw[:, i, :, :].rearrange("p b c -> p (b c)"),
                                             H[:, HALF * j:HALF * j + HALF], start=True, stop=True)
                    for t in range(NT):
                        ins = nc.tensor.matmul(bank(4, 2)[:, 128 * t:128 * t + 128], H[:, 128 * t:128 * t + 128],
                                               aw[:, 2, :, :].rearrange("p b c -> p (b c)"), start=True, stop=True)
                    ins.then_inc(pe_aqkv, 1)
                    pe.wait_ge(dve_aqkv, done + 1)
                    for u in range(B * NT):
                        b, t = u // NT, u % NT
                        if u:
                            pe.wait_ge(act_ap, done * (B * NT) + u)
                        for j in range(NQ):
                            ins = nc.tensor.matmul(bank(j), aq[C * b:C * b + C, 128 * t:128 * t + 128],
                                                   ak[C * b:C * b + C, HALF * j:HALF * j + HALF], start=True, stop=True)
                        ins.then_inc(pe_asc, 1)
                        pe.wait_ge(dve_apn, done * (B * NT) + u + 1)
                        for kt in range(NT):
                            ins = nc.tensor.transpose(bank(2, 2)[:, 128 * kt:128 * kt + 128],
                                                      ap_[:, 128 * kt:128 * kt + 128], ident)
                        ins.then_inc(pe_atr, 1)
                        pe.wait_ge(dve_apt, done * (B * NT) + u + 1)
                        for kt in range(NT):
                            ins = nc.tensor.matmul(bank(4, 2)[C * b:C * b + C, 128 * t:128 * t + 128],
                                                   av[:, 128 * kt + C * b:128 * kt + C * b + C],
                                                   apt[:, 128 * kt:128 * kt + 128], start=kt == 0, stop=kt == NT - 1)
                        ins.then_inc(pe_ao, 1)
                    pe.wait_ge(dve_ao, done + 1)
                    for j in range(NQ):
                        nc.tensor.matmul(bank(6 + j), aw[:, 3, :, :].rearrange("p b c -> p (b c)"),
                                         ao[:, HALF * j:HALF * j + HALF], start=True, stop=True).then_inc(pe_ay, 1)
                    pe.reg_add(na, na, 1)
                    pe.reg_add(hv, hv, NQ)
                with pe.If((k // 2) % 2 == 0):
                    hold(pe, h_ready, pe.snap(hv))
                    decide_row(1)
                with pe.If((k // 2) % 2 == 1):
                    done = pe.snap(nf)
                    have = pe.snap(hv)
                    pe.wait_ge(w_live, done + 2)
                    for j in range(NQ):
                        pe.wait_ge(h_ready, have + (j - 1))
                        for b in range(B):
                            for mc in range(2):
                                nc.tensor.matmul(bank(4 * j + 2 * b + mc), w1z[:, b, 128 * mc:128 * mc + 128],
                                                 H[:, HALF * j:HALF * j + HALF], start=True, stop=True).then_inc(pe_z, 1)
                        if j == 1:
                            hold(pe, h_ready, have + 1)
                            decide_row(1)
                        pe.wait_ge(act_z, done * 4 + 2 * j + 2)
                        pe.wait_ge(dve_z, done * 4 + 2 * j + 2)
                        for kc_ in range(2):
                            for b in range(B):
                                ins = nc.tensor.matmul(bank(4 * j)[C * b:C * b + C, :], w2l[:, kc_, :], z[:, j, b, kc_, :],
                                                       start=kc_ == 0, stop=kc_ == 1)
                        ins.then_inc(pe_h, 1)
                    pe.reg_add(nf, nf, 1)
                    pe.reg_add(hv, hv, NQ)
                pe.reg_add(n, n, 1)
                hold(pe, decided, pe.snap(n) + 1)
                pe.reg_load(key, ctl[0:1, 0:1])

            have = pe.snap(hv)
            for j in range(NQ):
                pe.wait_ge(h_ready, have + (j - 1))
                for t in range(4 * j, 4 * j + 4):
                    ins = nc.tensor.transpose(bank(2 + j)[:, 128 * (t % 4):128 * (t % 4) + 128],
                                              H[:, 128 * t:128 * t + 128], ident)
                ins.then_inc(pe_oT, 1)

        @block.scalar
        def _(act):
            act.wait_ge(dve_var, 1)
            nc.scalar.activation(gtmp[:, 3:4], gtmp[:, 2:3], ACT.Sqrt).then_inc(act_sd, 1)
            act.wait_ge(dve_qb, 1)
            act.wait_ge(zeroed, 3)
            for j in range(NQ):
                rows = slice(IMG // 2 * j, IMG // 2 * (j + 1))
                act.wait_ge(pe_q, j + 1)
                for h in range(NH):
                    ins = nc.scalar.activation(qbd[0:C, rows, 0, h, :], bank(4 + j)[0:C, :].rearrange("p (r w) -> p r w", w=IMG),
                                               ACT.Identity, scale=kc("qmask", C)[:, h:h + 1], bias=qbm[0:C, h:h + 1])
                ins.then_inc(act_q, 1)
                act.wait_ge(pe_k, j + 1)
                nc.scalar.activation(kT[:, HALF * j:HALF * j + HALF], bank(6 + j), ACT.Identity,
                                     bias=qkb[:, 1:2]).then_inc(act_k, 1)
            for i in range(B * IMG):
                act.wait_ge(dve_s, i + 1)
                if i >= 12:
                    act.wait_ge(dve_t, i // 4 - 2)
                nc.scalar.activation(prob[:, i // 4 % 3, WIN * (i % 4):WIN * (i % 4) + WIN], sneg[:, i % 4, :], ACT.Exp,
                                     scale=-1.0, bias=nmax[:, i:i + 1], accum_out=psumr[:, i:i + 1]).then_inc(act_p, 1)
                if i % 16 == 7 and i > 16:
                    g = i // 16 - 1
                    act.wait_ge(pe_rb, g + 1)
                    if g >= 2:
                        act.wait_ge(dve_att, g - 1)
                    nc.scalar.activation(rbs[:, g % 2, :], bank(6)[:, 0:LANES], ACT.Copy).then_inc(act_rb, 1)
            g = GROUPS - 1
            act.wait_ge(pe_rb, g + 1)
            act.wait_ge(dve_att, g - 1)
            nc.scalar.activation(rbs[:, g % 2, :], bank(6)[:, 0:LANES], ACT.Copy).then_inc(act_rb, 1)

            def norm_parts(n, lo, hi, both):
                act.wait_ge(dve_c, n)
                nc.scalar.activation(sq[:, :, lo:hi, :], cen[:, :, lo:hi, :], ACT.Square).then_inc(act_sq, 1)
                act.wait_ge(dve_ve, n)
                cols = lst[:, :, :].rearrange("p k (t b) -> p k t b", b=B)[:, :, :, lo:hi]
                if both:
                    nc.scalar.activation(cols[:, 4], cols[:, 1], ACT.Sqrt)
                nc.scalar.activation(cols[:, 3], cols[:, 2], ACT.Sqrt).then_inc(act_sqrt, 1)

            norm_parts(1, 0, B, True)
            for b in range(B):
                act.wait_ge(pe_nT, b + 1)
                nc.scalar.activation(xh[:, b, :], bank(6 * b, 2), ACT.Copy).then_inc(act_xh, 1)

            def expsim(b, m):
                i = NT * b + m
                act.wait_ge(pe_sim, i + 1)
                nc.scalar.activation(sims[b][:, N * m:N * m + N], bank(2 + 2 * (i % 2), 2), ACT.Exp, scale=2.0,
                                     accum_out=rsum[:, i:i + 1]).then_inc(act_e, 1)

            def expcol(b, m):
                i = NT * b + m
                act.wait_ge(dve_r, i + 1)
                if i >= 2:
                    act.wait_ge(pe_u, i - 1)
                nc.scalar.activation(ff[:, i % 2, :], rr[:, i % 3, :], ACT.Exp, accum_out=csum[:, i:i + 1]).then_inc(act_f, 1)

            def take_sums(b):
                act.wait_ge(pe_u, NT * (b + 1))
                if b:
                    act.wait_ge(pe_y, b)
                nc.scalar.activation(us[:, :], bank(6, 2), ACT.Copy).then_inc(act_us, 1)

            for m in range(NT):
                expsim(0, m)
            for m in range(4):
                expsim(1, m)
            for m in range(NT):
                expcol(0, m)
            for m in range(4, NT):
                expsim(1, m)
            take_sums(0)
            norm_parts(2, 0, 1, False)
            norm_parts(3, 0, 1, False)
            for m in range(NT):
                expcol(1, m)
            take_sums(1)
            norm_parts(4, 1, 2, False)
            norm_parts(5, 1, 2, False)

            n, nf, na = (act.alloc_register(f"act_{s}") for s in ("n", "nf", "na"))
            for r in (n, nf, na):
                act.reg_mov(r, 0)
            key = act.alloc_register("act_key")
            act.wait_ge(decided, 1)
            act.reg_load(key, ctl[0:1, 0:1])
            with act.While(lambda: act.snap(key) < 4 * NB):
                k = pending(act, key)
                with act.If(k % 2 == 1):
                    done = act.snap(na)
                    for u in range(B * NT):
                        act.wait_ge(dve_amx, done * (B * NT) + u + 1)
                        nc.scalar.activation(ap_, bank(0, 2), ACT.Exp, scale=C ** -0.5, bias=am_stat[:, 1:2],
                                             accum_out=am_stat[:, 2:3]).then_inc(act_ap, 1)
                    act.reg_add(na, na, 1)
                with act.If((k // 2) % 2 == 1):
                    done = act.snap(nf)
                    act.wait_ge(w_live, done + 2)
                    for j in range(NQ):
                        for mc in range(2):
                            act.wait_ge(pe_z, done * 8 + 4 * j + mc + 1)
                            nc.scalar.activation(z[:, j, 0, mc, :], bank(4 * j + mc), ACT.Relu,
                                                 bias=b1l[:, mc:mc + 1]).then_inc(act_z, 1)
                    act.reg_add(nf, nf, 1)
                act.reg_add(n, n, 1)
                hold(act, decided, act.snap(n) + 1)
                act.reg_load(key, ctl[0:1, 0:1])

        @block.vector
        def _(dve):
            links = [0]

            def link(ins):
                links[0] += 1
                ins.then_inc(chain, 1)
                dve.wait_ge(chain, links[0])

            v = nc.vector
            dve.sem_inc(w_live, 1)
            dve.wait_ge(d_const, 16)
            compact = kc("shift", NH * RW)
            v.tensor_copy(sim1[0:NH * RW, 0:IMG * NH * IMG].rearrange("p (k h q) -> p k h q", k=IMG, h=NH),
                          bass.AP(compact.tensor, compact.offset, [compact.ap[0], [1, IMG], [2 * IMG - 1, NH], [1, IMG]])
                          ).then_inc(dve_shift, 1)
            for j in range(2):
                dve.wait_ge(pe_xT, 4 * j + 4)
                ins = v.bn_stats(gstat[:, j, :], bank(j))
            link(ins)
            v.bn_aggr(gmv[:, :], gstat[:, :, :].rearrange("p j s -> p (j s)")).then_inc(dve_avg, 1)
            dve.wait_ge(pe_avg, 1)
            link(v.tensor_tensor(gtmp[:, 0:1], gmv[:, 0:1], bank(2)[:, 0:1], ALU.subtract))
            link(v.tensor_tensor(gtmp[:, 1:2], gtmp[:, 0:1], gtmp[:, 0:1], ALU.mult))
            dve.wait_ge(dve_avg, 1)
            v.tensor_tensor(gtmp[:, 1:2], gtmp[:, 1:2], gmv[:, 1:2], ALU.add).then_inc(dve_avg, 1)
            dve.wait_ge(pe_vb, 1)
            v.tensor_tensor(brow[:, :], pb[:, :], bank(4)[:, 0:C], ALU.add).then_inc(dve_brow, 1)
            dve.wait_ge(d_const, 16)
            dve.wait_ge(d_qkb, 16 * B)
            v.tensor_scalar(qbm[:, :], kc("qmask"), qkb[:, 0:1], None, ALU.mult).then_inc(dve_qb, 1)
            dve.wait_ge(pe_avg, 2)
            v.tensor_scalar(gtmp[:, 2:3], bank(2)[:, 1:2], 1e-5, None, ALU.add).then_inc(dve_var, 1)
            dve.wait_ge(act_sd, 1)
            link(v.reciprocal(gtmp[:, 4:5], gtmp[:, 3:4]))
            for j in range(NQ):
                v.tensor_scalar(gnT[:, HALF * j:HALF * j + HALF], bank(j), bank(2)[:, 0:1], gtmp[:, 4:5],
                                ALU.subtract, ALU.mult).then_inc(dve_gn, 1)
            dve.wait_ge(pe_tab, 1)
            v.scalar_tensor_tensor(bias[:, :, :], bank(3)[:, 0:RW * IMG].rearrange("p (k d) -> p d k", d=RW), -1.0,
                                   kc("outside").unsqueeze(1).broadcast_to([128, RW, IMG]), ALU.mult, ALU.add).then_inc(dve_tab, 1)
            for j in range(NQ):
                rows = slice(IMG // 2 * j, IMG // 2 * (j + 1))
                dve.wait_ge(pe_q, j + 1)
                for h in range(NH):
                    ins = v.tensor_scalar(qbd[C:2 * C, rows, 1, h, :],
                                          bank(4 + j)[C:2 * C, :].rearrange("p (r w) -> p r w", w=IMG),
                                          qkb[C:2 * C, 0:1], kc("qmask")[C:2 * C, NH + h:NH + h + 1], ALU.add, ALU.mult)
                ins.then_inc(dve_q, 1)

            def take_values(c):
                dve.wait_ge(pe_v, c + 1)
                wide = [128, 16 * B, NH, HD]
                v.tensor_tensor(vbd[:, 16 * c:16 * c + 16, :, :].rearrange("p r b (h d) -> p (r b) h d", h=NH),
                                bank(c).rearrange("p (k d) -> p k d", d=HD).unsqueeze(2).broadcast_to(wide),
                                kc("vmask")[:, 0:C].rearrange("p (h d) -> p h d", h=NH).unsqueeze(1).broadcast_to(wide),
                                ALU.mult).then_inc(dve_v, 1)

            def shifted_scores(i):
                r = i // B
                d = first_row(r) - r + KW - 1
                dve.wait_ge(pe_s, r + 1)
                if i >= 4:
                    dve.wait_ge(act_p, i - 3)
                v.tensor_tensor_reduce(out=sneg[:, i % 4, :],
                                       in0=bank(2 + r % 2)[:, 256 * (i % B):256 * (i % B) + WIN],
                                       in1=bias[:, d:d + KW, :].rearrange("p d k -> p (d k)"), scale=1.0, scalar=3.0e38,
                                       op0=ALU.add, op1=ALU.min, accum_out=nmax[:, i:i + 1]).then_inc(dve_s, 1)

            def flip(c):
                g = c // 4
                dve.wait_ge(act_p, 4 * c + 4)
                if g >= 2:
                    dve.wait_ge(pe_pv, g - 1)
                v.transpose(probT[:, g % 2, 2 * (c % 4):2 * (c % 4) + 2, :, :].rearrange("p r b w -> p (r b w)"),
                            prob[:, c % 3, :]).then_inc(dve_t, 1)
                if c % 4 == 3:
                    v.reciprocal(prinv[:, ROWS * g:ROWS * g + ROWS, :].rearrange("p r b -> p (r b)"),
                                 psumr[:, 16 * g:16 * g + 16]).then_inc(dve_ri, 1)

            def normalise(g):
                dve.wait_ge(pe_pv, g + 1)
                dve.wait_ge(act_rb, g + 1)
                v.tensor_tensor(att[:, LANES * g:LANES * g + LANES], bank(4 + g % 2)[:, 0:LANES], rbs[:, g % 2, :],
                                ALU.mult).then_inc(dve_att, 1)

            def residual(g):
                dve.wait_ge(pe_pr, g + 1)
                dve.wait_ge(pool_xb, 1)
                v.tensor_tensor(t1[:, 2 * g:2 * g + 2, :, :].rearrange("p t b c -> p (t b c)"),
                                bank(7)[:, 256 * (g % 2):256 * (g % 2) + 256],
                                xtok[:, 2 * g:2 * g + 2, :, :].rearrange("p t b c -> p (t b c)"), ALU.add).then_inc(dve_t1, 1)

            dve.wait_ge(dve_tab, 1)
            for i in range(B * IMG):
                shifted_scores(i)
                if i % 4 == 3 and i >= 7:
                    flip(i // 4 - 1)
                if i in (15, 29):
                    take_values(i // 16)
                g = i // 16 - 1
                if i % 16 == 15 and g >= 0:
                    normalise(g)
                if i % 16 == 3 and g >= 1:
                    residual(g - 1)
            flip(15)
            residual(GROUPS - 2)
            normalise(GROUPS - 1)
            residual(GROUPS - 1)

            def stats(src, lo, hi, n, eps):
                w = hi - lo
                cols = lst[:, :, :].rearrange("p k (t b) -> p k t b", b=B)[:, :, :, lo:hi]
                wide = [128, NT, w, C]
                link(v.tensor_reduce(cols[:, 0], src[:, :, lo:hi, :], AX.X, ALU.add))
                link(v.tensor_scalar(cols[:, 0], cols[:, 0], 1.0 / C, None, ALU.mult))
                v.tensor_tensor(cen[:, :, lo:hi, :], src[:, :, lo:hi, :], cols[:, 0].unsqueeze(3).broadcast_to(wide),
                                ALU.subtract).then_inc(dve_c, 1)
                dve.wait_ge(act_sq, n)
                link(v.tensor_reduce(cols[:, 1], sq[:, :, lo:hi, :], AX.X, ALU.add))
                v.tensor_scalar(cols[:, 2], cols[:, 1], 1.0 / C, eps, ALU.mult, ALU.add).then_inc(dve_ve, 1)
                dve.wait_ge(act_sqrt, n)
                link(v.reciprocal(cols[:, 5], cols[:, 3]))
                return cols, wide

            dve.wait_ge(dve_t1, GROUPS)
            cols, wide = stats(t1, 0, B, 1, 1e-5)
            v.tensor_tensor(a[:, :, :, :], cen[:, :, :, :], cols[:, 5].unsqueeze(3).broadcast_to(wide), ALU.mult)
            link(v.tensor_tensor(cols[:, 6], cols[:, 4], cols[:, 5], ALU.mult))
            link(v.tensor_scalar(cols[:, 6], cols[:, 6], 1e-12, None, ALU.max))
            link(v.reciprocal(cols[:, 7], cols[:, 6]))
            link(v.tensor_tensor(cols[:, 6], cols[:, 7], cols[:, 5], ALU.mult))
            twice = [128, NT * B, 2, C]
            v.tensor_tensor(xn2.rearrange("p t b (k c) -> p (t b) k c", k=2),
                            cen[:, :, :, :].rearrange("p t b c -> p (t b) c").unsqueeze(2).broadcast_to(twice),
                            lst[:, 6, :].unsqueeze(2).unsqueeze(3).broadcast_to(twice), ALU.mult).then_inc(dve_xn, 1)
            for b in range(B):
                dve.wait_ge(act_xh, b + 1)
                link(v.tensor_tensor(xl[:, b, :], bank(6 * b, 2), xh[:, b, :].bitcast(F32), ALU.subtract))
                v.tensor_copy(xa[0:C, b, :], xh[0:C, b, :].bitcast(F32))
                v.tensor_copy(xa[C:2 * C, b, :], xl[C:2 * C, b, :].bitcast(F32)).then_inc(dve_xa, 1)
            dve.wait_ge(d_rows, 16 * 4)
            for b in range(B):
                dve.wait_ge(act_e, NT * (b + 1))
                if b:
                    dve.wait_ge(pe_rB, b)
                link(v.reciprocal(rinv[:, NT * b:NT * b + NT], rsum[:, NT * b:NT * b + NT]))
                v.tensor_tensor(dia[:, :, :], ident.unsqueeze(1).broadcast_to([128, NT, 128]),
                                rinv[:, NT * b:NT * b + NT].unsqueeze(2).broadcast_to([128, NT, 128]),
                                ALU.mult).then_inc(dve_dia, 1)
                dve.wait_ge(pe_rB, b + 1)

                def columns(m):
                    i = NT * b + m
                    dve.wait_ge(act_f, i + 1)
                    if b and m == 0:
                        dve.wait_ge(pe_u, NT)
                    link(v.reciprocal(cinv[:, i:i + 1], csum[:, i:i + 1]))
                    v.tensor_scalar(xc[:, m, :], a[:, m, b, :], cinv[:, i:i + 1], None, ALU.mult).then_inc(dve_xc, 1)

                for m in range(NT):
                    i = NT * b + m
                    if i >= 3:
                        dve.wait_ge(pe_u, i - 2)
                    v.tensor_tensor(rr[:, i % 3, :], sims[b][:, N * m:N * m + N], bank(0, 2), ALU.mult).then_inc(dve_r, 1)
                    if m:
                        columns(m - 1)
                columns(NT - 1)
                dve.wait_ge(pe_y, b + 1)
                if b == 0:
                    dve.wait_ge(dve_xn, 1)
                y = sq
                link(v.scalar_tensor_tensor(y[:, :, b, :], bank(0).rearrange("p (t c) -> p t c", c=C), -0.1, a[:, :, b, :],
                                            ALU.mult, ALU.add))
                cols, wide = stats(y, b, b + 1, 2 * b + 2, 1e-6)
                wide = [128, NT, C]
                link(v.tensor_tensor(y[:, :, b, :], cen[:, :, b, :], cols[:, 5].broadcast_to(wide), ALU.mult))
                link(v.tensor_tensor(y[:, :, b, :], y[:, :, b, :], lnw[:, :].unsqueeze(1).broadcast_to(wide), ALU.mult))
                link(v.tensor_tensor(y[:, :, b, :], y[:, :, b, :], lnb[:, :].unsqueeze(1).broadcast_to(wide), ALU.add))
                link(v.tensor_tensor(t2[:, :, b, :], y[:, :, b, :], t1[:, :, b, :], ALU.add))
                dve.nop().then_inc(dve_y, 1)
                cols, _ = stats(t2, b, b + 1, 2 * b + 3, 1e-5)
                v.tensor_tensor(xn[:, :, b, :], cen[:, :, b, :], cols[:, 5].broadcast_to(wide), ALU.mult).then_inc(dve_h0, 1)

            dve.wait_ge(d_mask, 16 * 2)
            dve.wait_ge(zeroed, 1)
            link(v.tensor_copy(mf[:, :, :], m8[:, :, :]))
            link(v.scalar_tensor_tensor(mf[0:1, 0, :], mf[0:1, 1, :], 2.0, mf[0:1, 0, :], ALU.mult, ALU.add))
            link(v.tensor_scalar(mf[0:1, 1, :], mf[0:1, 0, :], 0.0, DEAD, ALU.is_equal, ALU.mult))
            link(v.tensor_tensor(mf[0:1, 0, :], mf[0:1, 0, :], mf[0:1, 1, :], ALU.add))
            link(v.tensor_tensor(code[:, :].rearrange("u (o s) -> u s o", s=NB), mf[0:1, 0, :].rearrange("u (s o) -> u s o", o=NOPS),
                                 kc("step4", 1).unsqueeze(2).broadcast_to([1, NB, NOPS]), ALU.add))
            for j in range(NQ):
                dve.wait_ge(pe_hT, j + 1)
                v.tensor_copy(H[:, HALF * j:HALF * j + HALF], bank(6 + j)).then_inc(h_ready, 1)

            def decide():
                dve.drain()
                v.max(mx8[:, :], bank(1)[0:1, 0:NOPS])
                v.tensor_scalar(kcand[0:1, 0, :], kc("step4", 1), keyf[0:1, 0:1], DEAD, ALU.is_le, ALU.mult)
                dve.drain()
                v.max_index(ix8[:, :], mx8[:, :], bank(1)[0:1, 0:NOPS])
                dve.drain()
                op = dve.value_load(ix8[0:1, 0:1], min_val=0, max_val=NOPS - 1)
                v.tensor_tensor(kcand[0:1, 1, :], kcand[0:1, 0, :], code[0:1, bass.ds(op * NB, NB)], ALU.add)
                dve.drain()
                v.tensor_reduce(keyf[:, :], kcand[0:1, 1, :], AX.X, ALU.min)
                dve.drain()
                v.tensor_copy(ctl[:, :], keyf[:, :]).then_inc(decided, 1)
                dve.drain()

            dve.wait_ge(pe_row, 1)
            decide()
            n, nf, na = (dve.alloc_register(f"dve_{s}") for s in ("n", "nf", "na"))
            for r in (n, nf, na):
                dve.reg_mov(r, 0)
            key = dve.alloc_register("dve_key")
            dve.reg_load(key, ctl[0:1, 0:1])
            with dve.While(lambda: dve.snap(key) < 4 * NB):
                k = pending(dve, key)
                with dve.If(k % 2 == 1):
                    done = dve.snap(na)
                    dve.wait_ge(pe_aqkv, done + 1)
                    v.tensor_copy(aq, bank(0, 2))
                    v.tensor_copy(ak, bank(2, 2))
                    v.tensor_copy(av, bank(4, 2)).then_inc(dve_aqkv, 1)
                    for u in range(B * NT):
                        dve.wait_ge(pe_asc, done * (B * NT) + u + 1)
                        v.tensor_reduce(am_stat[:, 0:1], bank(0, 2), AX.X, ALU.max, negate=True)
                        dve.drain()
                        v.tensor_scalar(am_stat[:, 1:2], am_stat[:, 0:1], C ** -0.5, None, ALU.mult).then_inc(dve_amx, 1)
                        dve.wait_ge(act_ap, done * (B * NT) + u + 1)
                        v.reciprocal(am_stat[:, 3:4], am_stat[:, 2:3])
                        dve.drain()
                        v.tensor_scalar(ap_, ap_, am_stat[:, 3:4], None, ALU.mult).then_inc(dve_apn, 1)
                        dve.wait_ge(pe_atr, done * (B * NT) + u + 1)
                        v.tensor_copy(apt, bank(2, 2)).then_inc(dve_apt, 1)
                    dve.wait_ge(pe_ao, done * (B * NT) + B * NT)
                    v.tensor_copy(ao, bank(4, 2)).then_inc(dve_ao, 1)
                    for j in range(NQ):
                        dve.wait_ge(pe_ay, done * NQ + j + 2)
                        v.tensor_copy(H[:, HALF * j:HALF * j + HALF], bank(6 + j)).then_inc(h_ready, 1)
                    dve.reg_add(na, na, 1)
                with dve.If((k // 2) % 2 == 0):
                    hold(dve, pe_row, dve.snap(n) + 2)
                    decide()
                with dve.If((k // 2) % 2 == 1):
                    done = dve.snap(nf)
                    hold(dve, d_w, done * (16 * 6) + 16 * 6)
                    dve.drain()
                    for b in range(B):
                        v.tensor_copy(w1z[C * b:C * b + C, b, :], w1s[C * b:C * b + C, :])
                    v.tensor_copy(w2l[:, :, :], w2s[:, :, :])
                    v.tensor_copy(b1l[:, :], b1s[:, :])
                    v.tensor_copy(b2l[:, :], b2s[:, :]).then_inc(w_live, 1)
                    dve.drain()
                    for j in range(NQ):
                        for mc in range(2):
                            dve.wait_ge(pe_z, done * 8 + 4 * j + 2 + mc + 1)
                            v.tensor_scalar(z[:, j, 1, mc, :], bank(4 * j + 2 + mc), b1l[:, mc:mc + 1], 0.0,
                                            ALU.add, ALU.max).then_inc(dve_z, 1)
                        if j == 1:
                            hold(dve, pe_row, dve.snap(n) + 2)
                            decide()
                        dve.wait_ge(pe_h, done * NQ + j + 1)
                        v.tensor_scalar(H[:, HALF * j:HALF * j + HALF], bank(4 * j), b2l[:, 0:1], None,
                                        ALU.add).then_inc(h_ready, 1)
                    dve.reg_add(nf, nf, 1)
                dve.reg_add(n, n, 1)
                dve.reg_load(key, ctl[0:1, 0:1])

            for j in range(NQ):
                dve.wait_ge(pe_oT, j + 1)
                v.tensor_tensor(cen[:, 4 * j:4 * j + 4, :, :].rearrange("p t b c -> p (t b c)"), bank(2 + j),
                                t2[:, 4 * j:4 * j + 4, :, :].rearrange("p t b c -> p (t b c)"), ALU.add).then_inc(dve_o, 1)


_INS = ["x", "L0_conv_w_qkv", "L0_conv_b_qkv", "L0_conv_rpb", "L0_conv_w_proj", "L0_conv_b_proj",
        "L1_attn_ln_weight", "L1_attn_ln_bias", "L1_ffn_ffn_w1", "L1_ffn_ffn_b1", "L1_ffn_ffn_w2", "L1_ffn_ffn_b2",
        "L1_ffn_wq", "L1_ffn_wk", "L1_ffn_wv", "L1_ffn_wo", "L1_ffn_attn_mask", "L1_ffn_ffn_mask"]


def kernel(**inputs):
    import numpy as _np
    import concourse.bacc as _bacc
    from concourse import mybir as _mybir
    from concourse.bass_utils import run_bass_kernel_spmd as _run

    nc = _bacc.Bacc("TRN2", target_bir_lowering=False, num_devices=1)
    arrays, args = {}, []
    for name in _INS + ["const"]:
        a = constants() if name == "const" else _np.ascontiguousarray(inputs[name])
        arrays[f"in_{name}_dram"] = a
        args.append(nc.dram_tensor(f"in_{name}_dram", a.shape, _mybir.dt.from_np(a.dtype), kind="ExternalInput").ap())
    args.append(nc.dram_tensor("out_dram", (B, IMG, IMG, C), F32, kind="ExternalOutput").ap())
    build(nc, *args)
    r = _run(nc, [arrays], core_ids=[0])
    return r.results[0]["out_dram"]
```

```python
import concourse.bass as bass
from concourse import mybir
from concourse.alu_op_type import AluOpType as ALU
from contextlib import ExitStack

F32 = mybir.dt.float32
F32R = mybir.dt.float32r
I32 = mybir.dt.int32
U32 = mybir.dt.uint32
U8 = mybir.dt.uint8
ACT = mybir.ActivationFunctionType
AX = mybir.AxisListType

B, IMG, C = 2, 32, 64
N = IMG * IMG
NT = N // 128
NH, KW = 4, 7
HD = C // NH
RW = 2 * KW - 1
WIN = KW * IMG
OUTSIDE = 1.0e30
NB, NOPS = 33, 19
HID = 256
DEAD = 1000.0

FIRST, REST = {}, {}
for _cols, _names in ((FIRST, (("pairavg", 128), ("qmask", B * NH), ("wqkv", 3 * B * C), ("qkb", 2))),
                      (REST, (("vmask", B * C), ("eye32", IMG), ("outside", IMG), ("wpr", B * C), ("vb", 1), ("pb", C),
                              ("ident", 128), ("fold", C), ("lnw", C), ("lnb", C), ("ones", 128), ("step4", NB)))):
    _at = 0
    for _name, _w in _names:
        _cols[_name] = (_at, _at + _w)
        _at += _w
    _cols["all"] = (0, _at)

REC = {"w1": (0, HID), "w2": (HID, HID + 2 * C), "b1": (HID + 2 * C, HID + 2 * C + 2), "b2": (HID + 2 * C + 2, HID + 2 * C + 3)}
NREC = HID + 2 * C + 3
PAD = IMG


def laid_out(i):
    import numpy as np
    p = np.arange(128)
    first = np.zeros((128, FIRST["all"][1]), np.float32)
    rest = np.zeros((128, REST["all"][1]), np.float32)

    def put(name, v):
        to, cols = (first, FIRST) if name in FIRST else (rest, REST)
        lo, hi = cols[name]
        to[:v.shape[0], lo:hi] = v.reshape(v.shape[0], hi - lo)

    def diagonal(w):
        w = w.reshape(C, -1, C)
        out = np.zeros((B, C, w.shape[1], B, C), np.float32)
        for b in range(B):
            out[b, :, :, b, :] = w
        return out.reshape(B * C, -1)

    put("ident", np.eye(128))
    put("pairavg", 0.5 * (p[:, None] // 2 == p[None, :] // 2))
    own = (p[:, None] // C == np.arange(B * NH)[None] // NH) & (p[:, None] % C // HD == np.arange(B * NH)[None] % NH)
    put("qmask", -(HD ** -0.5) * own)
    put("vmask", 1.0 * (p[:, None] // IMG == np.arange(B * C)[None] % C // HD))
    put("eye32", 1.0 * (p[:, None] % IMG == np.arange(IMG)[None]))
    qw, kw = p[:, None] % IMG, np.arange(IMG)[None]
    lo = np.clip(qw - KW // 2, 0, IMG - KW)
    put("outside", OUTSIDE * ((kw < lo) | (kw >= lo + KW)))
    put("fold", 1.0 * (p[:, None] % C == np.arange(C)[None]))
    put("ones", np.ones((128, 128)))
    put("step4", 4.0 * np.arange(NB)[None])
    put("wqkv", diagonal(i["L0_conv_w_qkv"]))
    put("wpr", diagonal(i["L0_conv_w_proj"]))
    put("qkb", np.tile(i["L0_conv_b_qkv"][:2 * C].reshape(2, C).T, (B, 1)))
    put("vb", i["L0_conv_b_qkv"][2 * C:].reshape(C, 1))
    for name, key in (("pb", "L0_conv_b_proj"), ("lnw", "L1_attn_ln_weight"), ("lnb", "L1_attn_ln_bias")):
        put(name, np.broadcast_to(i[key][None], (128, C)))
    rec = np.empty((NB * NOPS, 128, NREC), np.float32)
    for b in range(B):
        rec[:, C * b:C * b + C, slice(*REC["w1"])] = i["L1_ffn_ffn_w1"].reshape(NB * NOPS, C, HID)
        rec[:, C * b:C * b + C, slice(*REC["b2"])] = i["L1_ffn_ffn_b2"].reshape(NB * NOPS, C, 1)
    rec[:, :, slice(*REC["w2"])] = i["L1_ffn_ffn_w2"].reshape(NB * NOPS, 2, 128, C).transpose(0, 2, 1, 3).reshape(NB * NOPS, 128, 2 * C)
    rec[:, :, slice(*REC["b1"])] = i["L1_ffn_ffn_b1"].reshape(NB * NOPS, 2, 128).transpose(0, 2, 1)
    x = i["x"].reshape(B, NT, 128, C)
    return {
        "x_tok": np.ascontiguousarray(x.transpose(2, 1, 0, 3)),
        "x_chan": np.ascontiguousarray(i["x"].reshape(B, N, C).transpose(0, 2, 1).reshape(B * C, N)),
        "first": first, "rest": rest, "rec": rec,
        "rpb": np.pad(i["L0_conv_rpb"].reshape(NH, RW * RW)[:, ::-1], ((0, 0), (PAD, PAD))),
        "masks": np.stack([i["L1_ffn_attn_mask"].reshape(-1), i["L1_ffn_ffn_mask"].reshape(-1)])[None],
        "wq": i["L1_ffn_wq"], "wk": i["L1_ffn_wk"], "wv": i["L1_ffn_wv"], "wo": i["L1_ffn_wo"],
    }


def first_row(r):
    return min(max(r - KW // 2, 0), IMG - KW)


ROWS = 8
GROUPS = IMG // ROWS
LANES = ROWS * IMG


def slot(r, kr):
    return kr - r + (KW // 2 if r // ROWS < GROUPS - 1 else KW - 1)


SLOTS = max(slot(r, first_row(r) + KW - 1) for r in range(IMG)) + 1


def key_rows(g):
    for kr in range(IMG):
        qs = [q for q in range(ROWS * g, ROWS * g + ROWS) if first_row(q) <= kr < first_row(q) + KW]
        if qs:
            yield kr, qs[0], len(qs)


def build(nc, x_tok, x_chan, first, rest, rec, rpb, masks, wq, wk, wv, wo, out):
    ctx = ExitStack()
    with ctx:
        def sb(name, shape, dt=F32):
            return ctx.enter_context(nc.sbuf_tensor(name, shape, dt))

        def sem(name):
            return ctx.enter_context(nc.semaphore(name))

        sfirst = sb("sfirst", [128, FIRST["all"][1]])
        srest = sb("srest", [128, REST["all"][1]])

        def kc(name, rows=128):
            t, cols = (sfirst, FIRST) if name in FIRST else (srest, REST)
            lo, hi = cols[name]
            return t[0:rows, lo:hi]

        ident = kc("ident")
        wqkv = kc("wqkv").rearrange("p (k m) -> p k m", k=3)
        wpr = kc("wpr")
        qkb = kc("qkb")
        xtok = sb("xtok", [128, NT, B, C])
        brow = sb("brow", [128, C])
        bias = sb("bias", [128, RW, IMG])
        gstat = sb("gstat", [128, 2, 6])
        gmv = sb("gmv", [128, 2])
        gtmp = sb("gtmp", [128, 6])
        qbm = sb("qbm", [128, B * NH])
        gnT = sb("gnT", [128, N])
        kT = sb("kT", [128, N])
        big = sb("big", [128, NT * N])
        qbd = big[:, :].rearrange("p (r b h w) -> p r b h w", r=IMG, b=B, h=NH)
        vbd = sb("vbd", [128, IMG, B, C])
        sneg = sb("sneg", [128, 4, WIN])
        nmax = sb("nmax", [128, IMG * B])
        psumr = sb("psumr", [128, IMG * B])
        prinv = sb("prinv", [128, IMG, B])
        prob = sb("prob", [128, 3, 4 * WIN])
        probT = sb("probT", [128, 2, ROWS, B, SLOTS * IMG])
        dinv = sb("dinv", [128, 2, B, ROWS, IMG])
        rbs = sb("rbs", [128, 2, LANES])
        att = sb("att", [128, N])
        t1 = sb("t1", [128, NT, B, C])
        cen = sb("cen", [128, NT, B, C])
        lst = sb("lst", [128, 8, NT * B])
        minus_half = sb("minus_half", [128, 1])
        bst = sb("bst", [128, NT * B, 6])
        mv = sb("mv", [128, 3, NT * B, 2])
        rs = sb("rs", [128, 4, NT * B])
        xh = sb("xh", [128, B, N], F32R)
        xl = sb("xl", [128, B, N], F32R)
        xa = sb("xa", [128, B, N], F32R)
        sim1 = sb("sim1", [128, NT * N])
        rsum = sb("rsum", [128, B * NT])
        rinv = sb("rinv", [128, B * NT])
        csum = sb("csum", [128, B * NT])
        cinv = sb("cinv", [128, B * NT])
        xc = sb("xc", [128, NT, C])
        stage = sb("stage", [128, NREC])
        w1z = sb("w1z", [128, B, HID])
        live = sb("live", [128, NREC - HID])
        w2l = live[:, 0:2 * C].rearrange("p (k d) -> p k d", k=2)
        b1l = live[:, 2 * C:2 * C + 2]
        b2l = live[:, 2 * C + 2:2 * C + 3]
        aw = sb("aw", [128, 4, B, C])
        m8 = sb("m8", [1, 2, NB * NOPS], U8)
        mx8 = sb("mx8", [1, 8])
        ix8 = sb("ix8", [1, 8], U32)
        keyf = sb("keyf", [1, 1])
        kcand = sb("kcand", [1, 2, NB])
        ctl = sb("ctl", [1, 1], I32)

        sims = [big, sim1]
        spare = probT[:, :, :, :, :].rearrange("p g r b w -> p (g r b w)")
        rr = spare[:, 0:3 * N].rearrange("p (i n) -> p i n", i=3)
        ff = spare[:, 3 * N:5 * N].rearrange("p (i n) -> p i n", i=2)
        us = spare[:, 5 * N:6 * N]
        dia = vbd[:, 0:NT, :, :].rearrange("p t b c -> p t (b c)")
        tokens = dict(t=NT, b=B, c=C)
        a = gnT[:, :].rearrange("p (t b c) -> p t b c", **tokens)
        xn = kT[:, :].rearrange("p (t b c) -> p t b c", **tokens)
        flatp = prob[:, :, :].rearrange("p i w -> p (i w)")
        t2 = flatp[:, 0:N].rearrange("p (t b c) -> p t b c", **tokens)
        mf = flatp[0:1, N:N + 2 * NB * NOPS].rearrange("u (i n) -> u i n", i=2)
        xchan = flatp[:, 0:N]
        rawbias = sim1[:, 0:RW * IMG].rearrange("p (d k) -> p d k", d=RW)
        code = dinv[0:1, :, :, :, :].rearrange("u g b r w -> u (g b r w)")[:, 0:NOPS * NB]
        sq = vbd[:, NT:2 * NT, :, :]
        H = att[:, :]
        xn2 = sim1[:, 0:2 * NT * B * C].rearrange("p (t b w) -> p t b w", t=NT, b=B)
        z = big[:, 0:8 * 512].rearrange("p (j b m n) -> p j b m n", j=2, b=B, m=2)
        aq, ak, av, ao, ap_, apt = (sim1[:, i * N:(i + 1) * N] for i in range(6))
        am_stat = lst[:, 0, 0:4]

        PS = ctx.enter_context(nc.psum_tensor("PS", [128, 8 * 512], F32))

        def bank(i, n=1):
            return PS[:, 512 * i:512 * (i + n)]

        d_x, d_first, d_rest, d_xtok, d_rpb = sem("d_x"), sem("d_first"), sem("d_rest"), sem("d_xtok"), sem("d_rpb")
        d_mask, d_w, d_aw, d_out = sem("d_mask"), sem("d_w"), sem("d_aw"), sem("d_out")
        zeroed, held = sem("zeroed"), sem("held")
        pe_vb, pe_avg, pe_q, pe_k = sem("pe_vb"), sem("pe_avg"), sem("pe_q"), sem("pe_k")
        pe_s, pe_v, pe_rb, pe_pv, pe_pr = sem("pe_s"), sem("pe_v"), sem("pe_rb"), sem("pe_pv"), sem("pe_pr")
        pe_nT, pe_sim, pe_rB, pe_u, pe_y = sem("pe_nT"), sem("pe_sim"), sem("pe_rB"), sem("pe_u"), sem("pe_y")
        pe_hT, pe_row, pe_z, pe_h, pe_oT = sem("pe_hT"), sem("pe_row"), sem("pe_z"), sem("pe_h"), sem("pe_oT")
        pe_aqkv, pe_asc, pe_atr, pe_ao, pe_ay = sem("pe_aqkv"), sem("pe_asc"), sem("pe_atr"), sem("pe_ao"), sem("pe_ay")
        chain, dve_zero, dve_rs = sem("chain"), sem("dve_zero"), sem("dve_rs")
        dve_brow, dve_avg, dve_var, dve_gn, dve_tab, dve_qb = (sem("dve_brow"), sem("dve_avg"), sem("dve_var"),
                                                              sem("dve_gn"), sem("dve_tab"), sem("dve_qb"))
        dve_q, dve_s, dve_v, dve_t, dve_ri, dve_att, dve_t1 = (sem("dve_q"), sem("dve_s"), sem("dve_v"), sem("dve_t"),
                                                               sem("dve_ri"), sem("dve_att"), sem("dve_t1"))
        dve_c, dve_ve, dve_xn, dve_xa, dve_dia, dve_r, dve_xc, dve_y, dve_h0 = (
            sem("dve_c"), sem("dve_ve"), sem("dve_xn"), sem("dve_xa"), sem("dve_dia"), sem("dve_r"), sem("dve_xc"),
            sem("dve_y"), sem("dve_h0"))
        h_ready, decided, w_live, dve_z, dve_o = sem("h_ready"), sem("decided"), sem("w_live"), sem("dve_z"), sem("dve_o")
        dve_aqkv, dve_amx, dve_apn, dve_apt, dve_ao = (sem("dve_aqkv"), sem("dve_amx"), sem("dve_apn"), sem("dve_apt"),
                                                       sem("dve_ao"))
        act_sd, act_q, act_k, act_p, act_rb = sem("act_sd"), sem("act_q"), sem("act_k"), sem("act_p"), sem("act_rb")
        act_sq, act_sqrt, act_xh, act_e, act_f, act_us = (sem("act_sq"), sem("act_sqrt"), sem("act_xh"), sem("act_e"),
                                                          sem("act_f"), sem("act_us"))
        act_z, act_ap = sem("act_z"), sem("act_ap")
        pool_xb, pool_d, pool_xn = sem("pool_xb"), sem("pool_d"), sem("pool_xn")
        pool_links, act_v = sem("pool_links"), sem("act_v")

        aw_v = [w.rearrange("s o c d -> (s o) c d") for w in (wq, wk, wv, wo)]
        NQ = 2
        HALF = N // NQ

        def pending(eng, reg):
            k = eng.snap(reg, min_val=0, max_val=4 * NB - 1)
            return k

        def hold(eng, s, value):
            eng.wait_ge(s, value)
            eng.sem_inc(held, 1)

        block = ctx.enter_context(nc.Block())

        @block.sync
        def _(sp):
            sp.dma_start(xchan[:, :], x_chan).then_inc(d_x, 16)
            sp.dma_start(sfirst[:, :], first).then_inc(d_first, 16)
            for h in range(NH):
                src = bass.AP(rpb.tensor, rpb.offset + h * (RW * RW + 2 * PAD) + PAD + (KW - 1) - (IMG - 1),
                              [[1, IMG], [RW, RW], [1, IMG]])
                sp.dma_start(rawbias[IMG * h:IMG * h + IMG, :, :], src).then_inc(d_rpb, 16)
            sp.dma_start(srest[:, :], rest).then_inc(d_rest, 16)
            sp.dma_start(xtok[:, :, :, :], x_tok).then_inc(d_xtok, 16)
            sp.dma_start(m8[:, :, :], masks).then_inc(d_mask, 16)

            n = sp.alloc_register("sp_n")
            nf = sp.alloc_register("sp_nf")
            na = sp.alloc_register("sp_na")
            for r in (n, nf, na):
                sp.reg_mov(r, 0)
            key = sp.alloc_register("sp_key")
            sp.wait_ge(decided, 1)
            sp.reg_load(key, ctl[0:1, 0:1])
            with sp.While(lambda: sp.snap(key) < 4 * NB):
                k = pending(sp, key)
                op = sp.value_load(ix8[0:1, 0:1], min_val=0, max_val=NOPS - 1)
                row = sp.snap((k // 4) * NOPS + op, min_val=0, max_val=NB * NOPS - 1)
                with sp.If(k % 2 == 1):
                    sp.wait_ge(pe_ay, sp.snap(na) * NQ + 1)
                    for i in range(4):
                        for b in range(B):
                            sp.dma_start(aw[C * b:C * b + C, i, b, :],
                                         aw_v[i][bass.ds(row, 1), :, :].rearrange("u c d -> (u c) d")).then_inc(d_aw, 16)
                    sp.reg_add(na, na, 1)
                with sp.If((k // 2) % 2 == 1):
                    sp.wait_ge(w_live, sp.snap(nf) + 1)
                    sp.dma_start(stage[:, :], rec[bass.ds(row, 1), :, :].rearrange("u p w -> (u p) w")).then_inc(d_w, 16)
                    sp.reg_add(nf, nf, 1)
                sp.reg_add(n, n, 1)
                hold(sp, decided, sp.snap(n) + 1)
                sp.reg_load(key, ctl[0:1, 0:1])

            for j in range(NQ):
                sp.wait_ge(dve_o, j + 1)
                sp.dma_start(out[:, 4 * j:4 * j + 4, :, :], cen[:, 4 * j:4 * j + 4, :, :]).then_inc(d_out, 16)
            sp.wait_ge(d_out, 16 * NQ)

        @block.gpsimd
        def _(pool):
            made = [0]

            def then(ins):
                made[0] += 1
                ins.then_inc(pool_links, 1)
                pool.wait_ge(pool_links, made[0])

            nc.gpsimd.memset(qbd[C:2 * C, :, 0, :, :], 0.0).then_inc(zeroed, 1)
            pool.wait_ge(zeroed, 1)
            nc.gpsimd.memset(vbd[:, :, :, :], 0.0).then_inc(zeroed, 1)
            pool.wait_ge(zeroed, 2)
            nc.gpsimd.memset(w1z[:, :, :], 0.0)
            nc.gpsimd.memset(aw[:, :, :, :], 0.0)
            nc.gpsimd.memset(keyf[:, :], -1.0)
            nc.gpsimd.memset(minus_half[:, :], -0.5)
            pool.drain()
            pool.sem_inc(zeroed, 1)
            pool.wait_ge(d_xtok, 16)
            pool.wait_ge(dve_brow, 1)
            nc.gpsimd.tensor_tensor(xtok[:, :, :, :].rearrange("p t b c -> p (t b) c"),
                                    xtok[:, :, :, :].rearrange("p t b c -> p (t b) c"),
                                    brow[:, :].unsqueeze(1).broadcast_to([128, NT * B, C]), ALU.add).then_inc(pool_xb, 1)

            def diagonals(g):
                pool.wait_ge(dve_ri, g + 1)
                if g >= 2:
                    pool.wait_ge(pe_rb, g - 1)
                for b in range(B):
                    ins = nc.gpsimd.tensor_tensor(
                        dinv[:, g % 2, b, :, :],
                        kc("eye32").unsqueeze(1).broadcast_to([128, ROWS, IMG]),
                        prinv[:, ROWS * g:ROWS * g + ROWS, b].unsqueeze(2).broadcast_to([128, ROWS, IMG]), ALU.mult)
                ins.then_inc(pool_d, 1)

            def norm1(g):
                cols = slice(4 * g, 4 * g + 4)
                pool.wait_ge(dve_rs, g + 1)
                then(nc.gpsimd.tensor_tensor(rs[:, 2:4, cols], rs[:, 0:2, cols],
                                             minus_half[:, 0:1].unsqueeze(2).broadcast_to([128, 2, 4]), ALU.pow))
                wide = [128, 4, C]
                flat = "p t b c -> p (t b) c"
                then(nc.gpsimd.tensor_tensor(cen[:, 2 * g:2 * g + 2, :, :].rearrange(flat), t1[:, 2 * g:2 * g + 2, :, :].rearrange(flat),
                                             mv[:, 0, cols, 0].unsqueeze(2).broadcast_to(wide), ALU.subtract))
                nc.gpsimd.tensor_tensor(a[:, 2 * g:2 * g + 2, :, :].rearrange(flat), cen[:, 2 * g:2 * g + 2, :, :].rearrange(flat),
                                        rs[:, 2, cols].unsqueeze(2).broadcast_to(wide), ALU.mult)
                twice = [128, 4, 2, C]
                nc.gpsimd.tensor_tensor(xn2[:, 2 * g:2 * g + 2, :, :].rearrange("p t b (k c) -> p (t b) k c", k=2),
                                        cen[:, 2 * g:2 * g + 2, :, :].rearrange(flat).unsqueeze(2).broadcast_to(twice),
                                        rs[:, 3, cols].unsqueeze(2).unsqueeze(3).broadcast_to(twice), ALU.mult)
                pool.drain()
                pool.sem_inc(pool_xn, 1)

            diagonals(0)
            diagonals(1)
            norm1(0)
            diagonals(2)
            norm1(1)
            diagonals(3)
            norm1(2)
            norm1(3)

        @block.tensor
        def _(pe):
            pe.sem_inc(pe_ay, 1)
            pe.wait_ge(d_first, 16)
            pe.wait_ge(dve_avg, 1)
            nc.tensor.matmul(bank(2)[:, 0:1], kc("pairavg"), gmv[:, 0:1], start=True, stop=True).then_inc(pe_avg, 1)
            pe.wait_ge(dve_avg, 2)
            nc.tensor.matmul(bank(2)[:, 1:2], kc("pairavg"), gtmp[:, 1:2], start=True, stop=True).then_inc(pe_avg, 1)
            for j in range(NQ):
                pe.wait_ge(dve_gn, j + 1)
                cols = gnT[:, HALF * j:HALF * j + HALF]
                nc.tensor.matmul(bank(4 + j), wqkv[:, 0, :], cols,
                                 start=True, stop=True).then_inc(pe_q, 1)
                nc.tensor.matmul(bank(6 + j), wqkv[:, 1, :], cols,
                                 start=True, stop=True).then_inc(pe_k, 1)

            def values(r):
                for h in range(NH):
                    ins = nc.tensor.matmul(bank(0, 2)[IMG * h:IMG * h + IMG, IMG * r:IMG * r + IMG],
                                           gnT[:, IMG * r:IMG * r + IMG],
                                           wqkv[:, 2, :].rearrange("p (b c) -> p b c", b=B)[:, :, HD * h:HD * h + HD],
                                           start=True, stop=True)
                if r % 16 == 15:
                    ins.then_inc(pe_v, 1)

            RING = (2, 3, 7)

            def scores(r):
                if r >= len(RING):
                    pe.wait_ge(dve_s, B * (r - len(RING) + 1))
                elif r == 2:
                    pe.wait_ge(act_k, 2)
                for b in range(B):
                    ins = nc.tensor.matmul(bank(RING[r % 3])[:, 256 * b:256 * b + WIN],
                                           qbd[:, r, b, :, :].rearrange("p h w -> p (h w)"),
                                           kT[:, IMG * first_row(r):IMG * first_row(r) + WIN],
                                           start=True, stop=True)
                ins.then_inc(pe_s, 1)

            def norms(g):
                pe.wait_ge(pool_d, g + 1)
                if g >= 1:
                    pe.wait_ge(dve_t1, g)
                    pe.wait_ge(act_rb, g)
                for b in range(B):
                    ins = nc.tensor.matmul(bank(6)[C * b:C * b + C, 0:LANES], kc("vmask")[:, 0:C],
                                           dinv[:, g % 2, b, :, :].rearrange("p r w -> p (r w)"), start=True, stop=True)
                ins.then_inc(pe_rb, 1)

            def weighted(g):
                pieces = list(key_rows(g))
                flat = probT[:, g % 2, :, :, :].rearrange("p r b w -> p (r b w)")
                for n, (kr, q, nq) in enumerate(pieces):
                    q0 = q - ROWS * g
                    for b in range(B):
                        base = (q0 * B + b) * SLOTS * IMG + slot(q, kr) * IMG
                        rhs = bass.AP(flat.tensor, flat.offset + base, [flat.ap[0], [(B * SLOTS - 1) * IMG, nq], [1, IMG]])
                        ins = nc.tensor.matmul(bank(4 + g % 2)[C * b:C * b + C, IMG * q0:IMG * (q0 + nq)],
                                               vbd[:, kr, b, :], rhs, start=n == 0, stop=n == len(pieces) - 1,
                                               skip_group_check=True)
                    if n == len(pieces) - 1:
                        ins.then_inc(pe_pv, 1)
                    yield

            def project(g):
                pe.wait_ge(dve_att, g + 1)
                pe.wait_ge(act_rb, g + 1)
                for t in (2 * g, 2 * g + 1):
                    ins = nc.tensor.matmul(bank(6)[:, LANES + 128 * (t % 2):LANES + 128 * (t % 2) + 128],
                                           att[:, 128 * t:128 * t + 128], wpr, start=True, stop=True)
                ins.then_inc(pe_pr, 1)

            def normal_tokens(j):
                pe.wait_ge(pool_xn, 2 * j + 2)
                for b in range(B):
                    for t in range(4 * j, 4 * j + 4):
                        to = bank(b) if j == 0 else bank(7 - b)
                        ins = nc.tensor.transpose(to[:, 128 * (t % 4):128 * (t % 4) + 128], xn2[:, t, b, :], ident)
                    ins.then_inc(pe_nT, 1)

            pe.wait_ge(d_rest, 16)
            nc.tensor.matmul(bank(3)[:, 0:C], kc("vb", C).broadcast_to([C, 128]), wpr[0:C, 0:C],
                             start=True, stop=True).then_inc(pe_vb, 1)
            for r in range(IMG // 2):
                values(r)
            pe.wait_ge(zeroed, 2)
            pe.wait_ge(dve_zero, 1)
            pe.wait_ge(dve_gn, NQ)
            pe.wait_ge(dve_brow, 1)
            work = iter(())
            for r in range(IMG):
                if r % (IMG // 2) == 0:
                    pe.wait_ge(act_q, r // (IMG // 2) + 1)
                    pe.wait_ge(dve_q, r // (IMG // 2) + 1)
                    if r == 0:
                        pe.wait_ge(act_k, 1)
                if first_row(r) + KW > IMG // 2 and (r == 0 or first_row(r - 1) + KW <= IMG // 2):
                    pe.wait_ge(act_k, 2)
                scores(r)
                g, rg = r // ROWS, r % ROWS
                if r in range(4, 12):
                    for rv in (2 * r + 8, 2 * r + 9):
                        values(rv)
                if rg == 3 and g >= 1:
                    for _ in work:
                        pass
                    pe.wait_ge(dve_t, 4 * g)
                    pe.wait_ge(act_v, min(g, 2))
                    if g == 1:
                        pe.wait_ge(act_q, 2)
                        pe.wait_ge(dve_q, 2)
                        pe.wait_ge(act_k, 2)
                    work = weighted(g - 1)
                for _ in range(3 if g == GROUPS - 1 else 2):
                    next(work, None)
                if rg == 4 and g >= 2:
                    project(g - 2)
                if rg == 7 and g >= 1:
                    norms(g - 1)
            for _ in work:
                pass
            project(GROUPS - 2)
            pe.wait_ge(dve_t, 4 * GROUPS)
            for _ in weighted(GROUPS - 1):
                pass
            norms(GROUPS - 1)
            normal_tokens(0)
            project(GROUPS - 1)

            pe.wait_ge(dve_t1, GROUPS)
            normal_tokens(1)

            def similarities(b, m):
                i = NT * b + m
                if m == 0:
                    pe.wait_ge(dve_xa, B + b + 1)
                if i >= 2:
                    pe.wait_ge(act_e, i - 1)
                for part, lhs in enumerate((xh, xl)):
                    for j in range(NQ):
                        ins = nc.tensor.matmul(bank(2 + 2 * (i % 2) + j), lhs[:, b, 128 * m:128 * m + 128],
                                               xa[:, b, HALF * j:HALF * j + HALF], start=part == 0, stop=part == 1)
                ins.then_inc(pe_sim, 1)

            def row_norms(b):
                pe.wait_ge(dve_dia, b + 1)
                for j in range(NQ):
                    ins = nc.tensor.matmul(bank(j), kc("ones"), dia[:, 4 * j:4 * j + 4, :].rearrange("p t n -> p (t n)"),
                                           start=True, stop=True)
                ins.then_inc(pe_rB, 1)

            def gathered(b, m):
                i = NT * b + m
                pe.wait_ge(dve_r, i + 1)
                if m == 0 and b == 1:
                    pe.wait_ge(act_us, 1)
                if m == 0 and b == 0:
                    pe.wait_ge(dve_xa, 2 * B)
                pe.wait_ge(act_f, i + 1)
                pe.wait_ge(dve_xc, i + 1)
                for j in range(NQ):
                    cols = slice(HALF * j, HALF * j + HALF)
                    nc.tensor.matmul(bank(6 + j)[0:C, :], a[:, m, b, :], rr[:, i % 3, cols], start=m == 0, stop=m == NT - 1)
                    ins = nc.tensor.matmul(bank(6 + j)[C:2 * C, :], xc[:, m, :], ff[:, i % 2, cols],
                                           start=m == 0, stop=m == NT - 1)
                ins.then_inc(pe_u, 1)

            def to_tokens(b):
                pe.wait_ge(act_us, b + 1)
                for t in range(NT):
                    ins = nc.tensor.matmul(bank(0)[:, C * t:C * t + C], us[:, 128 * t:128 * t + 128], kc("fold"),
                                           start=True, stop=True)
                ins.then_inc(pe_y, 1)

            for m in range(NT):
                similarities(0, m)
            similarities(1, 0)
            similarities(1, 1)
            row_norms(0)
            for m in range(2, 6):
                similarities(1, m)
            for m in range(NT):
                gathered(0, m)
            similarities(1, 6)
            similarities(1, 7)
            to_tokens(0)
            pe.wait_ge(dve_y, 1)
            row_norms(1)
            for m in range(NT):
                gathered(1, m)
            to_tokens(1)

            for j in range(NQ):
                pe.wait_ge(dve_y, 2)
                pe.wait_ge(dve_h0, 2)
                for t in range(4 * j, 4 * j + 4):
                    ins = nc.tensor.transpose(bank(6 + j)[:, 128 * (t % 4):128 * (t % 4) + 128],
                                              xn[:, t, :, :].rearrange("p b c -> p (b c)"), ident)
                ins.then_inc(pe_hT, 1)

            def decide_row(count):
                pe.wait_ge(h_ready, count)
                nc.tensor.transpose(bank(1)[0:1, 0:C], H[0:C, 0:1], ident[0:C, 0:C]).then_inc(pe_row, 1)

            decide_row(1)
            n, nf, na, hv = (pe.alloc_register(f"pe_{s}") for s in ("n", "nf", "na", "hv"))
            for r in (n, nf, na):
                pe.reg_mov(r, 0)
            pe.reg_mov(hv, NQ)
            key = pe.alloc_register("pe_key")
            pe.wait_ge(decided, 1)
            pe.reg_load(key, ctl[0:1, 0:1])
            with pe.While(lambda: pe.snap(key) < 4 * NB):
                k = pending(pe, key)
                with pe.If(k % 2 == 1):
                    done = pe.snap(na)
                    hold(pe, d_aw, done * (16 * 4 * B) + 16 * 4 * B)
                    pe.wait_ge(h_ready, pe.snap(hv))
                    for i in range(2):
                        for j in range(NQ):
                            nc.tensor.matmul(bank(2 * i + j), aw[:, i, :, :].rearrange("p b c -> p (b c)"),
                                             H[:, HALF * j:HALF * j + HALF], start=True, stop=True)
                    for t in range(NT):
                        ins = nc.tensor.matmul(bank(4, 2)[:, 128 * t:128 * t + 128], H[:, 128 * t:128 * t + 128],
                                               aw[:, 2, :, :].rearrange("p b c -> p (b c)"), start=True, stop=True)
                    ins.then_inc(pe_aqkv, 1)
                    pe.wait_ge(dve_aqkv, done + 1)
                    for u in range(B * NT):
                        b, t = u // NT, u % NT
                        if u:
                            pe.wait_ge(act_ap, done * (B * NT) + u)
                        for j in range(NQ):
                            ins = nc.tensor.matmul(bank(j), aq[C * b:C * b + C, 128 * t:128 * t + 128],
                                                   ak[C * b:C * b + C, HALF * j:HALF * j + HALF], start=True, stop=True)
                        ins.then_inc(pe_asc, 1)
                        pe.wait_ge(dve_apn, done * (B * NT) + u + 1)
                        for kt in range(NT):
                            ins = nc.tensor.transpose(bank(2, 2)[:, 128 * kt:128 * kt + 128],
                                                      ap_[:, 128 * kt:128 * kt + 128], ident)
                        ins.then_inc(pe_atr, 1)
                        pe.wait_ge(dve_apt, done * (B * NT) + u + 1)
                        for kt in range(NT):
                            ins = nc.tensor.matmul(bank(4, 2)[C * b:C * b + C, 128 * t:128 * t + 128],
                                                   av[:, 128 * kt + C * b:128 * kt + C * b + C],
                                                   apt[:, 128 * kt:128 * kt + 128], start=kt == 0, stop=kt == NT - 1)
                        ins.then_inc(pe_ao, 1)
                    pe.wait_ge(dve_ao, done + 1)
                    for j in range(NQ):
                        nc.tensor.matmul(bank(6 + j), aw[:, 3, :, :].rearrange("p b c -> p (b c)"),
                                         ao[:, HALF * j:HALF * j + HALF], start=True, stop=True).then_inc(pe_ay, 1)
                    pe.reg_add(na, na, 1)
                    pe.reg_add(hv, hv, NQ)
                with pe.If((k // 2) % 2 == 0):
                    hold(pe, h_ready, pe.snap(hv))
                    decide_row(1)
                with pe.If((k // 2) % 2 == 1):
                    done = pe.snap(nf)
                    have = pe.snap(hv)
                    pe.wait_ge(w_live, done + 2)
                    for j in range(NQ):
                        pe.wait_ge(h_ready, have + (j - 1))
                        for b in range(B):
                            for mc in range(2):
                                nc.tensor.matmul(bank(4 * j + 2 * b + mc), w1z[:, b, 128 * mc:128 * mc + 128],
                                                 H[:, HALF * j:HALF * j + HALF], start=True, stop=True).then_inc(pe_z, 1)
                        if j == 1:
                            hold(pe, h_ready, have + 1)
                            decide_row(1)
                        pe.wait_ge(act_z, done * 4 + 2 * j + 2)
                        pe.wait_ge(dve_z, done * 4 + 2 * j + 2)
                        for kc_ in range(2):
                            for b in range(B):
                                ins = nc.tensor.matmul(bank(4 * j)[C * b:C * b + C, :], w2l[:, kc_, :], z[:, j, b, kc_, :],
                                                       start=kc_ == 0, stop=kc_ == 1)
                        ins.then_inc(pe_h, 1)
                    pe.reg_add(nf, nf, 1)
                    pe.reg_add(hv, hv, NQ)
                pe.reg_add(n, n, 1)
                hold(pe, decided, pe.snap(n) + 1)
                pe.reg_load(key, ctl[0:1, 0:1])

            have = pe.snap(hv)
            for j in range(NQ):
                pe.wait_ge(h_ready, have + (j - 1))
                for t in range(4 * j, 4 * j + 4):
                    ins = nc.tensor.transpose(bank(2 + j)[:, 128 * (t % 4):128 * (t % 4) + 128],
                                              H[:, 128 * t:128 * t + 128], ident)
                ins.then_inc(pe_oT, 1)

        @block.scalar
        def _(act):
            act.wait_ge(d_first, 16)
            nc.scalar.activation(gtmp[:, 5:6], kc("pairavg")[:, 0:1], ACT.Sqrt)
            act.wait_ge(dve_var, 1)
            nc.scalar.activation(gtmp[:, 3:4], gtmp[:, 2:3], ACT.Sqrt).then_inc(act_sd, 1)
            act.wait_ge(dve_qb, 1)

            def queries(j, h):
                rows = slice(IMG // 2 * j, IMG // 2 * (j + 1))
                ins = nc.scalar.activation(qbd[0:C, rows, 0, h, :], bank(4 + j)[0:C, :].rearrange("p (r w) -> p r w", w=IMG),
                                           ACT.Identity, scale=kc("qmask", C)[:, h:h + 1], bias=qbm[0:C, h:h + 1])
                if h == NH - 1:
                    ins.then_inc(act_q, 1)

            def values(c, h):
                if h == 0:
                    act.wait_ge(pe_v, c + 1)
                if (c, h) == (0, 0):
                    act.wait_ge(zeroed, 2)
                part = slice(IMG * h, IMG * h + IMG)
                ins = nc.scalar.activation(vbd[part, 16 * c:16 * c + 16, :, HD * h:HD * h + HD],
                                           bank(c)[part, :].rearrange("p (r b d) -> p r b d", b=B, d=HD), ACT.Copy)
                if h == NH - 1:
                    ins.then_inc(act_v, 1)

            def divisors(g):
                act.wait_ge(pe_rb, g + 1)
                if g >= 2:
                    act.wait_ge(dve_att, g - 1)
                nc.scalar.activation(rbs[:, g % 2, :], bank(6)[:, 0:LANES], ACT.Copy).then_inc(act_rb, 1)

            def high(n):
                act.wait_ge(pe_nT, n + 1)
                j, b = n // B, n % B
                nc.scalar.activation(xh[:, b, HALF * j:HALF * j + HALF], bank(b) if j == 0 else bank(7 - b),
                                     ACT.Copy).then_inc(act_xh, 1)

            act.wait_ge(pe_q, 1)
            for h in range(NH):
                queries(0, h)
            for j in range(NQ):
                act.wait_ge(pe_k, j + 1)
                nc.scalar.activation(kT[:, HALF * j:HALF * j + HALF], bank(6 + j), ACT.Identity,
                                     bias=qkb[:, 1:2]).then_inc(act_k, 1)
            for i in range(B * IMG):
                if i < 8 and i % 2 == 0:
                    if i == 0:
                        act.wait_ge(pe_q, 2)
                    queries(1, i // 2)
                act.wait_ge(dve_s, i + 1)
                if i >= 12:
                    act.wait_ge(dve_t, i // 4 - 2)
                nc.scalar.activation(prob[:, i // 4 % 3, WIN * (i % 4):WIN * (i % 4) + WIN], sneg[:, i % 4, :], ACT.Exp,
                                     scale=-1.0, bias=nmax[:, i:i + 1], accum_out=psumr[:, i:i + 1]).then_inc(act_p, 1)
                if i in range(8, 16) and i % 2:
                    values(0, (i - 8) // 2)
                if i in range(26, 34) and i % 2:
                    values(1, (i - 26) // 2)
                if i % 16 == 13 and i > 16:
                    divisors(i // 16 - 1)
            for b in range(B):
                high(b)
            divisors(GROUPS - 1)
            for b in range(B):
                high(B + b)

            def norm_parts(n, lo, hi, both):
                act.wait_ge(dve_c, n)
                nc.scalar.activation(sq[:, :, lo:hi, :], cen[:, :, lo:hi, :], ACT.Square).then_inc(act_sq, 1)
                act.wait_ge(dve_ve, n)
                cols = lst[:, :, :].rearrange("p k (t b) -> p k t b", b=B)[:, :, :, lo:hi]
                if both:
                    nc.scalar.activation(cols[:, 4], cols[:, 1], ACT.Sqrt)
                nc.scalar.activation(cols[:, 3], cols[:, 2], ACT.Sqrt).then_inc(act_sqrt, 1)

            def expsim(b, m):
                i = NT * b + m
                act.wait_ge(pe_sim, i + 1)
                nc.scalar.activation(sims[b][:, N * m:N * m + N], bank(2 + 2 * (i % 2), 2), ACT.Exp, scale=2.0,
                                     accum_out=rsum[:, i:i + 1]).then_inc(act_e, 1)

            def expcol(b, m):
                i = NT * b + m
                act.wait_ge(dve_r, i + 1)
                if i >= 2:
                    act.wait_ge(pe_u, i - 1)
                nc.scalar.activation(ff[:, i % 2, :], rr[:, i % 3, :], ACT.Exp, accum_out=csum[:, i:i + 1]).then_inc(act_f, 1)

            def take_sums(b):
                act.wait_ge(pe_u, NT * (b + 1))
                if b:
                    act.wait_ge(pe_y, b)
                nc.scalar.activation(us[:, :], bank(6, 2), ACT.Copy).then_inc(act_us, 1)

            for m in range(NT):
                expsim(0, m)
            for m in range(4):
                expsim(1, m)
            for m in range(NT):
                expcol(0, m)
            for m in range(4, NT):
                expsim(1, m)
            take_sums(0)
            norm_parts(1, 0, 1, False)
            norm_parts(2, 0, 1, False)
            for m in range(NT):
                expcol(1, m)
            take_sums(1)
            norm_parts(3, 1, 2, False)
            norm_parts(4, 1, 2, False)

            n, nf, na = (act.alloc_register(f"act_{s}") for s in ("n", "nf", "na"))
            for r in (n, nf, na):
                act.reg_mov(r, 0)
            key = act.alloc_register("act_key")
            act.wait_ge(decided, 1)
            act.reg_load(key, ctl[0:1, 0:1])
            with act.While(lambda: act.snap(key) < 4 * NB):
                k = pending(act, key)
                with act.If(k % 2 == 1):
                    done = act.snap(na)
                    for u in range(B * NT):
                        act.wait_ge(dve_amx, done * (B * NT) + u + 1)
                        nc.scalar.activation(ap_, bank(0, 2), ACT.Exp, scale=C ** -0.5, bias=am_stat[:, 1:2],
                                             accum_out=am_stat[:, 2:3]).then_inc(act_ap, 1)
                    act.reg_add(na, na, 1)
                with act.If((k // 2) % 2 == 1):
                    done = act.snap(nf)
                    act.wait_ge(w_live, done + 2)
                    for j in range(NQ):
                        for mc in range(2):
                            act.wait_ge(pe_z, done * 8 + 4 * j + mc + 1)
                            nc.scalar.activation(z[:, j, 0, mc, :], bank(4 * j + mc), ACT.Relu,
                                                 bias=b1l[:, mc:mc + 1]).then_inc(act_z, 1)
                    act.reg_add(nf, nf, 1)
                act.reg_add(n, n, 1)
                hold(act, decided, act.snap(n) + 1)
                act.reg_load(key, ctl[0:1, 0:1])

        @block.vector
        def _(dve):
            links = [0]

            def link(ins):
                links[0] += 1
                ins.then_inc(chain, 1)
                dve.wait_ge(chain, links[0])

            v = nc.vector
            dve.sem_inc(w_live, 1)
            nc.vector.memset(qbd[0:C, :, 1, :, :], 0.0).then_inc(dve_zero, 1)
            dve.wait_ge(d_x, 16)
            for j in range(NQ):
                ins = v.bn_stats(gstat[:, j, :], xchan[:, HALF * j:HALF * j + HALF])
            link(ins)
            v.bn_aggr(gmv[:, :], gstat[:, :, :].rearrange("p j s -> p (j s)")).then_inc(dve_avg, 1)
            dve.wait_ge(pe_avg, 1)
            link(v.tensor_tensor(gtmp[:, 0:1], gmv[:, 0:1], bank(2)[:, 0:1], ALU.subtract))
            link(v.tensor_tensor(gtmp[:, 1:2], gtmp[:, 0:1], gtmp[:, 0:1], ALU.mult))
            dve.wait_ge(dve_avg, 1)
            v.tensor_tensor(gtmp[:, 1:2], gtmp[:, 1:2], gmv[:, 1:2], ALU.add).then_inc(dve_avg, 1)
            dve.wait_ge(d_first, 16)
            v.tensor_scalar(qbm[:, :], kc("qmask"), qkb[:, 0:1], None, ALU.mult).then_inc(dve_qb, 1)
            dve.wait_ge(pe_avg, 2)
            v.tensor_scalar(gtmp[:, 2:3], bank(2)[:, 1:2], 1e-5, None, ALU.add).then_inc(dve_var, 1)
            dve.wait_ge(act_sd, 1)
            link(v.reciprocal(gtmp[:, 4:5], gtmp[:, 3:4]))
            for j in range(NQ):
                v.tensor_scalar(gnT[:, HALF * j:HALF * j + HALF], xchan[:, HALF * j:HALF * j + HALF], bank(2)[:, 0:1],
                                gtmp[:, 4:5], ALU.subtract, ALU.mult).then_inc(dve_gn, 1)
            dve.wait_ge(d_rpb, 16 * NH)
            backwards = bass.AP(rawbias.tensor, rawbias.offset + RW * IMG - 1, [rawbias.ap[0], [-IMG, RW], [-1, IMG]])
            dve.wait_ge(d_rest, 16)
            link(v.scalar_tensor_tensor(bias[:, :, :], backwards, -1.0,
                                        kc("outside").unsqueeze(1).broadcast_to([128, RW, IMG]), ALU.mult, ALU.add))

            def queries(j, h):
                rows = slice(IMG // 2 * j, IMG // 2 * (j + 1))
                if h == 0:
                    dve.wait_ge(pe_q, j + 1)
                ins = v.tensor_scalar(qbd[C:2 * C, rows, 1, h, :],
                                      bank(4 + j)[C:2 * C, :].rearrange("p (r w) -> p r w", w=IMG),
                                      qkb[C:2 * C, 0:1], kc("qmask")[C:2 * C, NH + h:NH + h + 1], ALU.add, ALU.mult)
                if h == NH - 1:
                    ins.then_inc(dve_q, 1)

            dve.wait_ge(zeroed, 1)
            for h in range(NH):
                queries(0, h)
            dve.wait_ge(pe_vb, 1)
            v.tensor_tensor(brow[:, :], kc("pb"), bank(3)[:, 0:C], ALU.add).then_inc(dve_brow, 1)

            def shifted_scores(i):
                r = i // B
                d = first_row(r) - r + KW - 1
                dve.wait_ge(pe_s, r + 1)
                if i >= 4:
                    dve.wait_ge(act_p, i - 3)
                v.tensor_tensor_reduce(out=sneg[:, i % 4, :],
                                       in0=bank((2, 3, 7)[r % 3])[:, 256 * (i % B):256 * (i % B) + WIN],
                                       in1=bias[:, d:d + KW, :].rearrange("p d k -> p (d k)"), scale=1.0, scalar=3.0e38,
                                       op0=ALU.add, op1=ALU.min, accum_out=nmax[:, i:i + 1]).then_inc(dve_s, 1)

            def flip(c):
                g = c // 4
                dve.wait_ge(act_p, 4 * c + 4)
                if g >= 2:
                    dve.wait_ge(pe_pv, g - 1)
                r = 2 * c
                if slot(r, first_row(r)) == slot(r + 1, first_row(r + 1)):
                    spans = [(r, 2)]
                else:
                    spans = [(r, 1), (r + 1, 1)]
                for q, nq in spans:
                    lo = IMG * slot(q, first_row(q))
                    ins = v.transpose(probT[:, g % 2, q % ROWS:q % ROWS + nq, :, lo:lo + WIN].rearrange("p r b w -> p (r b) w"),
                                      prob[:, c % 3, B * WIN * (q - r):B * WIN * (q - r + nq)].rearrange("p (k w) -> p k w", w=WIN))
                ins.then_inc(dve_t, 1)
                if c % 4 == 3:
                    v.reciprocal(prinv[:, ROWS * g:ROWS * g + ROWS, :].rearrange("p r b -> p (r b)"),
                                 psumr[:, 16 * g:16 * g + 16]).then_inc(dve_ri, 1)

            def normalise(g):
                dve.wait_ge(pe_pv, g + 1)
                dve.wait_ge(act_rb, g + 1)
                v.tensor_tensor(att[:, LANES * g:LANES * g + LANES], bank(4 + g % 2)[:, 0:LANES], rbs[:, g % 2, :],
                                ALU.mult).then_inc(dve_att, 1)

            def residual(g):
                dve.wait_ge(pe_pr, g + 1)
                dve.wait_ge(pool_xb, 1)
                v.tensor_tensor(t1[:, 2 * g:2 * g + 2, :, :].rearrange("p t b c -> p (t b c)"),
                                bank(6)[:, LANES:LANES + 2 * 128],
                                xtok[:, 2 * g:2 * g + 2, :, :].rearrange("p t b c -> p (t b c)"), ALU.add).then_inc(dve_t1, 1)

            def token_stats(k, src, cols, eps):
                for t, b in cols:
                    ins = v.bn_stats(bst[:, B * t + b, :], src[:, t, b, :])
                link(ins)
                for t, b in cols:
                    ins = v.bn_aggr(mv[:, k, B * t + b, :], bst[:, B * t + b, :])
                link(ins)

            def norm1_stats(g):
                dve.wait_ge(dve_t1, g + 1)
                token_stats(0, t1, [(t, b) for t in (2 * g, 2 * g + 1) for b in range(B)], 1e-5)
                cols = slice(4 * g, 4 * g + 4)
                link(v.tensor_scalar(rs[:, 0, cols], mv[:, 0, cols, 1], 1e-5, None, ALU.add))
                link(v.tensor_scalar(rs[:, 1, cols], rs[:, 0, cols], 1e-24, None, ALU.mult))
                v.scalar_tensor_tensor(rs[:, 1, cols], mv[:, 0, cols, 1], float(C), rs[:, 1, cols], ALU.mult, ALU.max)
                dve.drain()
                dve.sem_inc(dve_rs, 1)

            def low(n):
                j, b = n // B, n % B
                dve.wait_ge(act_xh, n + 1)
                src, cols = bank(b) if j == 0 else bank(7 - b), slice(HALF * j, HALF * j + HALF)
                link(v.tensor_tensor(xl[:, b, cols], src, xh[:, b, cols].bitcast(F32), ALU.subtract))
                v.tensor_copy(xa[0:C, b, cols], xh[0:C, b, cols].bitcast(F32))
                v.tensor_copy(xa[C:2 * C, b, cols], xl[C:2 * C, b, cols].bitcast(F32)).then_inc(dve_xa, 1)

            for i in range(B * IMG):
                shifted_scores(i)
                if i < 8 and i % 2:
                    queries(1, i // 2)
                if i % 4 == 3 and i >= 7:
                    flip(i // 4 - 1)
                g = i // 16 - 2
                if g >= 0:
                    if i % 16 == 3:
                        normalise(g)
                    if i % 16 == 9:
                        residual(g)
                    if i % 16 == 13:
                        norm1_stats(g)
            flip(15)
            normalise(GROUPS - 2)
            residual(GROUPS - 2)
            norm1_stats(GROUPS - 2)
            for b in range(B):
                low(b)
            normalise(GROUPS - 1)
            residual(GROUPS - 1)
            norm1_stats(GROUPS - 1)
            for b in range(B):
                low(B + b)

            def stats(src, lo, hi, n, eps):
                w = hi - lo
                cols = lst[:, :, :].rearrange("p k (t b) -> p k t b", b=B)[:, :, :, lo:hi]
                wide = [128, NT, w, C]
                link(v.tensor_reduce(cols[:, 0], src[:, :, lo:hi, :], AX.X, ALU.add))
                link(v.tensor_scalar(cols[:, 0], cols[:, 0], 1.0 / C, None, ALU.mult))
                v.tensor_tensor(cen[:, :, lo:hi, :], src[:, :, lo:hi, :], cols[:, 0].unsqueeze(3).broadcast_to(wide),
                                ALU.subtract).then_inc(dve_c, 1)
                dve.wait_ge(act_sq, n)
                link(v.tensor_reduce(cols[:, 1], sq[:, :, lo:hi, :], AX.X, ALU.add))
                v.tensor_scalar(cols[:, 2], cols[:, 1], 1.0 / C, eps, ALU.mult, ALU.add).then_inc(dve_ve, 1)
                dve.wait_ge(act_sqrt, n)
                link(v.reciprocal(cols[:, 5], cols[:, 3]))
                return cols, wide

            for b in range(B):
                dve.wait_ge(act_e, NT * (b + 1))
                if b:
                    dve.wait_ge(pe_rB, b)
                link(v.reciprocal(rinv[:, NT * b:NT * b + NT], rsum[:, NT * b:NT * b + NT]))
                v.tensor_tensor(dia[:, :, :], ident.unsqueeze(1).broadcast_to([128, NT, 128]),
                                rinv[:, NT * b:NT * b + NT].unsqueeze(2).broadcast_to([128, NT, 128]),
                                ALU.mult).then_inc(dve_dia, 1)
                dve.wait_ge(pe_rB, b + 1)

                def columns(m):
                    i = NT * b + m
                    dve.wait_ge(act_f, i + 1)
                    if b and m == 0:
                        dve.wait_ge(pe_u, NT)
                    link(v.reciprocal(cinv[:, i:i + 1], csum[:, i:i + 1]))
                    v.tensor_scalar(xc[:, m, :], a[:, m, b, :], cinv[:, i:i + 1], None, ALU.mult).then_inc(dve_xc, 1)

                for m in range(NT):
                    i = NT * b + m
                    if i >= 3:
                        dve.wait_ge(pe_u, i - 2)
                    v.tensor_tensor(rr[:, i % 3, :], sims[b][:, N * m:N * m + N], bank(0, 2), ALU.mult).then_inc(dve_r, 1)
                    if m:
                        columns(m - 1)
                columns(NT - 1)
                dve.wait_ge(pe_y, b + 1)
                dve.wait_ge(pool_xn, GROUPS)
                y = sq
                link(v.scalar_tensor_tensor(y[:, :, b, :], bank(0).rearrange("p (t c) -> p t c", c=C), -0.1, a[:, :, b, :],
                                            ALU.mult, ALU.add))
                cols, wide = stats(y, b, b + 1, 2 * b + 1, 1e-6)
                wide = [128, NT, C]
                link(v.tensor_tensor(y[:, :, b, :], cen[:, :, b, :], cols[:, 5].broadcast_to(wide), ALU.mult))
                link(v.tensor_tensor(y[:, :, b, :], y[:, :, b, :], kc("lnw").unsqueeze(1).broadcast_to(wide), ALU.mult))
                link(v.tensor_tensor(y[:, :, b, :], y[:, :, b, :], kc("lnb").unsqueeze(1).broadcast_to(wide), ALU.add))
                link(v.tensor_tensor(t2[:, :, b, :], y[:, :, b, :], t1[:, :, b, :], ALU.add))
                dve.nop().then_inc(dve_y, 1)
                cols, _ = stats(t2, b, b + 1, 2 * b + 2, 1e-5)
                v.tensor_tensor(xn[:, :, b, :], cen[:, :, b, :], cols[:, 5].broadcast_to(wide), ALU.mult).then_inc(dve_h0, 1)

            dve.wait_ge(d_mask, 16)
            dve.wait_ge(zeroed, 3)
            link(v.tensor_copy(mf[:, :, :], m8[:, :, :]))
            link(v.scalar_tensor_tensor(mf[0:1, 0, :], mf[0:1, 1, :], 2.0, mf[0:1, 0, :], ALU.mult, ALU.add))
            link(v.tensor_scalar(mf[0:1, 1, :], mf[0:1, 0, :], 0.0, DEAD, ALU.is_equal, ALU.mult))
            link(v.tensor_tensor(mf[0:1, 0, :], mf[0:1, 0, :], mf[0:1, 1, :], ALU.add))
            link(v.tensor_tensor(code[:, :].rearrange("u (o s) -> u s o", s=NB), mf[0:1, 0, :].rearrange("u (s o) -> u s o", o=NOPS),
                                 kc("step4", 1).unsqueeze(2).broadcast_to([1, NB, NOPS]), ALU.add))
            for j in range(NQ):
                dve.wait_ge(pe_hT, j + 1)
                v.tensor_copy(H[:, HALF * j:HALF * j + HALF], bank(6 + j)).then_inc(h_ready, 1)

            def decide():
                dve.drain()
                v.max(mx8[:, :], bank(1)[0:1, 0:NOPS])
                v.tensor_scalar(kcand[0:1, 0, :], kc("step4", 1), keyf[0:1, 0:1], DEAD, ALU.is_le, ALU.mult)
                dve.drain()
                v.max_index(ix8[:, :], mx8[:, :], bank(1)[0:1, 0:NOPS])
                dve.drain()
                op = dve.value_load(ix8[0:1, 0:1], min_val=0, max_val=NOPS - 1)
                v.tensor_tensor(kcand[0:1, 1, :], kcand[0:1, 0, :], code[0:1, bass.ds(op * NB, NB)], ALU.add)
                dve.drain()
                v.tensor_reduce(keyf[:, :], kcand[0:1, 1, :], AX.X, ALU.min)
                dve.drain()
                v.tensor_copy(ctl[:, :], keyf[:, :]).then_inc(decided, 1)
                dve.drain()

            dve.wait_ge(pe_row, 1)
            decide()
            n, nf, na = (dve.alloc_register(f"dve_{s}") for s in ("n", "nf", "na"))
            for r in (n, nf, na):
                dve.reg_mov(r, 0)
            key = dve.alloc_register("dve_key")
            dve.reg_load(key, ctl[0:1, 0:1])
            with dve.While(lambda: dve.snap(key) < 4 * NB):
                k = pending(dve, key)
                with dve.If(k % 2 == 1):
                    done = dve.snap(na)
                    dve.wait_ge(pe_aqkv, done + 1)
                    v.tensor_copy(aq, bank(0, 2))
                    v.tensor_copy(ak, bank(2, 2))
                    v.tensor_copy(av, bank(4, 2)).then_inc(dve_aqkv, 1)
                    for u in range(B * NT):
                        dve.wait_ge(pe_asc, done * (B * NT) + u + 1)
                        v.tensor_reduce(am_stat[:, 0:1], bank(0, 2), AX.X, ALU.max, negate=True)
                        dve.drain()
                        v.tensor_scalar(am_stat[:, 1:2], am_stat[:, 0:1], C ** -0.5, None, ALU.mult).then_inc(dve_amx, 1)
                        dve.wait_ge(act_ap, done * (B * NT) + u + 1)
                        v.reciprocal(am_stat[:, 3:4], am_stat[:, 2:3])
                        dve.drain()
                        v.tensor_scalar(ap_, ap_, am_stat[:, 3:4], None, ALU.mult).then_inc(dve_apn, 1)
                        dve.wait_ge(pe_atr, done * (B * NT) + u + 1)
                        v.tensor_copy(apt, bank(2, 2)).then_inc(dve_apt, 1)
                    dve.wait_ge(pe_ao, done * (B * NT) + B * NT)
                    v.tensor_copy(ao, bank(4, 2)).then_inc(dve_ao, 1)
                    for j in range(NQ):
                        dve.wait_ge(pe_ay, done * NQ + j + 2)
                        v.tensor_copy(H[:, HALF * j:HALF * j + HALF], bank(6 + j)).then_inc(h_ready, 1)
                    dve.reg_add(na, na, 1)
                with dve.If((k // 2) % 2 == 0):
                    hold(dve, pe_row, dve.snap(n) + 2)
                    decide()
                with dve.If((k // 2) % 2 == 1):
                    done = dve.snap(nf)
                    hold(dve, d_w, done * 16 + 16)
                    dve.drain()
                    for b in range(B):
                        v.tensor_copy(w1z[C * b:C * b + C, b, :], stage[C * b:C * b + C, 0:HID])
                    v.tensor_copy(live[:, :], stage[:, HID:]).then_inc(w_live, 1)
                    dve.drain()
                    for j in range(NQ):
                        for mc in range(2):
                            dve.wait_ge(pe_z, done * 8 + 4 * j + 2 + mc + 1)
                            v.tensor_scalar(z[:, j, 1, mc, :], bank(4 * j + 2 + mc), b1l[:, mc:mc + 1], 0.0,
                                            ALU.add, ALU.max).then_inc(dve_z, 1)
                        if j == 1:
                            hold(dve, pe_row, dve.snap(n) + 2)
                            decide()
                        dve.wait_ge(pe_h, done * NQ + j + 1)
                        v.tensor_scalar(H[:, HALF * j:HALF * j + HALF], bank(4 * j), b2l[:, 0:1], None,
                                        ALU.add).then_inc(h_ready, 1)
                    dve.reg_add(nf, nf, 1)
                dve.reg_add(n, n, 1)
                dve.reg_load(key, ctl[0:1, 0:1])

            for j in range(NQ):
                dve.wait_ge(pe_oT, j + 1)
                v.tensor_tensor(cen[:, 4 * j:4 * j + 4, :, :].rearrange("p t b c -> p (t b c)"), bank(2 + j),
                                t2[:, 4 * j:4 * j + 4, :, :].rearrange("p t b c -> p (t b c)"), ALU.add).then_inc(dve_o, 1)




def kernel(**inputs):
    import numpy as _np
    import concourse.bacc as _bacc
    from concourse import mybir as _mybir
    from concourse.bass_utils import run_bass_kernel_spmd as _run

    nc = _bacc.Bacc("TRN2", target_bir_lowering=False, num_devices=1)
    arrays, args = {}, []
    for name, v in laid_out({k: _np.asarray(v) for k, v in inputs.items()}).items():
        v = _np.ascontiguousarray(v)
        arrays[f"in_{name}_dram"] = v
        args.append(nc.dram_tensor(f"in_{name}_dram", v.shape, _mybir.dt.from_np(v.dtype), kind="ExternalInput").ap())
    args.append(nc.dram_tensor("out_dram", (128, NT, B, C), F32, kind="ExternalOutput").ap())
    build(nc, *args)
    r = _run(nc, [arrays], core_ids=[0])
    return _np.ascontiguousarray(r.results[0]["out_dram"].transpose(2, 1, 0, 3)).reshape(B, IMG, IMG, C)
```

```python
import concourse.bass as bass
from concourse import mybir
from concourse.alu_op_type import AluOpType as ALU
from contextlib import ExitStack

F32 = mybir.dt.float32
F32R = mybir.dt.float32r
I32 = mybir.dt.int32
U32 = mybir.dt.uint32
U8 = mybir.dt.uint8
ACT = mybir.ActivationFunctionType
AX = mybir.AxisListType

B, IMG, C = 2, 32, 64
N = IMG * IMG
NT = N // 128
NH, KW = 4, 7
HD = C // NH
RW = 2 * KW - 1
WIN = KW * IMG
OUTSIDE = 1.0e30
NB, NOPS = 33, 19
HID = 256
DEAD = 1000.0

FIRST, REST = {}, {}
for _cols, _names in ((FIRST, (("pairavg", 128), ("qmask", B * NH), ("wqkv", 3 * B * C), ("qkb", 2))),
                      (REST, (("vmask", B * C), ("eye32", IMG), ("outside", IMG), ("wpr", B * C), ("vb", 1), ("pb", C),
                              ("ident", 128), ("fold", C), ("lnw", C), ("lnb", C), ("step4", NB)))):
    _at = 0
    for _name, _w in _names:
        _cols[_name] = (_at, _at + _w)
        _at += _w
    _cols["all"] = (0, _at)

REC = {"w1": (0, HID), "w2": (HID, HID + 2 * C), "b1": (HID + 2 * C, HID + 2 * C + 2), "b2": (HID + 2 * C + 2, HID + 2 * C + 3)}
NREC = HID + 2 * C + 3
PAD = IMG


def laid_out(i):
    import numpy as np
    p = np.arange(128)
    first = np.zeros((128, FIRST["all"][1]), np.float32)
    rest = np.zeros((128, REST["all"][1]), np.float32)

    def put(name, v):
        to, cols = (first, FIRST) if name in FIRST else (rest, REST)
        lo, hi = cols[name]
        to[:v.shape[0], lo:hi] = v.reshape(v.shape[0], hi - lo)

    def diagonal(w):
        w = w.reshape(C, -1, C)
        out = np.zeros((B, C, w.shape[1], B, C), np.float32)
        for b in range(B):
            out[b, :, :, b, :] = w
        return out.reshape(B * C, -1)

    put("ident", np.eye(128))
    put("pairavg", 0.5 * (p[:, None] // 2 == p[None, :] // 2))
    own = (p[:, None] // C == np.arange(B * NH)[None] // NH) & (p[:, None] % C // HD == np.arange(B * NH)[None] % NH)
    put("qmask", -(HD ** -0.5) * own)
    put("vmask", 1.0 * (p[:, None] // IMG == np.arange(B * C)[None] % C // HD))
    put("eye32", 1.0 * (p[:, None] % IMG == np.arange(IMG)[None]))
    qw, kw = p[:, None] % IMG, np.arange(IMG)[None]
    lo = np.clip(qw - KW // 2, 0, IMG - KW)
    put("outside", OUTSIDE * ((kw < lo) | (kw >= lo + KW)))
    put("fold", 1.0 * (p[:, None] % C == np.arange(C)[None]))
    put("step4", 4.0 * np.arange(NB)[None])
    put("wqkv", diagonal(i["L0_conv_w_qkv"]))
    put("wpr", diagonal(i["L0_conv_w_proj"]))
    put("qkb", np.tile(i["L0_conv_b_qkv"][:2 * C].reshape(2, C).T, (B, 1)))
    put("vb", i["L0_conv_b_qkv"][2 * C:].reshape(C, 1))
    for name, key in (("pb", "L0_conv_b_proj"), ("lnw", "L1_attn_ln_weight"), ("lnb", "L1_attn_ln_bias")):
        put(name, np.broadcast_to(i[key][None], (128, C)))
    rec = np.empty((NB * NOPS, 128, NREC), np.float32)
    for b in range(B):
        rec[:, C * b:C * b + C, slice(*REC["w1"])] = i["L1_ffn_ffn_w1"].reshape(NB * NOPS, C, HID)
        rec[:, C * b:C * b + C, slice(*REC["b2"])] = i["L1_ffn_ffn_b2"].reshape(NB * NOPS, C, 1)
    rec[:, :, slice(*REC["w2"])] = i["L1_ffn_ffn_w2"].reshape(NB * NOPS, 2, 128, C).transpose(0, 2, 1, 3).reshape(NB * NOPS, 128, 2 * C)
    rec[:, :, slice(*REC["b1"])] = i["L1_ffn_ffn_b1"].reshape(NB * NOPS, 2, 128).transpose(0, 2, 1)
    x = i["x"].reshape(B, NT, 128, C)
    return {
        "x_tok": np.ascontiguousarray(x.transpose(2, 1, 0, 3)),
        "x_chan": np.ascontiguousarray(i["x"].reshape(B, N, C).transpose(0, 2, 1).reshape(B * C, N)),
        "first": first, "rest": rest, "rec": rec,
        "rpb": np.pad(i["L0_conv_rpb"].reshape(NH, RW * RW)[:, ::-1], ((0, 0), (PAD, PAD))),
        "masks": np.stack([i["L1_ffn_attn_mask"].reshape(-1), i["L1_ffn_ffn_mask"].reshape(-1)])[None],
        "wq": i["L1_ffn_wq"], "wk": i["L1_ffn_wk"], "wv": i["L1_ffn_wv"], "wo": i["L1_ffn_wo"],
    }


def first_row(r):
    return min(max(r - KW // 2, 0), IMG - KW)


ROWS = 8
GROUPS = IMG // ROWS
LANES = ROWS * IMG


def slot(r, kr):
    return kr - r + (KW // 2 if r // ROWS < GROUPS - 1 else KW - 1)


SLOTS = max(slot(r, first_row(r) + KW - 1) for r in range(IMG)) + 1


def key_rows(g, part):
    for kr in range(IMG):
        qs = [q for q in range(ROWS * g + part.start, ROWS * g + part.stop) if first_row(q) <= kr < first_row(q) + KW]
        if qs:
            yield kr, qs[0], len(qs)


def build(nc, x_tok, x_chan, first, rest, rec, rpb, masks, wq, wk, wv, wo, out):
    ctx = ExitStack()
    with ctx:
        def sb(name, shape, dt=F32):
            return ctx.enter_context(nc.sbuf_tensor(name, shape, dt))

        def sem(name):
            return ctx.enter_context(nc.semaphore(name))

        sfirst = sb("sfirst", [128, FIRST["all"][1]])
        srest = sb("srest", [128, REST["all"][1]])

        def kc(name, rows=128):
            t, cols = (sfirst, FIRST) if name in FIRST else (srest, REST)
            lo, hi = cols[name]
            return t[0:rows, lo:hi]

        ident = kc("ident")
        wqkv = kc("wqkv").rearrange("p (k m) -> p k m", k=3)
        wpr = kc("wpr")
        qkb = kc("qkb")
        xtok = sb("xtok", [128, NT, B, C])
        brow = sb("brow", [128, C])
        bias = sb("bias", [128, RW, IMG])
        gstat = sb("gstat", [128, 2, 6])
        gmv = sb("gmv", [128, 2])
        gtmp = sb("gtmp", [128, 5])
        warm = sb("warm", [128, 6])
        qbm = sb("qbm", [128, B * NH])
        gnT = sb("gnT", [128, N])
        kT = sb("kT", [128, N])
        big = sb("big", [128, NT * N])
        qbd = big[:, :].rearrange("p (r b h w) -> p r b h w", r=IMG, b=B, h=NH)
        vbd = sb("vbd", [128, IMG, B, C])
        sneg = sb("sneg", [128, 4, WIN])
        nmax = sb("nmax", [128, IMG * B])
        psumr = sb("psumr", [128, IMG * B])
        prinv = sb("prinv", [128, IMG, B])
        prob = sb("prob", [128, 3, 4 * WIN])
        probT = sb("probT", [128, 2, ROWS, B, SLOTS * IMG])
        dinv = sb("dinv", [128, 2, B, ROWS, IMG])
        rbs = sb("rbs", [128, 2, LANES])
        att = sb("att", [128, N])
        t1 = sb("t1", [128, NT, B, C])
        cen = sb("cen", [128, NT, B, C])
        minus_half = sb("minus_half", [128, 1])
        bst = sb("bst", [128, NT * B, 6])
        mv = sb("mv", [128, NT * B, 2])
        sd = sb("sd", [128, 2, NT * B])
        rstd = sb("rstd", [128, NT * B])
        rs = sb("rs", [128, 4, NT * B])
        xh = sb("xh", [128, B, N], F32R)
        xl = sb("xl", [128, B, N], F32R)
        xa = sb("xa", [128, B, N], F32R)
        sim1 = sb("sim1", [128, NT * N])
        rsum = sb("rsum", [128, B * NT])
        rinv = sb("rinv", [128, B * NT])
        csum = sb("csum", [128, B * NT])
        cinv = sb("cinv", [128, B * NT])
        stage = sb("stage", [128, NREC])
        w1z = sb("w1z", [128, B, HID])
        live = sb("live", [128, NREC - HID])
        w2l = live[:, 0:2 * C].rearrange("p (k d) -> p k d", k=2)
        b1l = live[:, 2 * C:2 * C + 2]
        b2l = live[:, 2 * C + 2:2 * C + 3]
        aw = sb("aw", [128, 4, B, C])
        m8 = sb("m8", [1, 2, NB * NOPS], U8)
        z0 = sb("z0", [128, 2])
        mx8 = sb("mx8", [1, 8])
        ix8 = sb("ix8", [1, 8], U32)
        keyf = sb("keyf", [1, 1])
        kcand = sb("kcand", [1, 2, NB])
        ctl = sb("ctl", [1, 1], I32)

        sims = [big, sim1]
        spare = probT[:, :, :, :, :].rearrange("p g r b w -> p (g r b w)")
        rr = spare[:, 0:4 * N].rearrange("p (i n) -> p i n", i=4)
        ff = spare[:, 4 * N:8 * N].rearrange("p (i n) -> p i n", i=4)
        us = spare[:, 8 * N:10 * N].rearrange("p (b n) -> p b n", b=B)
        tokens = dict(t=NT, b=B, c=C)
        a = gnT[:, :].rearrange("p (t b c) -> p t b c", **tokens)
        xn = kT[:, :].rearrange("p (t b c) -> p t b c", **tokens)
        flatp = prob[:, :, :].rearrange("p i w -> p (i w)")
        t2 = flatp[:, 0:N].rearrange("p (t b c) -> p t b c", **tokens)
        mf = flatp[0:1, N:N + 2 * NB * NOPS].rearrange("u (i n) -> u i n", i=2)
        xchan = flatp[:, 0:N]
        rawbias = sim1[:, 0:RW * IMG].rearrange("p (d k) -> p d k", d=RW)
        code = dinv[0:1, :, :, :, :].rearrange("u g b r w -> u (g b r w)")[:, 0:NOPS * NB]
        t1b = cen[:, :, :, :]
        y = vbd[:, NT:2 * NT, :, :]
        xc = vbd[:, 2 * NT:3 * NT, :, :].rearrange("p t b c -> p b t c")
        H = att[:, :]
        xn2 = sim1[:, 0:2 * NT * B * C].rearrange("p (t b w) -> p t b w", t=NT, b=B)
        z = big[:, 0:8 * 512].rearrange("p (j b m n) -> p j b m n", j=2, b=B, m=2)
        aq, ak, av, ao, ap_, apt = (sim1[:, i * N:(i + 1) * N] for i in range(6))
        am_stat = prinv[:, 0:2, :].rearrange("p r b -> p (r b)")

        PS = ctx.enter_context(nc.psum_tensor("PS", [128, 8 * 512], F32))

        def bank(i, n=1):
            return PS[:, 512 * i:512 * (i + n)]

        token0, row0 = bank(5)[:, 0:2], bank(5)[0:1, C:2 * C]

        d_x = [sem("d_x0"), sem("d_x1")]
        d_first, d_rest, d_xtok, d_rpb = sem("d_first"), sem("d_rest"), sem("d_xtok"), sem("d_rpb")
        d_mask, d_w, d_aw, d_out = sem("d_mask"), sem("d_w"), sem("d_aw"), sem("d_out")
        zeroed, held = sem("zeroed"), sem("held")
        pe_vb, pe_avg, pe_q, pe_k = sem("pe_vb"), sem("pe_avg"), sem("pe_q"), sem("pe_k")
        pe_s, pe_v, pe_rb, pe_pv, pe_pr = sem("pe_s"), sem("pe_v"), sem("pe_rb"), sem("pe_pv"), sem("pe_pr")
        pe_nT, pe_sim, pe_rB, pe_u, pe_y = sem("pe_nT"), sem("pe_sim"), sem("pe_rB"), sem("pe_u"), sem("pe_y")
        pe_hT, pe_row, pe_z, pe_h, pe_oT = sem("pe_hT"), sem("pe_row"), sem("pe_z"), sem("pe_h"), sem("pe_oT")
        pe_aqkv, pe_asc, pe_atr, pe_ao, pe_ay = sem("pe_aqkv"), sem("pe_asc"), sem("pe_atr"), sem("pe_ao"), sem("pe_ay")
        chain, dve_zero, dve_rs = sem("chain"), sem("dve_zero"), sem("dve_rs")
        dve_brow, dve_avg, dve_var, dve_gn, dve_qb = (sem("dve_brow"), sem("dve_avg"), sem("dve_var"),
                                                              sem("dve_gn"), sem("dve_qb"))
        dve_q, dve_s, dve_t, dve_ri, dve_att, dve_t1 = (sem("dve_q"), sem("dve_s"), sem("dve_t"),
                                                               sem("dve_ri"), sem("dve_att"), sem("dve_t1"))
        dve_ve0, dve_ve1, dve_xn, dve_xa, dve_rinv, dve_r, dve_xc, dve_y, dve_h0 = (
            sem("dve_ve0"), sem("dve_ve1"), sem("dve_xn"), sem("dve_xa"), sem("dve_rinv"), sem("dve_r"), sem("dve_xc"),
            sem("dve_y"), sem("dve_h0"))
        h_ready, decided, w_live, rest_live = sem("h_ready"), sem("decided"), sem("w_live"), sem("rest_live")
        dve_z, dve_o = sem("dve_z"), sem("dve_o")
        dve_aqkv, dve_amx, dve_apn, dve_apt, dve_ao = (sem("dve_aqkv"), sem("dve_amx"), sem("dve_apn"), sem("dve_apt"),
                                                       sem("dve_ao"))
        act_sd, act_q, act_k, act_p, act_rb = sem("act_sd"), sem("act_q"), sem("act_k"), sem("act_p"), sem("act_rb")
        act_sqrt, act_xh, act_xa, act_e, act_f, act_us = (sem("act_sqrt"), sem("act_xh"), sem("act_xa"), sem("act_e"),
                                                          sem("act_f"), sem("act_us"))
        act_z, act_ap, act_root = sem("act_z"), sem("act_ap"), sem("act_root")
        pe_z0, act_z0 = sem("pe_z0"), sem("act_z0")
        act_h, act_v, dve_d = sem("act_h"), sem("act_v"), sem("dve_d")
        pool_xb, pool_d, pool_xn, pool_a = sem("pool_xb"), sem("pool_d"), sem("pool_xn"), sem("pool_a")
        pool_t1b, pool_t2, pool_h0, pool_links = sem("pool_t1b"), sem("pool_t2"), sem("pool_h0"), sem("pool_links")

        aw_v = [w.rearrange("s o c d -> (s o) c d") for w in (wq, wk, wv, wo)]
        NQ = 2
        HALF = N // NQ

        def pending(eng, reg):
            return eng.snap(reg, min_val=0, max_val=4 * NB - 1)

        def hold(eng, s, value):
            eng.wait_ge(s, value)
            eng.sem_inc(held, 1)

        block = ctx.enter_context(nc.Block())

        @block.sync
        def _(sp):
            for j in range(NQ):
                sp.dma_start(xchan[:, HALF * j:HALF * j + HALF], x_chan[:, HALF * j:HALF * j + HALF]).then_inc(d_x[j], 16)
            sp.dma_start(sfirst[:, :], first).then_inc(d_first, 16)
            for h in range(NH):
                src = bass.AP(rpb.tensor, rpb.offset + h * (RW * RW + 2 * PAD) + PAD + (KW - 1) - (IMG - 1),
                              [[1, IMG], [RW, RW], [1, IMG]])
                sp.dma_start(rawbias[IMG * h:IMG * h + IMG, :, :], src).then_inc(d_rpb, 16)
            sp.dma_start(srest[:, :], rest).then_inc(d_rest, 16)
            sp.dma_start(xtok[:, :, :, :], x_tok).then_inc(d_xtok, 16)
            sp.dma_start(m8[:, :, :], masks).then_inc(d_mask, 16)

            n = sp.alloc_register("sp_n")
            nf = sp.alloc_register("sp_nf")
            na = sp.alloc_register("sp_na")
            for r in (n, nf, na):
                sp.reg_mov(r, 0)
            key = sp.alloc_register("sp_key")
            sp.wait_ge(decided, 1)
            sp.reg_load(key, ctl[0:1, 0:1])
            with sp.While(lambda: sp.snap(key) < 4 * NB):
                k = pending(sp, key)
                op = sp.value_load(ix8[0:1, 0:1], min_val=0, max_val=NOPS - 1)
                row = sp.snap((k // 4) * NOPS + op, min_val=0, max_val=NB * NOPS - 1)
                with sp.If((k // 2) % 2 == 1):
                    sp.dma_start(stage[:, :], rec[bass.ds(row, 1), :, :].rearrange("u p w -> (u p) w")).then_inc(d_w, 16)
                    sp.reg_add(nf, nf, 1)
                with sp.If(k % 2 == 1):
                    sp.wait_ge(pe_ay, sp.snap(na) * NQ + 1)
                    for i in range(4):
                        for b in range(B):
                            sp.dma_start(aw[C * b:C * b + C, i, b, :],
                                         aw_v[i][bass.ds(row, 1), :, :].rearrange("u c d -> (u c) d")).then_inc(d_aw, 16)
                    sp.reg_add(na, na, 1)
                hold(sp, w_live, sp.snap(nf) + 1)
                hold(sp, rest_live, sp.snap(nf) + 1)
                sp.reg_add(n, n, 1)
                hold(sp, decided, sp.snap(n) + 1)
                sp.reg_load(key, ctl[0:1, 0:1])

            for j in range(NQ):
                sp.wait_ge(dve_o, j + 1)
                sp.dma_start(out[:, 4 * j:4 * j + 4, :, :], cen[:, 4 * j:4 * j + 4, :, :]).then_inc(d_out, 16)
            sp.wait_ge(d_out, 16 * NQ)

        @block.gpsimd
        def _(pool):
            made = [0]

            def then(ins):
                made[0] += 1
                ins.then_inc(pool_links, 1)
                pool.wait_ge(pool_links, made[0])

            nc.gpsimd.memset(qbd[C:2 * C, :, 0, :, :], 0.0).then_inc(zeroed, 1)
            pool.wait_ge(zeroed, 1)
            nc.gpsimd.memset(vbd[:, :, :, :], 0.0).then_inc(zeroed, 1)
            pool.wait_ge(zeroed, 2)
            nc.gpsimd.memset(w1z[:, :, :], 0.0)
            nc.gpsimd.memset(aw[:, :, :, :], 0.0)
            nc.gpsimd.memset(keyf[:, :], -1.0)
            nc.gpsimd.memset(minus_half[:, :], -0.5)
            pool.drain()
            pool.sem_inc(zeroed, 1)
            pool.wait_ge(zeroed, 3)
            nc.gpsimd.memset(qbd[0:C, IMG // 2:, 1, :, :], 0.0).then_inc(zeroed, 1)
            pool.wait_ge(d_xtok, 16)
            pool.wait_ge(dve_brow, 1)
            nc.gpsimd.tensor_tensor(xtok[:, :, :, :].rearrange("p t b c -> p (t b) c"),
                                    xtok[:, :, :, :].rearrange("p t b c -> p (t b) c"),
                                    brow[:, :].unsqueeze(1).broadcast_to([128, NT * B, C]), ALU.add).then_inc(pool_xb, 1)

            def diagonals(g):
                pool.wait_ge(dve_ri, g + 1)
                if g >= 2:
                    pool.wait_ge(pe_rb, g - 1)
                for b in range(B):
                    ins = nc.gpsimd.tensor_tensor(
                        dinv[:, g % 2, b, :, :],
                        kc("eye32").unsqueeze(1).broadcast_to([128, ROWS, IMG]),
                        prinv[:, ROWS * g:ROWS * g + ROWS, b].unsqueeze(2).broadcast_to([128, ROWS, IMG]), ALU.mult)
                ins.then_inc(pool_d, 1)

            def norm1(g):
                cols = slice(4 * g, 4 * g + 4)
                last = g == GROUPS - 1
                pool.wait_ge(dve_rs, g + 1)
                if not last:
                    then(nc.gpsimd.tensor_tensor(rs[:, 2:4, cols], rs[:, 0:2, cols],
                                                 minus_half[:, 0:1].unsqueeze(2).broadcast_to([128, 2, 4]), ALU.pow))
                else:
                    pool.wait_ge(dve_xn, 1)
                wide = [128, 4, C]
                flat = "p t b c -> p (t b) c"
                then(nc.gpsimd.tensor_tensor(cen[:, 2 * g:2 * g + 2, :, :].rearrange(flat), t1[:, 2 * g:2 * g + 2, :, :].rearrange(flat),
                                             mv[:, cols, 0].unsqueeze(2).broadcast_to(wide), ALU.subtract))
                if not last:
                    twice = [128, 4, 2, C]
                    nc.gpsimd.tensor_tensor(xn2[:, 2 * g:2 * g + 2, :, :].rearrange("p t b (k c) -> p (t b) k c", k=2),
                                            cen[:, 2 * g:2 * g + 2, :, :].rearrange(flat).unsqueeze(2).broadcast_to(twice),
                                            rs[:, 3, cols].unsqueeze(2).unsqueeze(3).broadcast_to(twice), ALU.mult).then_inc(pool_xn, 1)
                nc.gpsimd.tensor_tensor(a[:, 2 * g:2 * g + 2, :, :].rearrange(flat), cen[:, 2 * g:2 * g + 2, :, :].rearrange(flat),
                                        rs[:, 2, cols].unsqueeze(2).broadcast_to(wide), ALU.mult).then_inc(pool_a, 1)

            diagonals(0)
            diagonals(1)
            norm1(0)
            diagonals(2)
            norm1(1)
            norm1(2)
            norm1(3)
            pool.wait_ge(pool_a, GROUPS)
            nc.gpsimd.tensor_tensor(t1b[:, :, :, :].rearrange("p t b c -> p (t b) c"), t1[:, :, :, :].rearrange("p t b c -> p (t b) c"),
                                    kc("lnb").unsqueeze(1).broadcast_to([128, NT * B, C]), ALU.add).then_inc(pool_t1b, 1)
            wide = [128, NT // 2, C]

            def half(j):
                return slice(4 * j, 4 * j + 4), slice(4 * B * j, 4 * B * j + 4 * B, B)

            def inverse_root(n, cols):
                pool.wait_ge(dve_ve0, n)
                then(nc.gpsimd.tensor_tensor(rstd[:, cols], sd[:, 0, cols], minus_half[:, 0:1].broadcast_to([128, NT // 2]), ALU.pow))

            for j in range(NQ):
                t, cols = half(j)
                inverse_root(2 * j + 1, cols)
                of = y[:, t, 0, :]
                then(nc.gpsimd.tensor_tensor(of, of, mv[:, cols, 0].unsqueeze(2).broadcast_to(wide), ALU.subtract))
                then(nc.gpsimd.tensor_tensor(of, of, rstd[:, cols].unsqueeze(2).broadcast_to(wide), ALU.mult))
                then(nc.gpsimd.tensor_tensor(of, of, kc("lnw").unsqueeze(1).broadcast_to(wide), ALU.mult))
                nc.gpsimd.tensor_tensor(t2[:, t, 0, :], of, t1b[:, t, 0, :], ALU.add).then_inc(pool_t2, 1)
                inverse_root(2 * j + 2, cols)
                pool.wait_ge(pool_t2, j + 1)
                then(nc.gpsimd.tensor_tensor(of, t2[:, t, 0, :], mv[:, cols, 0].unsqueeze(2).broadcast_to(wide), ALU.subtract))
                nc.gpsimd.tensor_tensor(xn[:, t, 0, :], of, rstd[:, cols].unsqueeze(2).broadcast_to(wide), ALU.mult).then_inc(pool_h0, 1)

        @block.tensor
        def _(pe):
            pe.sem_inc(pe_ay, 1)

            def keep_clock(n, to=bank(5), of=srest[:, 0:512]):
                for _ in range(n):
                    nc.tensor.matmul(to[:, 0:of.shape[1]], of[:, 0:128], of, start=True, stop=True)

            pe.wait_ge(d_first, 16)
            pe.wait_ge(dve_avg, 1)
            nc.tensor.matmul(bank(2)[:, 0:1], kc("pairavg"), gmv[:, 0:1], start=True, stop=True).then_inc(pe_avg, 1)
            keep_clock(1, bank(0), sfirst[:, 0:256])
            pe.wait_ge(dve_avg, 2)
            nc.tensor.matmul(bank(2)[:, 1:2], kc("pairavg"), gtmp[:, 1:2], start=True, stop=True).then_inc(pe_avg, 1)
            keep_clock(1, bank(0), sfirst[:, 0:256])
            for j in range(NQ):
                pe.wait_ge(dve_gn, j + 1)
                cols = gnT[:, HALF * j:HALF * j + HALF]
                nc.tensor.matmul(bank(4 + j), wqkv[:, 0, :], cols,
                                 start=True, stop=True).then_inc(pe_q, 1)
                nc.tensor.matmul(bank(6 + j), wqkv[:, 1, :], cols,
                                 start=True, stop=True).then_inc(pe_k, 1)

            def values(r):
                for h in range(NH):
                    ins = nc.tensor.matmul(bank(0, 2)[IMG * h:IMG * h + IMG, IMG * r:IMG * r + IMG],
                                           gnT[:, IMG * r:IMG * r + IMG],
                                           wqkv[:, 2, :].rearrange("p (b c) -> p b c", b=B)[:, :, HD * h:HD * h + HD],
                                           start=True, stop=True)
                if r % 16 == 15:
                    ins.then_inc(pe_v, 1)

            RING = (2, 3, 7)

            def scores(r):
                if r >= len(RING):
                    pe.wait_ge(dve_s, B * (r - len(RING) + 1))
                elif r == 2:
                    pe.wait_ge(act_k, 2)
                for b in range(B):
                    ins = nc.tensor.matmul(bank(RING[r % 3])[:, 256 * b:256 * b + WIN],
                                           qbd[:, r, b, :, :].rearrange("p h w -> p (h w)"),
                                           kT[:, IMG * first_row(r):IMG * first_row(r) + WIN],
                                           start=True, stop=True)
                ins.then_inc(pe_s, 1)

            def norms(g):
                last = g == GROUPS - 1
                if last:
                    pe.wait_ge(dve_d, 1)
                else:
                    pe.wait_ge(pool_d, g + 1)
                    if g >= 1:
                        pe.wait_ge(dve_t1, g)
                        pe.wait_ge(act_rb, g)
                for b in range(B):
                    ins = nc.tensor.matmul(bank(7 if last else 6)[C * b:C * b + C, 0:LANES], kc("vmask")[:, 0:C],
                                           dinv[:, g % 2, b, :, :].rearrange("p r w -> p (r w)"), start=True, stop=True)
                ins.then_inc(pe_rb, 1)

            def weighted(g, part=range(ROWS)):
                pieces = list(key_rows(g, part))
                flat = probT[:, g % 2, :, :, :].rearrange("p r b w -> p (r b w)")
                for n, (kr, q, nq) in enumerate(pieces):
                    q0 = q - ROWS * g
                    for b in range(B):
                        base = (q0 * B + b) * SLOTS * IMG + slot(q, kr) * IMG
                        rhs = bass.AP(flat.tensor, flat.offset + base, [flat.ap[0], [(B * SLOTS - 1) * IMG, nq], [1, IMG]])
                        ins = nc.tensor.matmul(bank(4 + g % 2)[C * b:C * b + C, IMG * q0:IMG * (q0 + nq)],
                                               vbd[:, kr, b, :], rhs, start=n == 0 and part.start == 0,
                                               stop=n == len(pieces) - 1 and part.stop == ROWS,
                                               skip_group_check=True)
                    if n == len(pieces) - 1 and part.stop == ROWS:
                        ins.then_inc(pe_pv, 1)
                    yield

            def project(g):
                pe.wait_ge(dve_att, g + 1)
                if g < GROUPS - 1:
                    pe.wait_ge(act_rb, g + 1)
                else:
                    pe.wait_ge(dve_t1, g)
                for t in (2 * g, 2 * g + 1):
                    ins = nc.tensor.matmul(bank(6)[:, LANES + 128 * (t % 2):LANES + 128 * (t % 2) + 128],
                                           att[:, 128 * t:128 * t + 128], wpr, start=True, stop=True)
                ins.then_inc(pe_pr, 1)

            def normal_tokens(j):
                if j == 0:
                    pe.wait_ge(pool_xn, 2)
                else:
                    pe.wait_ge(pool_xn, 3)
                    pe.wait_ge(dve_xn, 1)
                for b in range(B):
                    for t in range(4 * j, 4 * j + 4):
                        to = bank(b) if j == 0 else bank(7 - b)
                        ins = nc.tensor.transpose(to[:, 128 * (t % 4):128 * (t % 4) + 128], xn2[:, t, b, :], ident)
                    ins.then_inc(pe_nT, 1)

            pe.wait_ge(d_rest, 16)
            nc.tensor.matmul(bank(1)[:, 0:C], kc("vb", C).broadcast_to([C, 128]), wpr[0:C, 0:C],
                             start=True, stop=True).then_inc(pe_vb, 1)
            pe.wait_ge(zeroed, 2)
            pe.wait_ge(dve_zero, 1)
            pe.wait_ge(dve_gn, NQ)
            work = iter(())
            for r in range(IMG):
                if r % (IMG // 2) == 0:
                    pe.wait_ge(act_q, r // (IMG // 2) + 1)
                    pe.wait_ge(dve_q, r // (IMG // 2) + 1)
                    if r:
                        pe.wait_ge(zeroed, 4)
                    if r == 0:
                        pe.wait_ge(act_k, 1)
                if first_row(r) + KW > IMG // 2 and (r == 0 or first_row(r - 1) + KW <= IMG // 2):
                    pe.wait_ge(act_k, 2)
                scores(r)
                if r == 1:
                    for rv in range(IMG // 2):
                        values(rv)
                g, rg = r // ROWS, r % ROWS
                if r == 4:
                    pe.wait_ge(dve_brow, 1)
                if r in range(4, 12):
                    for rv in (2 * r + 8, 2 * r + 9):
                        values(rv)
                if rg == 3 and g >= 1:
                    for _ in work:
                        pass
                    pe.wait_ge(dve_t, 4 * g)
                    pe.wait_ge(act_v, min(g, 2))
                    if g == 1:
                        pe.wait_ge(act_q, 2)
                        pe.wait_ge(dve_q, 2)
                        pe.wait_ge(act_k, 2)
                    work = weighted(g - 1)
                for _ in range(3 if g == GROUPS - 1 else 2):
                    next(work, None)
                if rg == 4 and g >= 2:
                    project(g - 2)
                if rg == 7 and g >= 1:
                    norms(g - 1)
            for _ in work:
                pass
            pe.wait_ge(act_v, 2)
            keep_clock(2, bank(0))
            pe.wait_ge(dve_t, 4 * GROUPS - 1)
            for n, _ in enumerate(weighted(GROUPS - 1, range(ROWS - 2))):
                if n == 5:
                    project(GROUPS - 2)
            pe.wait_ge(dve_t, 4 * GROUPS)
            for _ in weighted(GROUPS - 1, range(ROWS - 2, ROWS)):
                pass
            norms(GROUPS - 1)
            normal_tokens(0)
            project(GROUPS - 1)
            keep_clock(4)

            pe.wait_ge(dve_t1, GROUPS)
            normal_tokens(1)
            keep_clock(2)

            def similarities(b, m):
                i = NT * b + m
                if m == 0:
                    pe.wait_ge(dve_xa, NQ * (b + 1))
                    pe.wait_ge(act_xa, B + b + 1)
                if i >= 2:
                    pe.wait_ge(act_e, i - 1)
                for part, lhs in enumerate((xh, xl)):
                    for j in range(NQ):
                        ins = nc.tensor.matmul(bank(2 + 2 * (i % 2) + j), lhs[:, b, 128 * m:128 * m + 128],
                                               xa[:, b, HALF * j:HALF * j + HALF], start=part == 0, stop=part == 1)
                ins.then_inc(pe_sim, 1)

            def row_norms(b, j):
                pe.wait_ge(dve_rinv, NQ * b + j + 1)
                if b == 1:
                    pe.wait_ge(act_e, B * NT)
                for t in range(4 * j, 4 * j + 4):
                    ins = nc.tensor.matmul(bank(2 * b + j)[:, 128 * (t % 4):128 * (t % 4) + 128],
                                           rinv[:, NT * b + t:NT * b + t + 1].broadcast_to([128, 128]), ident, start=True, stop=True)
                ins.then_inc(pe_rB, 1)

            def gathered(b, m, halves):
                i = NT * b + m
                pe.wait_ge(dve_r, i + 1)
                pe.wait_ge(act_f, i + 1)
                pe.wait_ge(dve_xc, i + 1)
                for j in halves:
                    cols = slice(HALF * j, HALF * j + HALF)
                    row, col = (rr[:, m % 4, cols], ff[:, m % 4, cols]) if b == 0 else (
                        sim1[:, N * m + HALF * j:N * m + HALF * j + HALF], big[:, N * m + HALF * j:N * m + HALF * j + HALF])
                    to = bank(6 - 2 * b + j)
                    nc.tensor.matmul(to[0:C, :], a[:, m, b, :], row, start=m == 0, stop=m == NT - 1)
                    ins = nc.tensor.matmul(to[C:2 * C, :], xc[:, b, m, :], col, start=m == 0, stop=m == NT - 1)
                if b == 0 or m == NT - 1:
                    ins.then_inc(pe_u, 1)

            def to_tokens(b, j, to):
                pe.wait_ge(act_us, NQ * b + j + 1)
                for t in range(4 * j, 4 * j + 4):
                    ins = nc.tensor.matmul(to[:, C * t:C * t + C], us[:, b, 128 * t:128 * t + 128], kc("fold"),
                                           start=True, stop=True)
                ins.then_inc(pe_y, 1)

            for m in range(NT):
                similarities(0, m)
            pe.wait_ge(dve_xa, 2 * B)
            row_norms(0, 0)
            similarities(1, 0)
            row_norms(0, 1)
            for m in range(1, 4):
                similarities(1, m)
            for m in range(NT):
                if m in range(1, 5):
                    similarities(1, m + 3)
                gathered(0, m, range(NQ))
                if m == 4:
                    for j in range(NQ):
                        row_norms(1, j)
            pe.wait_ge(dve_r, NT)
            order = [(0, 0), (0, 1), (1, 0), (0, 2), (0, 3), (1, 1), (0, 4), (0, 5), (1, 2), (0, 6), (0, 7)]
            for j, m in order:
                gathered(1, m, (j,))
                if (j, m) == (1, 0):
                    for half in range(NQ):
                        to_tokens(0, half, bank(0))
            for m in range(3, NT):
                gathered(1, m, (1,))
                if m == 3:
                    to_tokens(1, 0, bank(1))
            to_tokens(1, 1, bank(6))

            n, nf, na, hv = (pe.alloc_register(f"pe_{s}") for s in ("n", "nf", "na", "hv"))
            for r in (n, nf, na):
                pe.reg_mov(r, 0)
            pe.reg_mov(hv, NQ)
            key = pe.alloc_register("pe_key")
            for j in range(NQ):
                pe.wait_ge(pool_h0, j + 1)
                pe.wait_ge(dve_h0, j + 1)
                for t in range(4 * j, 4 * j + 4):
                    ins = nc.tensor.transpose(bank(7 - j)[:, 128 * (t % 4):128 * (t % 4) + 128],
                                              xn[:, t, :, :].rearrange("p b c -> p (b c)"), ident)
                ins.then_inc(pe_hT, 1)
                if j == 0:
                    keep_clock(3)
                    pe.wait_ge(decided, 1)
                    pe.reg_load(key, ctl[0:1, 0:1])
                    pe.wait_ge(dve_ve1, NQ + 1)
                    keep_clock(1)
                    pe.wait_ge(dve_ve1, 2 * NQ)
                    keep_clock(1)
                else:
                    keep_clock(1)

            def decide_row(count):
                pe.wait_ge(h_ready, count)
                nc.tensor.transpose(bank(1)[0:1, 0:C], H[0:C, 0:1], ident[0:C, 0:C]).then_inc(pe_row, 1)

            with pe.While(lambda: pe.snap(key) < 4 * NB):
                k = pending(pe, key)
                with pe.If(k % 2 == 1):
                    done = pe.snap(na)
                    hold(pe, d_aw, done * (16 * 4 * B) + 16 * 4 * B)
                    pe.wait_ge(act_h, 1)
                    pe.wait_ge(h_ready, pe.snap(hv))
                    for i in range(2):
                        for j in range(NQ):
                            nc.tensor.matmul(bank(2 * i + j), aw[:, i, :, :].rearrange("p b c -> p (b c)"),
                                             H[:, HALF * j:HALF * j + HALF], start=True, stop=True)
                    for t in range(NT):
                        ins = nc.tensor.matmul(bank(4, 2)[:, 128 * t:128 * t + 128], H[:, 128 * t:128 * t + 128],
                                               aw[:, 2, :, :].rearrange("p b c -> p (b c)"), start=True, stop=True)
                    ins.then_inc(pe_aqkv, 1)
                    pe.wait_ge(dve_aqkv, done + 1)
                    for u in range(B * NT):
                        b, t = u // NT, u % NT
                        if u:
                            pe.wait_ge(act_ap, done * (B * NT) + u)
                        for j in range(NQ):
                            ins = nc.tensor.matmul(bank(j), aq[C * b:C * b + C, 128 * t:128 * t + 128],
                                                   ak[C * b:C * b + C, HALF * j:HALF * j + HALF], start=True, stop=True)
                        ins.then_inc(pe_asc, 1)
                        pe.wait_ge(dve_apn, done * (B * NT) + u + 1)
                        for kt in range(NT):
                            ins = nc.tensor.transpose(bank(2, 2)[:, 128 * kt:128 * kt + 128],
                                                      ap_[:, 128 * kt:128 * kt + 128], ident)
                        ins.then_inc(pe_atr, 1)
                        pe.wait_ge(dve_apt, done * (B * NT) + u + 1)
                        for kt in range(NT):
                            ins = nc.tensor.matmul(bank(4, 2)[C * b:C * b + C, 128 * t:128 * t + 128],
                                                   av[:, 128 * kt + C * b:128 * kt + C * b + C],
                                                   apt[:, 128 * kt:128 * kt + 128], start=kt == 0, stop=kt == NT - 1)
                        ins.then_inc(pe_ao, 1)
                    pe.wait_ge(dve_ao, done + 1)
                    for j in range(NQ):
                        nc.tensor.matmul(bank(6 + j), aw[:, 3, :, :].rearrange("p b c -> p (b c)"),
                                         ao[:, HALF * j:HALF * j + HALF], start=True, stop=True).then_inc(pe_ay, 1)
                    pe.reg_add(na, na, 1)
                    pe.reg_add(hv, hv, NQ)
                with pe.If((k // 2) % 2 == 0):
                    pe.wait_ge(act_h, 1)
                    hold(pe, h_ready, pe.snap(hv))
                    decide_row(1)
                with pe.If((k // 2) % 2 == 1):
                    done = pe.snap(nf)
                    have = pe.snap(hv)

                    def hidden(j, b, mc):
                        nc.tensor.matmul(bank(4 * j + 2 * b + mc), w1z[:, b, 128 * mc:128 * mc + 128],
                                         H[:, HALF * j:HALF * j + HALF], start=True, stop=True).then_inc(pe_z, 1)

                    def new_state(j, mc):
                        for b in range(B):
                            ins = nc.tensor.matmul(bank(4 * j)[C * b:C * b + C, :], w2l[:, mc, :], z[:, j, b, mc, :],
                                                   start=mc == 0, stop=mc == 1)
                        if mc == 1:
                            ins.then_inc(pe_h, 1)

                    pe.wait_ge(act_h, 1)
                    pe.wait_ge(h_ready, have - 1)
                    pe.wait_ge(w_live, done + 2)
                    for mc in range(2):
                        ins = nc.tensor.matmul(token0[:, mc:mc + 1], w1z[:, 0, 128 * mc:128 * mc + 128], H[:, 0:1],
                                               start=True, stop=True)
                    ins.then_inc(pe_z0, 1)
                    hidden(0, 0, 0)
                    hidden(0, 0, 1)
                    hold(pe, rest_live, done + 2)
                    pe.wait_ge(act_z0, done + 1)
                    for kc_ in range(2):
                        nc.tensor.matmul(row0, z0[:, kc_:kc_ + 1], w2l[:, kc_, :], start=kc_ == 0, stop=False)
                    nc.tensor.matmul(row0, b2l[0:C, :], ident[0:C, 0:C], start=False, stop=True).then_inc(pe_row, 1)
                    hidden(0, 1, 0)
                    hidden(0, 1, 1)
                    pe.wait_ge(act_z, done * 6 + 3)
                    new_state(0, 0)
                    pe.wait_ge(h_ready, have)
                    hidden(1, 0, 0)
                    pe.wait_ge(act_z, done * 6 + 4)
                    new_state(0, 1)
                    hidden(1, 1, 0)
                    hidden(1, 1, 1)
                    hold(pe, decided, pe.snap(n) + 2)
                    hidden(1, 0, 1)
                    pe.wait_ge(act_z, done * 6 + 5)
                    pe.wait_ge(dve_z, done * 2 + 1)
                    new_state(1, 0)
                    pe.wait_ge(act_z, done * 6 + 6)
                    pe.wait_ge(dve_z, done * 2 + 2)
                    new_state(1, 1)
                    keep_clock(1)
                    pe.reg_add(nf, nf, 1)
                    pe.reg_add(hv, hv, NQ)
                pe.reg_add(n, n, 1)
                hold(pe, decided, pe.snap(n) + 1)
                pe.reg_load(key, ctl[0:1, 0:1])

            have = pe.snap(hv)
            for j in range(NQ):
                pe.wait_ge(act_h, 1)
                pe.wait_ge(h_ready, have + (j - 1))
                for t in range(4 * j, 4 * j + 4):
                    ins = nc.tensor.transpose(bank(2 + j)[:, 128 * (t % 4):128 * (t % 4) + 128],
                                              H[:, 128 * t:128 * t + 128], ident)
                ins.then_inc(pe_oT, 1)

        @block.scalar
        def _(act):
            act.sem_inc(w_live, 1)
            act.wait_ge(d_first, 16)

            def have_table(n, f):
                nc.scalar.activation(warm[:, n:n + 1], kc("pairavg")[:, 0:1], f)

            have_table(0, ACT.Sqrt)
            act.wait_ge(dve_var, 1)
            nc.scalar.activation(gtmp[:, 3:4], gtmp[:, 2:3], ACT.Sqrt).then_inc(act_sd, 1)
            have_table(5, ACT.Exp)
            act.wait_ge(dve_qb, 1)

            def queries(j, h):
                rows = slice(IMG // 2 * j, IMG // 2 * (j + 1))
                ins = nc.scalar.activation(qbd[0:C, rows, 0, h, :], bank(4 + j)[0:C, :].rearrange("p (r w) -> p r w", w=IMG),
                                           ACT.Identity, scale=kc("qmask", C)[:, h:h + 1], bias=qbm[0:C, h:h + 1])
                if h == NH - 1:
                    ins.then_inc(act_q, 1)

            def values(c, h):
                if h == 0:
                    act.wait_ge(pe_v, c + 1)
                if (c, h) == (0, 0):
                    act.wait_ge(zeroed, 2)
                part = slice(IMG * h, IMG * h + IMG)
                ins = nc.scalar.activation(vbd[part, 16 * c:16 * c + 16, :, HD * h:HD * h + HD],
                                           bank(c)[part, :].rearrange("p (r b d) -> p r b d", b=B, d=HD), ACT.Copy)
                if h == NH - 1:
                    ins.then_inc(act_v, 1)

            def divisors(g):
                act.wait_ge(pe_rb, g + 1)
                if g >= 2:
                    act.wait_ge(dve_att, g - 1)
                nc.scalar.activation(rbs[:, g % 2, :], bank(7 if g == GROUPS - 1 else 6)[:, 0:LANES], ACT.Copy).then_inc(act_rb, 1)

            def high(n):
                act.wait_ge(pe_nT, n + 1)
                j, b = n // B, n % B
                of, cols = bank(b) if j == 0 else bank(7 - b), slice(HALF * j, HALF * j + HALF)
                nc.scalar.activation(xh[:, b, cols], of, ACT.Copy).then_inc(act_xh, 1)
                act.wait_ge(act_xh, n + 1)
                nc.scalar.activation(xa[0:C, b, cols], xh[0:C, b, cols].bitcast(F32), ACT.Copy).then_inc(act_xa, 1)

            act.wait_ge(pe_q, 1)
            for h in range(NH):
                queries(0, h)
            for j in range(NQ):
                act.wait_ge(pe_k, j + 1)
                nc.scalar.activation(kT[:, HALF * j:HALF * j + HALF], bank(6 + j), ACT.Identity,
                                     bias=qkb[:, 1:2]).then_inc(act_k, 1)
            for i in range(B * IMG):
                if i < 8 and i % 2 == 0:
                    if i == 0:
                        act.wait_ge(pe_q, 2)
                    queries(1, i // 2)
                act.wait_ge(dve_s, i + 1)
                if i >= 12:
                    act.wait_ge(dve_t, i // 4 - 2)
                nc.scalar.activation(prob[:, i // 4 % 3, WIN * (i % 4):WIN * (i % 4) + WIN], sneg[:, i % 4, :], ACT.Exp,
                                     scale=-1.0, bias=nmax[:, i:i + 1], accum_out=psumr[:, i:i + 1]).then_inc(act_p, 1)
                if i in range(8, 16) and i % 2:
                    values(0, (i - 8) // 2)
                if i in range(26, 34) and i % 2:
                    values(1, (i - 26) // 2)
                if i % 16 == 13 and i > 16:
                    divisors(i // 16 - 1)
            divisors(GROUPS - 1)
            have_table(1, ACT.Sqrt)
            for b in range(B):
                high(b)
            act.wait_ge(dve_rs, GROUPS)
            cols = slice(NT * B - 4, NT * B)
            nc.scalar.activation(rs[:, 2:4, cols], rs[:, 0:2, cols], ACT.Sqrt).then_inc(act_root, 1)
            have_table(2, ACT.Exp)
            for b in range(B):
                high(B + b)

            def expsim(b, m):
                i = NT * b + m
                act.wait_ge(pe_sim, i + 1)
                nc.scalar.activation(sims[b][:, N * m:N * m + N], bank(2 + 2 * (i % 2), 2), ACT.Exp, scale=2.0,
                                     accum_out=rsum[:, i:i + 1]).then_inc(act_e, 1)

            def expcol(b, m):
                i = NT * b + m
                act.wait_ge(dve_r, i + 1)
                if b == 0:
                    if m >= 4:
                        act.wait_ge(pe_u, m - 3)
                    to, of = ff[:, m % 4, :], rr[:, m % 4, :]
                else:
                    to, of = big[:, N * m:N * m + N], sim1[:, N * m:N * m + N]
                nc.scalar.activation(to, of, ACT.Exp, accum_out=csum[:, i:i + 1]).then_inc(act_f, 1)

            def take_sums(b, j):
                act.wait_ge(pe_u, NT if b == 0 else NT + j + 1)
                nc.scalar.activation(us[:, b, HALF * j:HALF * j + HALF], bank(6 - 2 * b + j), ACT.Copy).then_inc(act_us, 1)

            def root(n, j):
                act.wait_ge(dve_ve1, n + 1)
                cols = slice(4 * B * j + 1, 4 * B * j + 4 * B, B)
                nc.scalar.activation(sd[:, 1, cols], sd[:, 0, cols], ACT.Sqrt).then_inc(act_sqrt, 1)

            for m in range(NT):
                expsim(0, m)
            for m in range(2):
                expsim(1, m)
            for m in range(NT):
                expcol(0, m)
                if m < 6:
                    expsim(1, m + 2)
            for m in range(NT):
                expcol(1, m)
                if m == 2:
                    for j in range(NQ):
                        take_sums(0, j)
            have_table(3, ACT.Sqrt)
            take_sums(1, 0)
            root(0, 0)
            take_sums(1, 1)
            root(1, 0)
            act.wait_ge(pe_hT, 1)
            nc.scalar.activation(H[:, 0:HALF], bank(7), ACT.Copy).then_inc(act_h, 1)
            root(2, 1)
            act.wait_ge(zeroed, 3)
            n, nf, na = (act.alloc_register(f"act_{s}") for s in ("n", "nf", "na"))
            for r in (n, nf, na):
                act.reg_mov(r, 0)
            key = act.alloc_register("act_key")
            act.wait_ge(decided, 1)
            act.reg_load(key, ctl[0:1, 0:1])
            root(3, 1)
            with act.While(lambda: act.snap(key) < 4 * NB):
                k = pending(act, key)
                with act.If(k % 2 == 1):
                    done = act.snap(na)
                    for u in range(B * NT):
                        act.wait_ge(dve_amx, done * (B * NT) + u + 1)
                        nc.scalar.activation(ap_, bank(0, 2), ACT.Exp, scale=C ** -0.5, bias=am_stat[:, 1:2],
                                             accum_out=am_stat[:, 2:3]).then_inc(act_ap, 1)
                    act.reg_add(na, na, 1)
                with act.If((k // 2) % 2 == 1):
                    done = act.snap(nf)
                    have_table(4, ACT.Relu)
                    hold(act, d_w, done * 16 + 16)
                    nc.scalar.activation(w1z[0:C, 0, :], stage[0:C, 0:HID], ACT.Copy).then_inc(w_live, 1)
                    hold(act, rest_live, done + 2)
                    act.wait_ge(pe_z0, done + 1)
                    for mc in range(2):
                        ins = nc.scalar.activation(z0[:, mc:mc + 1], token0[:, mc:mc + 1], ACT.Relu, bias=b1l[:, mc:mc + 1])
                    ins.then_inc(act_z0, 1)
                    for j in range(NQ):
                        for b, mc in ((0, 0), (0, 1), (1, 0), (1, 1))[:4 - 2 * j]:
                            act.wait_ge(pe_z, done * 8 + (2 * b + mc + 1 if j == 0 else 5 + 3 * mc))
                            nc.scalar.activation(z[:, j, b, mc, :], bank(4 * j + 2 * b + mc), ACT.Relu,
                                                 bias=b1l[:, mc:mc + 1]).then_inc(act_z, 1)
                    act.reg_add(nf, nf, 1)
                act.reg_add(n, n, 1)
                hold(act, decided, act.snap(n) + 1)
                act.reg_load(key, ctl[0:1, 0:1])

        @block.vector
        def _(dve):
            links = [0]

            def link(ins):
                links[0] += 1
                ins.then_inc(chain, 1)
                dve.wait_ge(chain, links[0])

            v = nc.vector
            dve.sem_inc(h_ready, 1)
            dve.sem_inc(rest_live, 1)
            nc.vector.memset(qbd[0:C, 0:IMG // 2, 1, :, :], 0.0).then_inc(dve_zero, 1)
            for j in range(NQ):
                dve.wait_ge(d_x[j], 16)
                ins = v.bn_stats(gstat[:, j, :], xchan[:, HALF * j:HALF * j + HALF])
            link(ins)
            v.bn_aggr(gmv[:, :], gstat[:, :, :].rearrange("p j s -> p (j s)")).then_inc(dve_avg, 1)
            dve.wait_ge(pe_avg, 1)
            link(v.tensor_tensor(gtmp[:, 0:1], gmv[:, 0:1], bank(2)[:, 0:1], ALU.subtract))
            link(v.tensor_tensor(gtmp[:, 1:2], gtmp[:, 0:1], gtmp[:, 0:1], ALU.mult))
            dve.wait_ge(dve_avg, 1)
            v.tensor_tensor(gtmp[:, 1:2], gtmp[:, 1:2], gmv[:, 1:2], ALU.add).then_inc(dve_avg, 1)
            dve.wait_ge(d_first, 16)
            v.tensor_scalar(qbm[:, :], kc("qmask"), qkb[:, 0:1], None, ALU.mult).then_inc(dve_qb, 1)
            dve.wait_ge(pe_avg, 2)
            v.tensor_scalar(gtmp[:, 2:3], bank(2)[:, 1:2], 1e-5, None, ALU.add).then_inc(dve_var, 1)
            dve.wait_ge(act_sd, 1)
            link(v.reciprocal(gtmp[:, 4:5], gtmp[:, 3:4]))
            for j in range(NQ):
                v.tensor_scalar(gnT[:, HALF * j:HALF * j + HALF], xchan[:, HALF * j:HALF * j + HALF], bank(2)[:, 0:1],
                                gtmp[:, 4:5], ALU.subtract, ALU.mult).then_inc(dve_gn, 1)
            dve.wait_ge(d_rpb, 16 * NH)
            backwards = bass.AP(rawbias.tensor, rawbias.offset + RW * IMG - 1, [rawbias.ap[0], [-IMG, RW], [-1, IMG]])
            dve.wait_ge(d_rest, 16)
            link(v.scalar_tensor_tensor(bias[:, :, :], backwards, -1.0,
                                        kc("outside").unsqueeze(1).broadcast_to([128, RW, IMG]), ALU.mult, ALU.add))

            def queries(j, h):
                rows = slice(IMG // 2 * j, IMG // 2 * (j + 1))
                if h == 0:
                    dve.wait_ge(pe_q, j + 1)
                ins = v.tensor_scalar(qbd[C:2 * C, rows, 1, h, :],
                                      bank(4 + j)[C:2 * C, :].rearrange("p (r w) -> p r w", w=IMG),
                                      qkb[C:2 * C, 0:1], kc("qmask")[C:2 * C, NH + h:NH + h + 1], ALU.add, ALU.mult)
                if h == NH - 1:
                    ins.then_inc(dve_q, 1)

            dve.wait_ge(zeroed, 1)
            for h in range(NH):
                queries(0, h)
            dve.wait_ge(pe_vb, 1)
            v.tensor_tensor(brow[:, :], kc("pb"), bank(1)[:, 0:C], ALU.add).then_inc(dve_brow, 1)

            def shifted_scores(i):
                r = i // B
                d = first_row(r) - r + KW - 1
                dve.wait_ge(pe_s, r + 1)
                if i >= 4:
                    dve.wait_ge(act_p, i - 3)
                v.tensor_tensor_reduce(out=sneg[:, i % 4, :],
                                       in0=bank((2, 3, 7)[r % 3])[:, 256 * (i % B):256 * (i % B) + WIN],
                                       in1=bias[:, d:d + KW, :].rearrange("p d k -> p (d k)"), scale=1.0, scalar=3.0e38,
                                       op0=ALU.add, op1=ALU.min, accum_out=nmax[:, i:i + 1]).then_inc(dve_s, 1)

            def flip(c):
                g = c // 4
                dve.wait_ge(act_p, 4 * c + 4)
                if g >= 2:
                    dve.wait_ge(pe_pv, g - 1)
                r = 2 * c
                if slot(r, first_row(r)) == slot(r + 1, first_row(r + 1)):
                    spans = [(r, 2)]
                else:
                    spans = [(r, 1), (r + 1, 1)]
                for q, nq in spans:
                    lo = IMG * slot(q, first_row(q))
                    ins = v.transpose(probT[:, g % 2, q % ROWS:q % ROWS + nq, :, lo:lo + WIN].rearrange("p r b w -> p (r b) w"),
                                      prob[:, c % 3, B * WIN * (q - r):B * WIN * (q - r + nq)].rearrange("p (k w) -> p k w", w=WIN))
                ins.then_inc(dve_t, 1)
                if c % 4 == 3:
                    v.reciprocal(prinv[:, ROWS * g:ROWS * g + ROWS, :].rearrange("p r b -> p (r b)"),
                                 psumr[:, 16 * g:16 * g + 16]).then_inc(dve_ri, 1)

            def normalise(g):
                dve.wait_ge(pe_pv, g + 1)
                dve.wait_ge(act_rb, g + 1)
                v.tensor_tensor(att[:, LANES * g:LANES * g + LANES], bank(4 + g % 2)[:, 0:LANES], rbs[:, g % 2, :],
                                ALU.mult).then_inc(dve_att, 1)

            def residual(g):
                dve.wait_ge(pe_pr, g + 1)
                dve.wait_ge(pool_xb, 1)
                v.tensor_tensor(t1[:, 2 * g:2 * g + 2, :, :].rearrange("p t b c -> p (t b c)"),
                                bank(6)[:, LANES:LANES + 2 * 128],
                                xtok[:, 2 * g:2 * g + 2, :, :].rearrange("p t b c -> p (t b c)"), ALU.add).then_inc(dve_t1, 1)

            def token_stats(src, cols):
                for t, b in cols:
                    ins = v.bn_stats(bst[:, B * t + b, :], src[:, t, b, :])
                link(ins)
                for t, b in cols:
                    ins = v.bn_aggr(mv[:, B * t + b, :], bst[:, B * t + b, :])
                link(ins)

            EPS = 1e-5

            def norm1_stats(g):
                dve.wait_ge(dve_t1, g + 1)
                token_stats(t1, [(t, b) for t in (2 * g, 2 * g + 1) for b in range(B)])
                cols = slice(4 * g, 4 * g + 4)
                v.tensor_scalar(rs[:, 0, cols], mv[:, cols, 1], EPS, None, ALU.add)
                v.tensor_scalar(rs[:, 1, cols], mv[:, cols, 1], float(C), EPS * 1e-24, ALU.mult, ALU.max)
                dve.drain()
                dve.sem_inc(dve_rs, 1)

            def low(n):
                j, b = n // B, n % B
                dve.wait_ge(act_xh, n + 1)
                src, cols = bank(b) if j == 0 else bank(7 - b), slice(HALF * j, HALF * j + HALF)
                link(v.tensor_tensor(xl[:, b, cols], src, xh[:, b, cols].bitcast(F32), ALU.subtract))
                v.tensor_copy(xa[C:2 * C, b, cols], xl[C:2 * C, b, cols].bitcast(F32)).then_inc(dve_xa, 1)

            def diagonals(g):
                dve.wait_ge(dve_ri, g + 1)
                dve.wait_ge(pe_rb, g - 1)
                for b in range(B):
                    ins = v.tensor_tensor(dinv[:, g % 2, b, :, :], kc("eye32").unsqueeze(1).broadcast_to([128, ROWS, IMG]),
                                          prinv[:, ROWS * g:ROWS * g + ROWS, b].unsqueeze(2).broadcast_to([128, ROWS, IMG]), ALU.mult)
                ins.then_inc(dve_d, 1)

            for i in range(B * IMG):
                shifted_scores(i)
                if i < 8 and i % 2:
                    queries(1, i // 2)
                if i % 4 == 3 and i >= 7:
                    flip(i // 4 - 1)
                g = i // 16 - 2
                if g >= 0:
                    if i % 16 == 3:
                        normalise(g)
                    if i % 16 == 9:
                        residual(g)
                    if i % 16 == 13:
                        norm1_stats(g)
            normalise(GROUPS - 2)
            flip(15)
            diagonals(GROUPS - 1)
            residual(GROUPS - 2)
            normalise(GROUPS - 1)
            norm1_stats(GROUPS - 2)
            residual(GROUPS - 1)
            norm1_stats(GROUPS - 1)
            last = slice(NT * B - 4, NT * B)
            dve.wait_ge(act_root, 1)
            link(v.reciprocal(rs[:, 2:4, last], rs[:, 2:4, last]))
            for t in (NT - 2, NT - 1):
                for b in range(B):
                    k = B * t + b
                    ins = v.tensor_scalar(xn2[:, t, b, :].rearrange("p (k c) -> p k c", k=2),
                                          t1[:, t, b, :].unsqueeze(1).broadcast_to([128, 2, C]),
                                          mv[:, k, 0:1], rs[:, 3, k:k + 1], ALU.subtract, ALU.mult)
            ins.then_inc(dve_xn, 1)
            for b in range(B):
                for j in range(NQ):
                    low(B * j + b)

            dve.wait_ge(d_mask, 16)
            dve.wait_ge(zeroed, 3)
            link(v.tensor_copy(mf[:, :, :], m8[:, :, :]))
            link(v.scalar_tensor_tensor(mf[0:1, 0, :], mf[0:1, 1, :], 2.0, mf[0:1, 0, :], ALU.mult, ALU.add))
            link(v.tensor_scalar(mf[0:1, 1, :], mf[0:1, 0, :], 0.0, DEAD, ALU.is_equal, ALU.mult))
            link(v.tensor_tensor(mf[0:1, 0, :], mf[0:1, 0, :], mf[0:1, 1, :], ALU.add))
            link(v.tensor_tensor(code[:, :].rearrange("u (o s) -> u s o", s=NB), mf[0:1, 0, :].rearrange("u (s o) -> u s o", o=NOPS),
                                 kc("step4", 1).unsqueeze(2).broadcast_to([1, NB, NOPS]), ALU.add))
            def inverse_sums(b, j):
                dve.wait_ge(act_e, NT * b + 4 * j + 4)
                at = slice(NT * b + 4 * j, NT * b + 4 * j + 4)
                v.reciprocal(rinv[:, at], rsum[:, at]).then_inc(dve_rinv, 1)

            def rows(b, m):
                if b == 0 and m >= 4:
                    dve.wait_ge(pe_u, m - 3)
                of = sims[b][:, N * m:N * m + N]
                v.tensor_tensor(rr[:, m % 4, :] if b == 0 else of, of, bank(2 * b, 2), ALU.mult).then_inc(dve_r, 1)

            def columns(b, m):
                i = NT * b + m
                dve.wait_ge(act_f, i + 1)
                link(v.reciprocal(cinv[:, i:i + 1], csum[:, i:i + 1]))
                v.tensor_scalar(xc[:, b, m, :], a[:, m, b, :], cinv[:, i:i + 1], None, ALU.mult).then_inc(dve_xc, 1)

            for j in range(NQ):
                inverse_sums(0, j)
            dve.wait_ge(pool_a, GROUPS)
            dve.wait_ge(pe_rB, NQ)
            for m in range(NT):
                rows(0, m)
                if m:
                    columns(0, m - 1)
                if m == 5:
                    for j in range(NQ):
                        inverse_sums(1, j)
            columns(0, NT - 1)

            def keep(b, tiles, of):
                n = len(tiles)
                t = slice(tiles[0], tiles[0] + n)
                link(v.scalar_tensor_tensor(y[:, t, b, :], of[:, C * t.start:C * t.stop].rearrange("p (t c) -> p t c", c=C), -0.1,
                                            a[:, t, b, :], ALU.mult, ALU.add))

            def variances(src, b, tiles, eps, signal):
                token_stats(src, [(t, b) for t in tiles])
                cols = slice(B * tiles[0] + b, B * tiles[-1] + b + 1, B)
                v.tensor_scalar(sd[:, 0, cols], mv[:, cols, 1], eps, None, ALU.add).then_inc(signal, 1)

            def half(j):
                return range(4 * j, 4 * j + 4)

            dve.wait_ge(pe_rB, 2 * NQ)
            for m in range(NT):
                rows(1, m)
                if m:
                    columns(1, m - 1)
                if m == 4:
                    dve.wait_ge(pe_y, NQ)
                    keep(0, half(0), bank(0))
                    variances(y, 0, half(0), 1e-6, dve_ve0)
                if m == 7:
                    dve.wait_ge(pool_t2, 1)
                    variances(t2, 0, half(0), 1e-5, dve_ve0)
            columns(1, NT - 1)
            keep(0, half(1), bank(0))
            variances(y, 0, half(1), 1e-6, dve_ve0)

            def normed(j, of, n):
                tiles = half(j)
                cols = slice(4 * B * j + 1, 4 * B * j + 4 * B, B)
                dve.wait_ge(pe_y, NQ + j + 1)
                keep(1, tiles, of)
                variances(y, 1, tiles, 1e-6, dve_ve1)
                for t in tiles:
                    ins = v.scalar_tensor_tensor(y[:, t, 1, :], y[:, t, 1, :], mv[:, B * t + 1, 0:1], kc("lnw"), ALU.subtract, ALU.mult)
                dve.wait_ge(act_sqrt, n)
                link(v.reciprocal(rstd[:, cols], sd[:, 1, cols]))
                for t in tiles:
                    ins = v.scalar_tensor_tensor(t2[:, t, 1, :], y[:, t, 1, :], rstd[:, B * t + 1:B * t + 2], t1b[:, t, 1, :],
                                                 ALU.mult, ALU.add)
                link(ins)
                variances(t2, 1, tiles, 1e-5, dve_ve1)
                at = slice(4 * j, 4 * j + 4)
                v.tensor_tensor(y[:, at, 1, :], t2[:, at, 1, :], mv[:, cols, 0].unsqueeze(2).broadcast_to([128, 4, C]), ALU.subtract)
                dve.wait_ge(act_sqrt, n + 1)
                link(v.reciprocal(rstd[:, cols], sd[:, 1, cols]))
                ins = v.tensor_tensor(xn[:, at, 1, :], y[:, at, 1, :], rstd[:, cols].unsqueeze(2).broadcast_to([128, 4, C]), ALU.mult)
                ins.then_inc(dve_h0, 1)

            def decide(row):
                dve.drain()
                v.max(mx8[:, :], row)
                dve.drain()
                v.max_index(ix8[:, :], mx8[:, :], row)
                dve.drain()
                op = dve.value_load(ix8[0:1, 0:1], min_val=0, max_val=NOPS - 1)
                v.tensor_tensor(kcand[0:1, 1, :], kcand[0:1, 0, :], code[0:1, bass.ds(op * NB, NB)], ALU.add)
                dve.drain()
                v.tensor_reduce(keyf[:, :], kcand[0:1, 1, :], AX.X, ALU.min)
                dve.drain()
                v.tensor_copy(ctl[:, :], keyf[:, :]).then_inc(decided, 1)
                past_steps()
                dve.drain()

            def past_steps():
                v.tensor_scalar(kcand[0:1, 0, :], kc("step4", 1), keyf[0:1, 0:1], DEAD, ALU.is_le, ALU.mult)

            past_steps()

            dve.wait_ge(pool_h0, 1)
            decide(xn[0:1, 0, 0, 0:NOPS])
            dve.wait_ge(pool_t1b, 1)
            normed(0, bank(1), 1)
            dve.wait_ge(pool_t2, 2)
            variances(t2, 0, half(1), 1e-5, dve_ve0)
            normed(1, bank(6), 3)
            n, nf, na = (dve.alloc_register(f"dve_{s}") for s in ("n", "nf", "na"))
            for r in (n, nf, na):
                dve.reg_mov(r, 0)
            key = dve.alloc_register("dve_key")
            dve.reg_load(key, ctl[0:1, 0:1])
            dve.wait_ge(pe_hT, 2)
            v.tensor_copy(H[:, HALF:2 * HALF], bank(6)).then_inc(h_ready, 1)
            with dve.While(lambda: dve.snap(key) < 4 * NB):
                k = pending(dve, key)
                with dve.If(k % 2 == 1):
                    done = dve.snap(na)
                    dve.wait_ge(pe_aqkv, done + 1)
                    v.tensor_copy(aq, bank(0, 2))
                    v.tensor_copy(ak, bank(2, 2))
                    v.tensor_copy(av, bank(4, 2)).then_inc(dve_aqkv, 1)
                    for u in range(B * NT):
                        dve.wait_ge(pe_asc, done * (B * NT) + u + 1)
                        v.tensor_reduce(am_stat[:, 0:1], bank(0, 2), AX.X, ALU.max, negate=True)
                        dve.drain()
                        v.tensor_scalar(am_stat[:, 1:2], am_stat[:, 0:1], C ** -0.5, None, ALU.mult).then_inc(dve_amx, 1)
                        dve.wait_ge(act_ap, done * (B * NT) + u + 1)
                        v.reciprocal(am_stat[:, 3:4], am_stat[:, 2:3])
                        dve.drain()
                        v.tensor_scalar(ap_, ap_, am_stat[:, 3:4], None, ALU.mult).then_inc(dve_apn, 1)
                        dve.wait_ge(pe_atr, done * (B * NT) + u + 1)
                        v.tensor_copy(apt, bank(2, 2)).then_inc(dve_apt, 1)
                    dve.wait_ge(pe_ao, done * (B * NT) + B * NT)
                    v.tensor_copy(ao, bank(4, 2)).then_inc(dve_ao, 1)
                    for j in range(NQ):
                        dve.wait_ge(pe_ay, done * NQ + j + 2)
                        v.tensor_copy(H[:, HALF * j:HALF * j + HALF], bank(6 + j)).then_inc(h_ready, 1)
                    dve.reg_add(na, na, 1)
                with dve.If((k // 2) % 2 == 0):
                    hold(dve, pe_row, dve.snap(n) + 1)
                    decide(bank(1)[0:1, 0:NOPS])
                with dve.If((k // 2) % 2 == 1):
                    done = dve.snap(nf)
                    hold(dve, d_w, done * 16 + 16)
                    dve.drain()
                    v.tensor_copy(w1z[C:2 * C, 1, :], stage[C:2 * C, 0:HID])
                    v.tensor_copy(live[:, :], stage[:, HID:]).then_inc(rest_live, 1)
                    dve.drain()
                    hold(dve, pe_row, dve.snap(n) + 1)
                    decide(row0[:, 0:NOPS])
                    for j in range(NQ):
                        if j == 1:
                            for mc in range(2):
                                dve.wait_ge(pe_z, done * 8 + 6 + mc)
                                v.tensor_scalar(z[:, 1, 1, mc, :], bank(6 + mc), b1l[:, mc:mc + 1], 0.0,
                                                ALU.add, ALU.max).then_inc(dve_z, 1)
                        dve.wait_ge(pe_h, done * NQ + j + 1)
                        v.tensor_scalar(H[:, HALF * j:HALF * j + HALF], bank(4 * j), b2l[:, 0:1], None,
                                        ALU.add).then_inc(h_ready, 1)
                    dve.reg_add(nf, nf, 1)
                dve.reg_add(n, n, 1)
                dve.reg_load(key, ctl[0:1, 0:1])

            for j in range(NQ):
                dve.wait_ge(pe_oT, j + 1)
                v.tensor_tensor(cen[:, 4 * j:4 * j + 4, :, :].rearrange("p t b c -> p (t b c)"), bank(2 + j),
                                t2[:, 4 * j:4 * j + 4, :, :].rearrange("p t b c -> p (t b c)"), ALU.add).then_inc(dve_o, 1)


def kernel(**inputs):
    import numpy as _np
    import concourse.bacc as _bacc
    from concourse import mybir as _mybir
    from concourse.bass_utils import run_bass_kernel_spmd as _run

    nc = _bacc.Bacc("TRN2", target_bir_lowering=False, num_devices=1)
    arrays, args = {}, []
    for name, v in laid_out({k: _np.asarray(v) for k, v in inputs.items()}).items():
        v = _np.ascontiguousarray(v)
        arrays[f"in_{name}_dram"] = v
        args.append(nc.dram_tensor(f"in_{name}_dram", v.shape, _mybir.dt.from_np(v.dtype), kind="ExternalInput").ap())
    args.append(nc.dram_tensor("out_dram", (128, NT, B, C), F32, kind="ExternalOutput").ap())
    build(nc, *args)
    r = _run(nc, [arrays], core_ids=[0])
    return _np.ascontiguousarray(r.results[0]["out_dram"].transpose(2, 1, 0, 3)).reshape(B, IMG, IMG, C)
```
